# Optimizing a Trainium2 kernel written in Bass

```python
import numpy as np
import jax
import jax.numpy as jnp

def _softmax(x, axis=-1):
    return jax.nn.softmax(x, axis=axis)

def _gelu(x):
    return jax.nn.gelu(x, approximate=True)

def _silu(x):
    return jax.nn.silu(x)

def _sigmoid(x):
    return jax.nn.sigmoid(x)

def _layernorm(x, axis=-1, eps=1e-05):
    m = jnp.mean(x, axis=axis, keepdims=True)
    v = jnp.var(x, axis=axis, keepdims=True)
    return (x - m) / jnp.sqrt(v + eps)

def _scatter_add(tgt, idx, src, axis=0):
    return tgt.at[idx].add(src)

def _segment_sum(src, seg, n):
    return jax.ops.segment_sum(src, seg, n)
kernel_name = 'mk_seq_postln_d2_jaxref_r8_2be78f'

def setup_inputs(seed: int=0):
    np.random.seed(seed)
    _w = jnp.asarray

    def _L0_attn_setup():
        import jax, jax.numpy as jnp
        import numpy as np
        import math
        D_MODEL = 256
        D_STATE = 16
        EXPAND = 2
        D_INNER = D_MODEL * EXPAND
        DT_RANK = math.ceil(D_MODEL / 16)
        BATCH, SEQ_LEN = (2, 64)
        key = jax.random.key(seed)
        ks = jax.random.split(key, 6)
        x = jax.random.normal(ks[0], (BATCH, SEQ_LEN, D_INNER), dtype=jnp.float32)
        A_log = jnp.log(jax.random.uniform(ks[1], (D_INNER, D_STATE), minval=0.5, maxval=16.0, dtype=jnp.float32))
        D = jnp.ones((D_INNER,), dtype=jnp.float32)
        x_proj_w = 0.02 * jax.random.normal(ks[2], (DT_RANK + 2 * D_STATE, D_INNER), dtype=jnp.float32)
        dt_init_std = DT_RANK ** (-0.5)
        dt_proj_w = jax.random.uniform(ks[3], (D_INNER, DT_RANK), minval=-dt_init_std, maxval=dt_init_std, dtype=jnp.float32)
        dt = jnp.exp(jax.random.uniform(ks[4], (D_INNER,), dtype=jnp.float32) * (math.log(0.1) - math.log(0.001)) + math.log(0.001))
        dt = jnp.clip(dt, 0.0001, None)
        dt_proj_b = dt + jnp.log(-jnp.expm1(-dt))
        return {'x': x, 'A_log': A_log, 'D': D, 'x_proj_w': x_proj_w, 'dt_proj_w': dt_proj_w, 'dt_proj_b': dt_proj_b}
    _L0_attn_in = _L0_attn_setup()

    def _L0_ffn_setup():
        import jax, jax.numpy as jnp
        import numpy as np
        HD, M = (512, 1792)
        key = jax.random.key(seed)
        k_x, k_g, k_u, k_d = jax.random.split(key, 4)
        scale = 1.0 / np.sqrt(HD)
        x = jax.random.normal(k_x, (4, 256, HD), dtype=jnp.float16)
        W_gate = jax.random.normal(k_g, (M, HD), dtype=jnp.float16) * jnp.float16(scale)
        W_up = jax.random.normal(k_u, (M, HD), dtype=jnp.float16) * jnp.float16(scale)
        W_down = jax.random.normal(k_d, (HD, M), dtype=jnp.float16) * jnp.float16(1.0 / np.sqrt(M))
        return {'x': x, 'W_gate': W_gate, 'W_up': W_up, 'W_down': W_down}
    _L0_ffn_in = _L0_ffn_setup()

    def _L1_attn_setup():
        import math
        import jax, jax.numpy as jnp
        import numpy as np

        def _rope_tables(T, h, dtype):
            pos = jnp.arange(T, dtype=jnp.float32)
            thetas = 1.0 / 10000.0 ** (jnp.arange(0, h, 2, dtype=jnp.float32) / h)
            pt = jnp.outer(pos, thetas)
            pt = jnp.concatenate([pt, pt], axis=-1)
            return (jnp.sin(pt).astype(dtype), jnp.cos(pt).astype(dtype))

        def _apply_rope(x, sin, cos):
            h = x.shape[-1]
            rot = jnp.concatenate([-x[..., h // 2:], x[..., :h // 2]], axis=-1)
            return x * cos + rot * sin
        key = jax.random.key(seed)
        ks = jax.random.split(key, 5)
        B, T, C = (2, 256, 512)
        s = 1.0 / math.sqrt(C)
        return {'x': jax.random.normal(ks[0], (B, T, C), dtype=jnp.float32), 'wq': jax.random.normal(ks[1], (C, C), dtype=jnp.float32) * s, 'wk': jax.random.normal(ks[2], (C, C), dtype=jnp.float32) * s, 'wv': jax.random.normal(ks[3], (C, C), dtype=jnp.float32) * s, 'wo': jax.random.normal(ks[4], (C, C), dtype=jnp.float32) * s}
    _L1_attn_in = _L1_attn_setup()

    def _L1_ffn_setup():
        import jax, jax.numpy as jnp
        import numpy as np
        HIDDEN = 512
        INTER = 1376
        GROUPSIZE = 128
        PACK = 8

        def dequant_gptq(qweight, scales, zeros, groupsize):
            K = qweight.shape[0] * PACK
            N = qweight.shape[1]
            k = jnp.arange(K)
            q = qweight[k // PACK, :] >> (k % PACK * 4)[:, None] & 15
            n = jnp.arange(N)
            z = zeros[:, n // PACK] >> (n % PACK * 4)[None, :] & 15
            s = scales.astype(jnp.float32)
            zp = (z.astype(jnp.float32) + 1.0) * s
            g = k // groupsize
            return q.astype(jnp.float32) * s[g] - zp[g]
        key = jax.random.key(seed)
        ks = jax.random.split(key, 11)
        imax = 2147483647
        G_h = HIDDEN // GROUPSIZE
        G_i = (INTER + GROUPSIZE - 1) // GROUPSIZE
        x = (jax.random.normal(ks[0], (2, 256, HIDDEN), dtype=jnp.float32) * 0.5).astype(jnp.float16)
        return {'x': x, 'gate_qweight': jax.random.randint(ks[1], (HIDDEN // PACK, INTER), 0, imax, dtype=jnp.int32), 'gate_scales': (jax.random.uniform(ks[2], (G_h, INTER), dtype=jnp.float32) * 0.01 + 0.001).astype(jnp.float16), 'gate_zeros': jax.random.randint(ks[3], (G_h, INTER // PACK), 0, imax, dtype=jnp.int32), 'up_qweight': jax.random.randint(ks[4], (HIDDEN // PACK, INTER), 0, imax, dtype=jnp.int32), 'up_scales': (jax.random.uniform(ks[5], (G_h, INTER), dtype=jnp.float32) * 0.01 + 0.001).astype(jnp.float16), 'up_zeros': jax.random.randint(ks[6], (G_h, INTER // PACK), 0, imax, dtype=jnp.int32), 'down_qweight': jax.random.randint(ks[7], (INTER // PACK, HIDDEN), 0, imax, dtype=jnp.int32), 'down_scales': (jax.random.uniform(ks[8], (G_i, HIDDEN), dtype=jnp.float32) * 0.01 + 0.001).astype(jnp.float16), 'down_zeros': jax.random.randint(ks[9], (G_i, HIDDEN // PACK), 0, imax, dtype=jnp.int32)}
    _L1_ffn_in = _L1_ffn_setup()
    _d = {'L0_attn_x': _L0_attn_in['x'], 'L0_attn_A_log': _L0_attn_in['A_log'], 'L0_attn_D': _L0_attn_in['D'], 'L0_attn_x_proj_w': _L0_attn_in['x_proj_w'], 'L0_attn_dt_proj_w': _L0_attn_in['dt_proj_w'], 'L0_attn_dt_proj_b': _L0_attn_in['dt_proj_b'], 'L0_ffn_W_gate': _L0_ffn_in['W_gate'], 'L0_ffn_W_up': _L0_ffn_in['W_up'], 'L0_ffn_W_down': _L0_ffn_in['W_down'], 'L1_attn_wq': _L1_attn_in['wq'], 'L1_attn_wk': _L1_attn_in['wk'], 'L1_attn_wv': _L1_attn_in['wv'], 'L1_attn_wo': _L1_attn_in['wo'], 'L1_ffn_gate_qweight': _L1_ffn_in['gate_qweight'], 'L1_ffn_gate_scales': _L1_ffn_in['gate_scales'], 'L1_ffn_gate_zeros': _L1_ffn_in['gate_zeros'], 'L1_ffn_up_qweight': _L1_ffn_in['up_qweight'], 'L1_ffn_up_scales': _L1_ffn_in['up_scales'], 'L1_ffn_up_zeros': _L1_ffn_in['up_zeros'], 'L1_ffn_down_qweight': _L1_ffn_in['down_qweight'], 'L1_ffn_down_scales': _L1_ffn_in['down_scales'], 'L1_ffn_down_zeros': _L1_ffn_in['down_zeros']}
    _x0 = _d['L0_attn_x']
    _d['L0_attn_x'] = jax.random.normal(jax.random.fold_in(jax.random.key(seed), 1), (1, 1024, 512), dtype=_x0.dtype)
    del _x0
    return _d

def reference(L0_attn_x, L0_attn_A_log, L0_attn_D, L0_attn_x_proj_w, L0_attn_dt_proj_w, L0_attn_dt_proj_b, L0_ffn_W_gate, L0_ffn_W_up, L0_ffn_W_down, L1_attn_wq, L1_attn_wk, L1_attn_wv, L1_attn_wo, L1_ffn_gate_qweight, L1_ffn_gate_scales, L1_ffn_gate_zeros, L1_ffn_up_qweight, L1_ffn_up_scales, L1_ffn_up_zeros, L1_ffn_down_qweight, L1_ffn_down_scales, L1_ffn_down_zeros):

    def _L0_attn_ref(x, A_log, D, x_proj_w, dt_proj_w, dt_proj_b):
        import jax, jax.numpy as jnp
        import numpy as np
        import math
        D_MODEL = 256
        D_STATE = 16
        EXPAND = 2
        D_INNER = D_MODEL * EXPAND
        DT_RANK = math.ceil(D_MODEL / 16)
        BATCH, SEQ_LEN = (2, 64)
        A = -jnp.exp(A_log)
        xp = jnp.einsum('bld,rd->blr', x, x_proj_w)
        dt_in = xp[..., :DT_RANK]
        B = xp[..., DT_RANK:DT_RANK + D_STATE]
        C = xp[..., DT_RANK + D_STATE:]
        dt = jax.nn.softplus(jnp.einsum('blr,dr->bld', dt_in, dt_proj_w) + dt_proj_b)
        dA = jnp.exp(dt[..., None] * A)
        dBx = dt[..., None] * B[:, :, None, :] * x[..., None]

        def step(h, inp):
            dA_t, dBx_t, C_t = inp
            h = dA_t * h + dBx_t
            y = jnp.einsum('bdn,bn->bd', h, C_t)
            return (h, y)
        h0 = jnp.zeros((x.shape[0], D_INNER, D_STATE), dtype=x.dtype)
        _, ys = jax.lax.scan(step, h0, (jnp.moveaxis(dA, 1, 0), jnp.moveaxis(dBx, 1, 0), jnp.moveaxis(C, 1, 0)))
        y = jnp.moveaxis(ys, 0, 1) + D * x
        return y

    def _L0_ffn_ref(x, W_gate, W_up, W_down):
        import jax, jax.numpy as jnp
        import numpy as np
        HD, M = (512, 1792)
        gate = jnp.einsum('bsh,mh->bsm', x, W_gate)
        up = jnp.einsum('bsh,mh->bsm', x, W_up)
        h = jax.nn.silu(gate) * up
        out = jnp.einsum('bsm,hm->bsh', h, W_down)
        return out

    def _L1_attn_ref(x, wq, wk, wv, wo):
        import math
        import jax, jax.numpy as jnp
        import numpy as np

        def _rope_tables(T, h, dtype):
            pos = jnp.arange(T, dtype=jnp.float32)
            thetas = 1.0 / 10000.0 ** (jnp.arange(0, h, 2, dtype=jnp.float32) / h)
            pt = jnp.outer(pos, thetas)
            pt = jnp.concatenate([pt, pt], axis=-1)
            return (jnp.sin(pt).astype(dtype), jnp.cos(pt).astype(dtype))

        def _apply_rope(x, sin, cos):
            h = x.shape[-1]
            rot = jnp.concatenate([-x[..., h // 2:], x[..., :h // 2]], axis=-1)
            return x * cos + rot * sin
        B, T, C = x.shape
        n_head = 32
        h = C // n_head

        def proj(w):
            y = jnp.einsum('btc,dc->btd', x, w)
            return y.reshape(B, T, n_head, h).transpose(0, 2, 1, 3)
        q, k, v = (proj(wq), proj(wk), proj(wv))
        sin, cos = _rope_tables(T, h, x.dtype)
        q = _apply_rope(q, sin, cos)
        k = _apply_rope(k, sin, cos)
        scores = jnp.einsum('bnth,bnsh->bnts', q, k) * (1.0 / math.sqrt(h))
        causal = jnp.tril(jnp.ones((T, T), dtype=bool))
        scores = jnp.where(causal, scores, -jnp.inf)
        attn = jax.nn.softmax(scores, axis=-1)
        out = jnp.einsum('bnts,bnsh->bnth', attn, v)
        out = out.transpose(0, 2, 1, 3).reshape(B, T, C)
        return jnp.einsum('btc,dc->btd', out, wo)

    def _L1_ffn_ref(x, gate_qweight, gate_scales, gate_zeros, up_qweight, up_scales, up_zeros, down_qweight, down_scales, down_zeros):
        import jax, jax.numpy as jnp
        import numpy as np
        HIDDEN = 512
        INTER = 1376
        GROUPSIZE = 128
        PACK = 8

        def dequant_gptq(qweight, scales, zeros, groupsize):
            K = qweight.shape[0] * PACK
            N = qweight.shape[1]
            k = jnp.arange(K)
            q = qweight[k // PACK, :] >> (k % PACK * 4)[:, None] & 15
            n = jnp.arange(N)
            z = zeros[:, n // PACK] >> (n % PACK * 4)[None, :] & 15
            s = scales.astype(jnp.float32)
            zp = (z.astype(jnp.float32) + 1.0) * s
            g = k // groupsize
            return q.astype(jnp.float32) * s[g] - zp[g]
        B, S, H = x.shape
        x2 = x.reshape(-1, H).astype(jnp.float32)
        Wg = dequant_gptq(gate_qweight, gate_scales, gate_zeros, GROUPSIZE)
        Wu = dequant_gptq(up_qweight, up_scales, up_zeros, GROUPSIZE)
        Wd = dequant_gptq(down_qweight, down_scales, down_zeros, GROUPSIZE)
        gate = x2 @ Wg
        up = x2 @ Wu
        inter = gate * jax.nn.sigmoid(gate) * up
        out = (inter @ Wd).astype(jnp.float16)
        return out.reshape(B, S, H)
    x = L0_attn_x
    x = _layernorm(x + _L0_attn_ref(x, L0_attn_A_log, L0_attn_D, L0_attn_x_proj_w, L0_attn_dt_proj_w, L0_attn_dt_proj_b), axis=-1)
    x = _layernorm(x + _L0_ffn_ref(x, L0_ffn_W_gate, L0_ffn_W_up, L0_ffn_W_down), axis=-1)
    x = _layernorm(x + _L1_attn_ref(x, L1_attn_wq, L1_attn_wk, L1_attn_wv, L1_attn_wo), axis=-1)
    x = _layernorm(x + _L1_ffn_ref(x, L1_ffn_gate_qweight, L1_ffn_gate_scales, L1_ffn_gate_zeros, L1_ffn_up_qweight, L1_ffn_up_scales, L1_ffn_up_zeros, L1_ffn_down_qweight, L1_ffn_down_scales, L1_ffn_down_zeros), axis=-1)
    return x

_drawn_inputs = setup_inputs


def setup_inputs(seed=0):
    import zlib

    import numpy as np

    out = dict(_drawn_inputs(seed))
    spreads = {'L0_attn_D': (1.0, 0.2)}
    factors = {'L0_attn_A_log': 11.708,
     'L0_attn_dt_proj_w': 25.273,
     'L0_attn_dt_proj_b': 9.851,
     'L0_attn_x_proj_w': 3.226}
    for name, (base, spread) in spreads.items():
        noise = np.random.default_rng([zlib.crc32(name.encode()), seed]).standard_normal(out[name].shape)
        drawn = base * np.exp(spread * noise) if base else spread * noise
        out[name] = jnp.asarray(drawn.astype(out[name].dtype))
    for name, factor in factors.items():
        out[name] = (out[name] * factor).astype(out[name].dtype)
    return out
```

```python
import concourse.bass as bass
from concourse import mybir
from contextlib import ExitStack

P = 128
T = 1024
TT = T // P
D = 512
DC = D // P
NS = 16
DTR = 16
F0 = 1792
M0 = F0 // P
F1 = 1376
M1 = (F1 + P - 1) // P
TAIL = F1 - (M1 - 1) * P
NH = 32
HD = D // NH
NP = NH // 2
GH = 4
NG = NH // GH
HALF = 512
EPS = 1e-5
WS = 256.0
PACK = 8
SERIES = 2.0 ** -7
LAG = 3


class Tally:

    def __init__(self, eng, sem):
        self.eng, self.sem, self.at = eng, sem, 0

    def done(self, ins):
        ins.then_inc(self.sem, 1)
        self.at = self.at + 1
        self.eng.wait_ge(self.sem, self.at)

    def loop(self, i, per):
        self.base = self.at
        self.at = self.base + i * per

    def end(self, passes, per):
        self.at = self.base + passes * per


def build(nc, x_fm, a_log, d_skip, xw, dtw, wg0, wu0, wd0, wq, wk, wv, wo,
          w1_q, w1_s, w1_z, ident, fold, mask, cos, sin, shifts, out):
    f32, f16, bf16, i32, u8 = mybir.dt.float32, mybir.dt.float16, mybir.dt.bfloat16, mybir.dt.int32, mybir.dt.uint8
    ALU = mybir.AluOpType
    ACT = mybir.ActivationFunctionType
    AX = mybir.AxisListType.X
    ds = bass.ds

    ctx = ExitStack()
    with ctx:
        arena = ctx.enter_context(nc.sbuf_tensor("arena", [P, 200 * 256], f32))

        def view(kb, cols, dt):
            size = 4 if dt in (f32, i32) else 2
            a = int(kb * 256)
            return arena[:, a:a + cols * size // 4].bitcast(dt) if dt != f32 else arena[:, a:a + cols]

        def small(name, shape, dt=f32):
            return ctx.enter_context(nc.sbuf_tensor(name, shape, dt))

        def sem(name):
            return ctx.enter_context(nc.semaphore(name))

        ps = ctx.enter_context(nc.psum_tensor("ps", [P, 8, HALF], f32))

        def banks(a, n):
            return ps[:, a:a + n, :].rearrange("p b n -> p (b n)")

        xT = view(0, DC * T, f32).rearrange("p (c t) -> p c t", c=DC)
        dt_ = view(16, DC * T, f32).rearrange("p (c t) -> p c t", c=DC)
        dtx = view(32, DC * T, f32).rearrange("p (c t) -> p c t", c=DC)
        c_all = view(48, NS * T, f32).rearrange("p (n t) -> p n t", n=NS)
        dA = view(112, 2 * T, f32).rearrange("p (b t) -> p b t", b=2)
        hst = view(120, 2 * T, f32).rearrange("p (b t) -> p b t", b=2)
        hC = [view(kb, T, f32) for kb in (128, 132, 186, 190)]
        sel = view(136, 2 * NS * P, bf16).rearrange("p (n m) -> p n m", n=2 * NS)
        bc = view(144, T, bf16)
        rest = view(146, T, f32)
        mid = view(150, T, bf16)
        dt_in = view(152, T, f32)
        e_, log_e, small_e = rest, view(194, T, f32), view(198, T, f16)
        wg0_sb = view(158, DC * F0, f16).rearrange("p (c m) -> p c m", c=DC)
        wu0_sb = view(172, DC * F0, f16).rearrange("p (c m) -> p c m", c=DC)
        wd0_sb = view(186, M0 * D, f16).rearrange("p (m d) -> p m d", m=M0)
        xtok = view(16, TT * D, f32).rearrange("p (i d) -> p i d", i=TT)
        xh = view(32, DC * T, f16).rearrange("p (c t) -> p c t", c=DC)
        xl = view(40, DC * T, f16).rearrange("p (c t) -> p c t", c=DC)
        hh = view(48, M0 * T, f16).rearrange("p (m t) -> p m t", m=M0)
        hl = view(76, M0 * T, f16).rearrange("p (m t) -> p m t", m=M0)
        sg = view(104, 2 * T, f32).rearrange("p (b t) -> p b t", b=2)
        h32 = view(112, 2 * T, f32).rearrange("p (b t) -> p b t", b=2)
        wraw = view(0, 2 * DC * D, f32).rearrange("p (b c d) -> p b c d", b=2, c=DC)
        wsp = view(120, 4 * 2 * DC * D, f16).rearrange("p (w s c d) -> p w s c d", w=4, s=2, c=DC)

        ident_sb = small("ident_sb", [P, P])
        fold_sb = small("fold_sb", [P, 2 * NS])
        alog_sb = small("alog_sb", [P, DC, NS])
        negA = small("negA", [P, DC, NS])
        dskip_sb = small("dskip_sb", [P, DC])
        series_sb = small("series_sb", [P, 1])
        xw_sb = small("xw_sb", [P, DC, 2 * NS + DTR])
        dtw_sb = small("dtw_sb", [2 * NS + DTR + 1, D])
        xn = view(152, 2 * D, f32).rearrange("p (b d) -> p b d", b=2)
        st6 = small("st6", [P, 6])
        mv = small("mv", [P, 2])
        vare = small("vare", [P, 1])
        sdev = small("sdev", [P, 1])
        rstd = small("rstd", [P, 1])
        tok_stack = view(0, 2 * NH * 64, f16).rearrange("p (w h d) -> p w h d", w=2, h=NH)
        rot_a = view(188, 2 * D, f32).rearrange("p (w h d) -> p w h d", w=2, h=NH)
        rot_b = view(192, 2 * D, f32).rearrange("p (w h d) -> p w h d", w=2, h=NH)
        q_st = view(48, NP * T, f16).rearrange("p (r t) -> p r t", r=NP)
        k_st = view(80, NP * T, f16).rearrange("p (r t) -> p r t", r=NP)
        v_tok = view(156, TT * D, f32).rearrange("p (i d) -> p i d", i=TT)
        v_ring = [view(kb, TT * GH * 32, f32).rearrange("p (i a d) -> p i a d", i=TT, a=GH) for kb in (172, 176)]
        k_pad = [view(kb, GH * T, f16).rearrange("p (a t) -> p a t", a=GH) for kb in (112, 120)]
        p_t = [view(kb, GH * T, f32).rearrange("p (a t) -> p a t", a=GH) for kb in (0, 128)]
        o_tok = view(32, TT * D, f32).rearrange("p (i d) -> p i d", i=TT)
        o_raw = view(188, T, f32)
        m_row = view(192, T, f16)
        m_a = view(194, TT * GH, f32).rearrange("p (i a) -> p i a", i=TT)
        m_b = view(194.5, 4 * GH, f32).rearrange("p (i a) -> p i a", i=4)
        m_neg = view(195, TT * GH, f16).rearrange("p (i a) -> p i a", i=TT)
        r_den = view(195.5, 4 * GH, f32).rearrange("p (i a) -> p i a", i=4)
        oh = view(112, DC * T, f16).rearrange("p (c t) -> p c t", c=DC)
        ol = view(120, DC * T, f16).rearrange("p (c t) -> p c t", c=DC)
        x3h = view(64, DC * T, f16).rearrange("p (c t) -> p c t", c=DC)
        x3l = view(72, DC * T, f16).rearrange("p (c t) -> p c t", c=DC)
        cos_sb = small("cos_sb", [P, TT, HD])
        sin_sb = small("sin_sb", [P, TT, HD])
        mask_sb = small("mask_sb", [P, P])
        mask_b = small("mask_b", [P, P], bf16)
        ident_b = small("ident_b", [P, P], bf16)
        ident_h = small("ident_h", [P, P], f16)
        ld_tab, tables_made = sem("ld_tab"), sem("tables_made")
        q_proj, k_proj, v_proj = sem("q_proj"), sem("k_proj"), sem("v_proj")
        roped, rope_summed, stack_high, stack_low, stacks_set = (
            sem("roped"), sem("rope_summed"), sem("stack_high"), sem("stack_low"), sem("stacks_set"))
        q_turned, k_turned, q_kept, k_kept, v_kept = (
            sem("q_turned"), sem("k_turned"), sem("q_kept"), sem("k_kept"), sem("v_kept"))
        pads_zeroed, v_ones = sem("pads_zeroed"), sem("v_ones")
        k_padded = [sem("k_padded0"), sem("k_padded1")]
        v_ringed, ring_full, ring_read = sem("v_ringed"), sem("ring_full"), sem("ring_read")
        m_joined, m_negated, m_rows, r_made = sem("m_joined"), sem("m_negated"), sem("m_rows"), sem("r_made")
        st_full, exp_done, pv_step, o_kept = sem("st_full"), sem("exp_done"), sem("pv_step"), sem("o_kept")
        o_turned, oh_done, ol_done = sem("o_turned"), sem("oh_done"), sem("ol_done")

        KEYS = [0, 7, 6, 5, 4, 3, 2, 1]
        MAXES = [[0], [7], [6], [5], [4], [3], [2, 1], []]

        def max_units(i):
            w = P * (i + 1)
            if w <= HALF:
                n = HALF // w if w != 3 * P else 1
                return [(m_a[:, i, a:a + n], [(a + b, 0, w, b * w) for b in range(n)]) for a in range(0, GH, n)]
            units = [(m_a[:, i, a:a + 1], [(a, 0, HALF, 0)]) for a in range(GH)]
            w -= HALF
            n = HALF // w if w != 3 * P else 1
            return units + [(m_b[:, i - 4, a:a + n], [(a + b, HALF, w, b * w) for b in range(n)]) for a in range(0, GH, n)]
        UNITS = sum(len(max_units(i)) for i in range(TT)) + 1
        BODY = UNITS + 2

        def ring_base(g):
            return UNITS if isinstance(g, int) and g == 0 else 2 * UNITS - BODY + g * BODY

        def exp_units(j):
            return [(a,) for a in range(GH)] if T - P * j > HALF else [(0, 1), (2, 3)]
        EXPS = sum(len(exp_units(j)) for j in range(TT))
        NB = 2 * DC + DC
        w_words = [view(kb, NB * P, i32) for kb in (156, 162)]
        w_scales = [view(kb, NB * P, f16) for kb in (168, 171)]
        w_zeros = [view(kb, NB * P // PACK, i32) for kb in (174, 175)]
        w_nib = view(176, NB * P, i32)
        w_full = view(182, NB * P, f32)
        z_nib = view(196, NB * P // 2, f16).bitcast(u8)
        o_half = view(198, D, f16)
        gu = [view(kb, 2 * 2 * DC * P, f16).rearrange("p (s b n) -> p s b n", s=2, b=2 * DC) for kb in (60, 146)]
        wd1 = view(124, 2 * M1 * D, f16).rearrange("p (s m d) -> p s m d", s=2, m=M1)
        h1h = view(80, M1 * T, f16).rearrange("p (m t) -> p m t", m=M1)
        h1l = view(102, M1 * T, f16).rearrange("p (m t) -> p m t", m=M1)
        sg1 = view(0, 2 * T, f32).rearrange("p (b t) -> p b t", b=2)
        h132 = view(8, 2 * T, f32).rearrange("p (b t) -> p b t", b=2)
        shift_sb = small("shift_sb", [P, 1], i32)
        ld_shift = sem("ld_shift")
        ld_w1 = [sem("ld_w1_0"), sem("ld_w1_1")]
        w1_nib, w1_full, w1_scaled, w1_high, w1_low = (
            sem("w1_nib"), sem("w1_full"), sem("w1_scaled"), sem("w1_high"), sem("w1_low"))
        gate1_done, up1_done, silu1_done, h1_done, h1h_done, h1l_done = (
            sem("gate1_done"), sem("up1_done"), sem("silu1_done"), sem("h1_done"), sem("h1h_done"), sem("h1l_done"))
        out_stored = [sem("out_stored0"), sem("out_stored1")]

        ld_small, ld_w0 = sem("ld_small"), sem("ld_w0")
        ld_x = [sem(f"ld_x{c}") for c in range(DC)]
        ld_wraw = [sem(f"ld_wraw{w}") for w in range(4)]
        sel_built, consts_made = sem("sel_built"), sem("consts_made")
        xp_done, bc_split, dtin_done, negA_done = sem("xp_done"), sem("bc_split"), sem("dtin_done"), sem("negA_done")
        dtl_done, z_abs, softlog, dt_done = sem("dtl_done"), sem("z_abs"), sem("softlog"), sem("dt_done")
        b_bcast, c_bcast, c_kept = sem("b_bcast"), sem("c_bcast"), sem("c_kept")
        dA_done, dbx_done, scan_done, hc_done = sem("dA_done"), sem("dbx_done"), sem("scan_done"), sem("hc_done")
        y_added, y_taken = sem("y_added"), sem("y_taken")
        x_kept = sem("x_kept")
        ln_in, var_done, sdev_done, x_normed = sem("ln_in"), sem("var_done"), sem("sdev_done"), sem("x_normed")
        x_turned, xh_done, xl_done = sem("x_turned"), sem("xh_done"), sem("xl_done")
        gate_done, up_done, silu_done, h_done, hh_done, hl_done = (
            sem("gate_done"), sem("up_done"), sem("silu_done"), sem("h_done"), sem("hh_done"), sem("hl_done"))
        w_high, w_low = sem("w_high"), sem("w_low")
        dve_own, act_own, stored = sem("dve_own"), sem("act_own"), sem("stored")

        block = ctx.enter_context(nc.Block())

        @block.sync
        def _(sp):
            for dst, src in ((ident_sb[:], ident), (fold_sb[:], fold),
                             (xw_sb[:], xw.rearrange("(c p) r -> p c r", p=P)),
                             (dtw_sb[2 * NS:, :], dtw),
                             (dskip_sb[:], d_skip),
                             (alog_sb[:], a_log.rearrange("(c p) n -> p c n", p=P))):
                sp.dma_start(dst, src).then_inc(ld_small, 16)
            for c in range(DC):
                sp.dma_start(xT[:, c, :], x_fm[c * P:(c + 1) * P, :]).then_inc(ld_x[c], 16)
            sp.dma_start(wg0_sb[:], wg0.rearrange("(c p) m -> p c m", p=P)).then_inc(ld_w0, 16)
            sp.dma_start(wu0_sb[:], wu0.rearrange("(c p) m -> p c m", p=P)).then_inc(ld_w0, 16)
            sp.wait_ge(y_added, DC * NS)
            sp.dma_start(wd0_sb[:], wd0.rearrange("(m p) d -> p m d", p=P)).then_inc(ld_w0, 16)
            sp.wait_ge(ln_in, TT)
            for w, src in enumerate((wq, wk, wv, wo)):
                if w >= 2:
                    sp.wait_ge(w_low, w - 1)
                sp.dma_start(wraw[:, w % 2], src.rearrange("(c p) d -> p c d", p=P)).then_inc(ld_wraw[w], 16)
            for dst, src in ((cos_sb[:], cos.rearrange("(i p) d -> p i d", p=P)),
                             (sin_sb[:], sin.rearrange("(i p) d -> p i d", p=P)), (mask_sb[:], mask)):
                sp.dma_start(dst, src).then_inc(ld_tab, 16)

            def pad_keys(g, slot):
                for b in range(2):
                    sp.dma_start(k_pad[slot][64 * b:64 * b + 64, b::2, :],
                                 k_st[64 * b:64 * b + 64, ds(2 * g, 2), :]).then_inc(k_padded[slot], 16)

            def put_rows(g, use):
                sp.wait_ge(ring_read, use)
                for b in range(2):
                    for r in range(2):
                        sp.dma_start(q_st[64 * b + 48:64 * b + 49, ds(2 * g + r, 1), :],
                                     m_row[2 * r + b:2 * r + b + 1, :].unsqueeze(1)).then_inc(m_rows, 16)
            sp.wait_ge(k_kept, TT)
            sp.wait_ge(q_kept, TT)
            for slot in range(2):
                sp.wait_ge(pads_zeroed, slot + 1)
                pad_keys(slot, slot)
            put_rows(0, UNITS)

            def sync_body(g, slot, more=True):
                put_rows(g + 1, ring_base(g + 1))
                if more:
                    sp.wait_ge(st_full, EXPS * (g + 1))
                    pad_keys(g + 2, slot)
            sync_body(0, 0)
            with sp.Fori(0, 2) as k:
                for b in range(2):
                    sync_body(2 * k + 1 + b, 1 - b)
            sync_body(5, 1)
            sync_body(6, 0, False)
            sp.dma_start(shift_sb[:], shifts).then_inc(ld_shift, 16)

            def load_tile(m, slot):
                sp.dma_start(w_words[slot][:], w1_q[ds(m, 1)].rearrange("m r n -> (m r) n")).then_inc(ld_w1[slot], 16)
                sp.dma_start(w_scales[slot][:], w1_s[ds(m, 1), :].broadcast_to([P, NB * P])).then_inc(ld_w1[slot], 16)
                sp.dma_start(w_zeros[slot][:], w1_z[ds(m, 1), :].broadcast_to([P, NB * P // PACK])).then_inc(ld_w1[slot], 16)
            sp.wait_ge(pv_step, NG * TT)
            load_tile(0, 0)
            load_tile(1, 1)
            with sp.Fori(1, M1 // 2) as k:
                for u in range(2):
                    sp.wait_ge(w1_nib, 2 * k + u - 1)
                    sp.wait_ge(w1_scaled, 2 * k + u - 1)
                    load_tile(2 * k + u, u)
            sp.wait_ge(w1_nib, M1 - 2)
            sp.wait_ge(w1_scaled, M1 - 2)
            load_tile(M1 - 1, 0)
            for t in range(TT):
                sp.wait_ge(x_normed, 3 * TT + t + 1)
                sp.dma_start(out[0, t * P:(t + 1) * P, :], xn[:, t % 2, :]).then_inc(out_stored[t % 2], 16)
            for u in range(2):
                sp.wait_ge(out_stored[u], 16 * TT // 2)

        @block.tensor
        def _(pe):
            pe.wait_ge(ld_small, 6 * 16)
            for c in range(DC):
                pe.wait_ge(ld_x[c], 16)
                for h in range(2):
                    last = nc.tensor.matmul(banks(6 + h, 1)[0:2 * NS + DTR, :], xw_sb[:, c, :],
                                            xT[:, c, h * HALF:(h + 1) * HALF], start=(c == 0), stop=(c == DC - 1))
            last.then_inc(xp_done, 1)

            def dt_linear(c):
                for h in range(2):
                    last = nc.tensor.matmul(banks(4 + h, 1), dtw_sb[2 * NS:, c * P:(c + 1) * P],
                                            dt_in[2 * NS:2 * NS + DTR + 1, h * HALF:(h + 1) * HALF], start=True, stop=True)
                last.then_inc(dtl_done, 1)

            def bcast(row, bank, signal):
                for h in range(2):
                    last = nc.tensor.matmul(banks(bank + h, 1), sel[:, row, :], bc[:, h * HALF:(h + 1) * HALF],
                                            start=True, stop=True)
                last.then_inc(signal, 1)

            def add_y(slot, start, stop):
                for h in range(2):
                    last = nc.tensor.matmul(banks(6 + h, 1), ident_sb[:], hC[slot][:, h * HALF:(h + 1) * HALF],
                                            start=start, stop=stop)
                last.then_inc(y_added, 1)

            pe.wait_ge(dtin_done, 1)
            dt_linear(0)
            pe.wait_ge(bc_split, 1)
            pe.wait_ge(sel_built, 1)
            for c in range(DC):
                if c + 1 < DC:
                    pe.wait_ge(z_abs, c + 1)
                    pe.wait_ge(dt_done, c + 1)
                    if c == 1:
                        pe.wait_ge(c_kept, NS)
                    dt_linear(c + 1)
                def step(n, u, lagged, start=False, stop=False, first=False):
                    i = n + NS * c
                    if not first:
                        pe.wait_ge(scan_done, i - 1)
                    bcast(n, 2 * (u % 2), b_bcast)
                    if c == 0:
                        if first and u == 0:
                            pe.wait_ge(z_abs, 2)
                            pe.wait_ge(dt_done, 2)
                        else:
                            pe.wait_ge(c_kept, n)
                        bcast(n + NS, 4, c_bcast)
                    if lagged:
                        pe.wait_ge(hc_done, i - LAG + 1)
                        if start and c:
                            pe.wait_ge(y_taken, c)
                        add_y((u - LAG) % 4, start, stop)
                for n in range(4):
                    step(n, n, c > 0 or n == LAG, start=(n == LAG), stop=(n == LAG - 1), first=(c == 0 and n < 2))
                with pe.Fori(1, NS // 4) as k:
                    for u in range(4):
                        step(4 * k + u, u, True)
            for n in range(NS - LAG, NS):
                pe.wait_ge(hc_done, (DC - 1) * NS + n + 1)
                add_y(n % 4, False, n == NS - 1)

            def norm_stage(ln, make, turn=True, straight=False):
                def produce(t, u, first):
                    if not first:
                        pe.wait_ge(x_normed, TT * ln + t - 1)
                    make(t, u).then_inc(ln_in, 1)

                def turn_tile(t, u, first):
                    pe.wait_ge(x_normed, TT * ln + t + 1)
                    if not first:
                        pe.wait_ge(xl_done, TT * ln + t - 1)
                    for c in range(DC):
                        last = nc.tensor.transpose(ps[:, 2 + u, c * P:(c + 1) * P], xn[:, u, c * P:(c + 1) * P], ident_sb[:])
                    last.then_inc(x_turned, 1)

                produce(0, 0, True)
                produce(1, 1, True)
                if turn:
                    turn_tile(0, 0, True)
                    produce(2, 0, False)
                    turn_tile(1, 1, True)
                    produce(3, 1, False)
                    turn_tile(2, 0, False)
                    if straight:
                        for t in range(4, TT):
                            produce(t, t % 2, False)
                            turn_tile(t - 1, 1 - t % 2, False)
                    else:
                        with pe.Fori(2, TT // 2) as k:
                            for u in range(2):
                                produce(2 * k + u, u, False)
                                turn_tile(2 * k + u - 1, 1 - u, False)
                    turn_tile(TT - 1, 1, False)
                else:
                    with pe.Fori(1, TT // 2) as k:
                        for u in range(2):
                            produce(2 * k + u, u, False)

            def turn_residual(t, u):
                for c in range(DC):
                    last = nc.tensor.transpose(ps[:, u, c * P:(c + 1) * P], xT[:, c, t * P:(t + 1) * P], ident_sb[:])
                return last

            pe.wait_ge(y_taken, DC)
            norm_stage(0, turn_residual, straight=True)

            pe.wait_ge(ld_w0, 3 * 16)
            pe.wait_ge(xl_done, TT)

            def ffn0(m, u, first):
                for w, bank, free, signal in ((wg0_sb, 4 * u, silu_done, gate_done), (wu0_sb, 4 * u + 2, h_done, up_done)):
                    if not first:
                        pe.wait_ge(free, m - 1)
                    for c in range(DC):
                        for part in (xh, xl):
                            for h in range(2):
                                last = nc.tensor.matmul(banks(bank + h, 1), w[:, c, ds(m * P, P)],
                                                        part[:, c, h * HALF:(h + 1) * HALF],
                                                        start=(c == 0 and part is xh), stop=(c == DC - 1 and part is xl))
                    last.then_inc(signal, 1)
            ffn0(0, 0, True)
            ffn0(1, 1, True)
            with pe.Fori(1, M0 // 2) as k:
                for u in range(2):
                    ffn0(2 * k + u, u, False)

            def down0(t, u):
                for m in range(M0):
                    for part in (hh, hl):
                        last = nc.tensor.matmul(banks(u, 1), part[:, m, ds(t * P, P)], wd0_sb[:, m, :],
                                                start=(m == 0 and part is hh), stop=(m == M0 - 1 and part is hl))
                return last
            pe.wait_ge(h_done, M0)
            pe.wait_ge(hl_done, M0)
            norm_stage(1, down0)
            pe.wait_ge(xl_done, 2 * TT)
            pe.wait_ge(w_low, 4)
            pe.wait_ge(tables_made, 3)

            def project(w, src_h, src_l, t, bank, signal):
                for c in range(DC):
                    for part, s in ((src_h, 0), (src_l, 0), (src_h, 1)):
                        last = nc.tensor.matmul(banks(bank, 1), part[:, c, ds(t * P, P)], wsp[:, w, s, c, :],
                                                start=(c == 0 and part is src_h and s == 0), stop=(c == DC - 1 and s == 1))
                return last.then_inc(signal, 1) if signal is not None else last

            turned = banks(6, 2).bitcast(f16)

            def turn_stack(w, t):
                pe.wait_ge(stack_low, 2 * t + w + 1)
                for r in range(NP):
                    last = nc.tensor.transpose(turned[:, r * P:(r + 1) * P],
                                               tok_stack[:, w, 2 * r:2 * r + 2, :].rearrange("p h d -> p (h d)"), ident_h[:])
                last.then_inc((q_turned, k_turned)[w], 1)

            def qkv(t, u, first, lagged):
                if not first:
                    pe.wait_ge(roped, 2 * t - 3)
                project(0, xh, xl, t, 3 * u, q_proj)
                if lagged:
                    if not first:
                        pe.wait_ge(k_kept, t - 1)
                    turn_stack(0, t - 1)
                if not first:
                    pe.wait_ge(roped, 2 * t - 2)
                project(1, xh, xl, t, 3 * u + 1, k_proj)
                if lagged:
                    pe.wait_ge(q_kept, t)
                    turn_stack(1, t - 1)
                if not first:
                    pe.wait_ge(v_kept, t - 1)
                project(2, xh, xl, t, 3 * u + 2, v_proj)
            qkv(0, 0, True, False)
            qkv(1, 1, True, True)
            with pe.Fori(1, TT // 2) as k:
                for u in range(2):
                    qkv(2 * k + u, u, False, True)
            pe.wait_ge(k_kept, TT - 1)
            turn_stack(0, TT - 1)
            pe.wait_ge(q_kept, TT)
            turn_stack(1, TT - 1)

            def ring_slot(use, n):
                need = use + n - (n > 0)
                if not isinstance(need, int) or need > 0:
                    pe.wait_ge(ring_read, need)
                return n % 2

            def search(g, slot, i, use, n):
                for _, slices in max_units(i):
                    bank = ring_slot(use, n)
                    for a, key, w, col in slices:
                        dst = ps[:, bank, col:col + w]
                        diag = key + w == P * (i + 1)
                        last = nc.tensor.matmul(dst, q_st[:, ds(2 * g + a // 2, 1), i * P:(i + 1) * P].rearrange("p a t -> p (a t)"),
                                                k_pad[slot][:, a, key:key + w], start=True, stop=not diag)
                        if diag:
                            last = nc.tensor.matmul(dst[:, w - P:w], ident_b[:], mask_b[:], start=False, stop=True)
                    last.then_inc(ring_full, 1)
                    n += 1
                return n

            def turn_maxima(g, use, n):
                pe.wait_ge(m_negated, g + 1)
                bank = ring_slot(use, n)
                dst = ps[:, bank, :].bitcast(f16)
                for i in range(TT):
                    last = nc.tensor.transpose(dst[0:GH, i * P:(i + 1) * P], m_neg[:, i, :], ident_h[:])
                last.then_inc(ring_full, 1)
                return n + 1

            def keys(g, slot, j, e):
                w = T - P * j
                for heads in exp_units(j):
                    bank = 2 + 2 * (e % 2)
                    if not (isinstance(g, int) and g == 0 and e < 2):
                        pe.wait_ge(exp_done, EXPS * g + e - 1)
                    for b, a in enumerate(heads):
                        row = ds(2 * g + a // 2, 1)
                        for h in range(2 if w > HALF else 1):
                            lo, hi = h * HALF, min(w, (h + 1) * HALF)
                            dst = ps[:, bank + b + h, 0:hi - lo]
                            last = nc.tensor.matmul(dst, k_pad[slot][:, a, j * P:(j + 1) * P],
                                                    q_st[:, row, j * P + lo:j * P + hi].rearrange("p a t -> p (a t)"),
                                                    start=True, stop=(h == 1))
                            if h == 0:
                                last = nc.tensor.matmul(dst[:, 0:P], mask_b[:], ident_b[:], start=False, stop=True)
                    last.then_inc(st_full, 1)
                    e += 1
                return e

            def values(g, slot, q, e):
                j = KEYS[q]
                pe.wait_ge(exp_done, EXPS * g + e)
                pieces = ([(6, P * j, HALF, 0)] if j < 4 else []) + [(7, max(P * j - HALF, 0), HALF, max(HALF - P * j, 0))]
                for bank, lo, hi, col in pieces:
                    for a in range(GH):
                        last = nc.tensor.matmul(ps[32 * a:32 * a + 32, bank, lo:hi], v_ring[slot][:, j, a, :],
                                                p_t[q % 2][:, a, col:col + hi - lo], start=(q == 0), stop=(q == TT - 1))
                last.then_inc(pv_step, 1)

            def turn_out(use, n):
                for half in range(2):
                    bank = ring_slot(use, n)
                    for b in range(4):
                        i = 4 * half + b
                        last = nc.tensor.transpose(ps[:, bank, b * P:(b + 1) * P], o_raw[:, i * P:(i + 1) * P], ident_sb[:])
                    last.then_inc(ring_full, 1)
                    n += 1
                return n

            def body(g, slot, pads, first=False, final=False):
                use, n, e, before = ring_base(g), 0, 0, 0
                pe.wait_ge(m_rows, 64 * (g + 1))
                for q, j in enumerate(KEYS):
                    start = e
                    e = keys(g, slot, j, e)
                    if not final:
                        if q == 0:
                            pe.wait_ge(k_padded[1 - slot], 32 * pads)
                        for i in MAXES[q]:
                            n = search(g + 1, 1 - slot, i, use, n)
                    if q == 2 and not first:
                        pe.wait_ge(o_kept, g)
                        n = turn_out(use, n)
                    if q == TT - 1 and not final:
                        n = turn_maxima(g + 1, use, n)
                    if q == 1:
                        pe.wait_ge(v_ringed, g + 1)
                        if not first:
                            pe.wait_ge(o_kept, g)
                    if q:
                        values(g, slot, q - 1, start)
                values(g, slot, TT - 1, e)
            pe.wait_ge(roped, 2 * TT)
            pe.wait_ge(v_kept, TT)
            pe.wait_ge(k_kept, TT)
            pe.wait_ge(k_padded[0], 32)
            n = 0
            for tiles in MAXES:
                for i in tiles:
                    n = search(0, 0, i, 0, n)
            turn_maxima(0, 0, n)
            body(0, 0, 1, first=True)
            with pe.Fori(0, 3) as k:
                for b in range(2):
                    body(2 * k + 1 + b, 1 - b, k + 2)
            body(NG - 1, 1, 0, final=True)
            pe.wait_ge(o_kept, NG)
            turn_out(ring_base(NG - 1) + 2, 0)

            for t in range(TT):
                if t < 2:
                    pe.wait_ge(ring_read, ring_base(NG - 1) + 4)
                else:
                    pe.wait_ge(ol_done, t - 1)
                for c in range(DC):
                    last = nc.tensor.transpose(ps[:, 2 + t % 2, c * P:(c + 1) * P], o_tok[:, t, c * P:(c + 1) * P], ident_sb[:])
                last.then_inc(o_turned, 1)
            pe.wait_ge(ol_done, TT)
            norm_stage(2, lambda t, u: project(3, oh, ol, t, u, None))
            pe.wait_ge(xl_done, 3 * TT)

            def ffn1(m, u, first):
                pe.wait_ge(w1_low, m + 1)
                for w, bank, free, signal in ((0, 4 * u, silu1_done, gate1_done), (1, 4 * u + 2, h1_done, up1_done)):
                    if not first:
                        pe.wait_ge(free, m - 1)
                    for c in range(DC):
                        for s, part in ((0, x3h), (0, x3l), (1, x3h)):
                            for h in range(2):
                                last = nc.tensor.matmul(banks(bank + h, 1), gu[u][:, s, w * DC + c, :],
                                                        part[:, c, h * HALF:(h + 1) * HALF],
                                                        start=(c == 0 and s == 0 and part is x3h), stop=(c == DC - 1 and s == 1))
                    last.then_inc(signal, 1)
            ffn1(0, 0, True)
            ffn1(1, 1, True)
            with pe.Fori(1, M1 // 2) as k:
                for u in range(2):
                    ffn1(2 * k + u, u, False)
            ffn1(M1 - 1, 0, False)

            def down1(t, u):
                for m in range(M1):
                    for part, s in ((h1h, 0), (h1l, 0), (h1h, 1)):
                        last = nc.tensor.matmul(banks(u, 1), part[:, m, ds(t * P, P)], wd1[:, s, m, :],
                                                start=(m == 0 and part is h1h and s == 0), stop=(m == M1 - 1 and s == 1))
                return last
            pe.wait_ge(h1_done, M1)
            pe.wait_ge(h1l_done, M1)
            norm_stage(3, down1, turn=False)

        @block.scalar
        def _(act):
            own = Tally(act, act_own)
            nc.scalar.preload_act_table_set("natural_log_exp_and_others")
            act.wait_ge(ld_small, 6 * 16)
            own.done(nc.scalar.activation(negA[:], alog_sb[:], ACT.Exp))
            nc.scalar.mul(negA[:], negA[:], -1.0).then_inc(negA_done, 1)
            act.wait_ge(negA_done, 1)
            act.wait_ge(xp_done, 1)
            act.wait_ge(consts_made, 3)
            nc.scalar.copy(dt_in[2 * NS:2 * NS + DTR, :], banks(6, 2)[2 * NS:2 * NS + DTR, :]).then_inc(dtin_done, 1)

            def soft_log(c):
                act.wait_ge(dtl_done, c + 1)
                if c:
                    act.wait_ge(dt_done, c)
                nc.scalar.activation(e_[:], banks(4, 2), ACT.Abs).then_inc(z_abs, 1)
                act.wait_ge(z_abs, c + 1)
                own.done(nc.scalar.activation(e_[:], e_[:], ACT.Exp, scale=-1.0))
                nc.scalar.activation(dt_[:, c, :], e_[:], ACT.Square, scale=3.0 ** -0.5).then_inc(softlog, 1)
                nc.scalar.activation(small_e[:], e_[:], ACT.Relu, bias=series_sb[:], scale=-1.0).then_inc(softlog, 1)
                nc.scalar.activation(log_e[:], e_[:], ACT.Ln, bias=1.0).then_inc(softlog, 1)

            act.wait_ge(bc_split, 1)
            soft_log(0)
            for c in range(DC):
                if c + 1 < DC:
                    soft_log(c + 1)
                act.wait_ge(dt_done, c + 1)

                def step(n, u, first):
                    i = n + NS * c
                    if not (c == 0 and first):
                        act.wait_ge(scan_done, i - 1)
                    nc.scalar.activation(dA[:, u, :], dt_[:, c, :], ACT.Exp, scale=negA[:, c, ds(n, 1)]).then_inc(dA_done, 1)
                    if c == 0:
                        act.wait_ge(c_bcast, n + 1)
                        nc.scalar.copy(c_all[:, n, :], banks(4, 2)).then_inc(c_kept, 1)
                step(0, 0, True)
                step(1, 1, True)
                with act.Fori(1, NS // 2) as k:
                    for u in range(2):
                        step(2 * k + u, u, False)

            def norm_stage(ln, turn=True):
                def high(t, u):
                    act.wait_ge(x_turned, TT * ln + t + 1)
                    nc.scalar.copy(XH[ln][:, :, ds(t * P, P)], ps[:, 2 + u, :].rearrange("p (c t) -> p c t", c=DC)).then_inc(xh_done, 1)

                def root(t):
                    act.wait_ge(var_done, TT * ln + t + 1)
                    nc.scalar.activation(sdev[:], vare[:], ACT.Sqrt).then_inc(sdev_done, 1)
                root(0)
                if turn:
                    high(0, 0)
                root(1)
                with act.Fori(1, TT // 2) as k:
                    for u in range(2):
                        if turn:
                            high(2 * k + u - 1, 1 - u)
                        root(2 * k + u)
                if turn:
                    high(TT - 1, 1)
            XH = {0: xh, 1: xh}
            norm_stage(0)

            for w in range(4):
                act.wait_ge(ld_wraw[w], 16)
                nc.scalar.mul(wsp[:, w, 0], wraw[:, w % 2], WS).then_inc(w_high, 1)

            def ffn0(m, u, first):
                act.wait_ge(gate_done, m + 1)
                if not first:
                    act.wait_ge(h_done, m - 1)
                nc.scalar.activation(sg[:, u, :], banks(4 * u, 2), ACT.Silu).then_inc(silu_done, 1)
                act.wait_ge(h_done, m + 1)
                nc.scalar.copy(hh[:, m, :], h32[:, u, :]).then_inc(hh_done, 1)
            ffn0(0, 0, True)
            ffn0(1, 1, True)
            with act.Fori(1, M0 // 2) as k:
                for u in range(2):
                    ffn0(2 * k + u, u, False)
            norm_stage(1)
            act.wait_ge(ld_tab, 3 * 16)
            nc.scalar.copy(mask_b[:], mask_sb[:]).then_inc(tables_made, 1)
            nc.scalar.copy(ident_b[:], ident_sb[:]).then_inc(tables_made, 1)
            nc.scalar.copy(ident_h[:], ident_sb[:]).then_inc(tables_made, 1)
            nc.scalar.preload_act_table_set("natural_log_exp_and_others")

            def keep_queries(t):
                act.wait_ge(q_turned, t + 1)
                nc.scalar.copy(q_st[:, :, ds(t * P, P)], banks(6, 2).bitcast(f16).rearrange("p (r t) -> p r t", r=NP)).then_inc(q_kept, 1)

            def stack(t, u, first):
                for w in range(2):
                    act.wait_ge(rope_summed, 2 * t + w + 1)
                    if not first:
                        act.wait_ge((q_turned, k_turned)[w], t)
                    dst = tok_stack[:, w, :, 0:64 if w == 0 else 32].rearrange("p h (b d) -> p h b d", b=4 if w == 0 else 2)
                    nc.scalar.copy(dst[:, :, 0:3:2, :] if w == 0 else dst,
                                   rot_a[:, w].unsqueeze(2).broadcast_to([P, NH, 2, HD])).then_inc(stack_high, 1)
                act.wait_ge(v_proj, t + 1)
                nc.scalar.mul(v_tok[:, t, :], banks(3 * u + 2, 1), 1.0 / WS).then_inc(v_kept, 1)
            act.wait_ge(stacks_set, 2)
            stack(0, 0, True)
            keep_queries(0)
            stack(1, 1, False)
            with act.Fori(1, TT // 2) as k:
                for u in range(2):
                    keep_queries(2 * k + u - 1)
                    stack(2 * k + u, u, False)
            keep_queries(TT - 1)

            def keep_out(g, use):
                act.wait_ge(pv_step, TT * (g + 1))
                act.wait_ge(ring_read, use)
                nc.scalar.copy(o_raw[:], banks(6, 2)).then_inc(o_kept, 1)

            def body(g, first=False):
                e = 0
                for q, j in enumerate(KEYS):
                    w = T - P * j
                    if not (first and q < 2):
                        act.wait_ge(pv_step, TT * g + q - 1)
                    for heads in exp_units(j):
                        act.wait_ge(st_full, EXPS * g + e + 1)
                        bank, a = 2 + 2 * (e % 2), heads[0]
                        if len(heads) == 1:
                            dst, src = p_t[q % 2][:, a, 0:w], banks(bank, 2)[:, 0:w]
                        else:
                            dst, src = p_t[q % 2][:, a:a + 2, 0:w], ps[:, bank:bank + 2, 0:w]
                        nc.scalar.activation(dst, src, ACT.Exp, scale=float(HD) ** -0.5).then_inc(exp_done, 1)
                        e += 1
                    if q == 0 and not first:
                        keep_out(g - 1, ring_base(g))
            body(0, True)
            with act.Fori(1, NG) as g:
                body(g)
            keep_out(NG - 1, ring_base(NG - 1) + 2)

            def high_out(t):
                act.wait_ge(o_turned, t + 1)
                nc.scalar.copy(oh[:, :, t * P:(t + 1) * P], ps[:, 2 + t % 2, :].rearrange("p (c t) -> p c t", c=DC)).then_inc(oh_done, 1)
            for t in range(TT):
                high_out(t)
            XH[2] = x3h
            norm_stage(2)
            def weights_high(m, u, first=False):
                act.wait_ge(w1_scaled, m + 1)
                if not first:
                    act.wait_ge(up1_done, m - 1)
                nc.scalar.mul(gu[u][:, 0], w_full[:, 0:2 * DC * P].rearrange("p (b n) -> p b n", n=P), WS).then_inc(w1_high, 1)
                nc.scalar.mul(wd1[:, 0, m, :], w_full[:, 2 * DC * P:], WS).then_inc(w1_high, 1)

            def ffn1(m, u, first):
                act.wait_ge(gate1_done, m + 1)
                if not first:
                    act.wait_ge(h1_done, m - 1)
                nc.scalar.activation(sg1[:, u, :], banks(4 * u, 2), ACT.Silu, scale=1.0 / WS).then_inc(silu1_done, 1)
                act.wait_ge(h1_done, m + 1)
                nc.scalar.copy(h1h[:, m, :], h132[:, u, :]).then_inc(h1h_done, 1)
            weights_high(0, 0, True)
            weights_high(1, 1, True)
            ffn1(0, 0, True)
            weights_high(2, 0)
            ffn1(1, 1, True)
            with act.Fori(1, M1 // 2) as k:
                for u in range(2):
                    weights_high(2 * k + u + 1, 1 - u)
                    ffn1(2 * k + u, u, False)
            ffn1(M1 - 1, 0, False)
            norm_stage(3, turn=False)

        @block.gpsimd
        def _(pool):
            for c in range(DC):
                def step(n, u, first):
                    i = n + NS * c
                    pool.wait_ge(scan_done, i + 1)
                    if c == 0:
                        pool.wait_ge(c_kept, n + 1)
                    if not first:
                        pool.wait_ge(y_added, i - 3)
                    nc.gpsimd.tensor_tensor(hC[u][:], hst[:, u % 2, :], c_all[:, n, :], ALU.mult).then_inc(hc_done, 1)
                for n in range(4):
                    step(n, n, c == 0)
                with pool.Fori(1, NS // 4) as k:
                    for u in range(4):
                        step(4 * k + u, u, False)

            def keep(ln):
                with pool.Fori(0, TT // 2) as k:
                    for u in range(2):
                        pool.wait_ge(x_normed, TT * ln + 2 * k + u + 1)
                        nc.gpsimd.tensor_copy(xtok[:, 2 * k + u, :], xn[:, u, :]).then_inc(x_kept, 1)
            keep(0)
            keep(1)
            pool.wait_ge(w_low, 4)
            nc.gpsimd.memset(tok_stack[:], 0.0).then_inc(stacks_set, 1)
            pool.wait_ge(stacks_set, 1)
            nc.gpsimd.memset(tok_stack[:, 1, :, 48:49], 1.0).then_inc(stacks_set, 1)
            for slot in range(2):
                nc.gpsimd.memset(v_ring[slot][:], 1.0).then_inc(v_ones, 1)
            nc.gpsimd.memset(k_pad[0][:], 0.0).then_inc(pads_zeroed, 1)

            def stack(t):
                for w in range(2):
                    pool.wait_ge(roped, 2 * t + w + 1)
                    nc.gpsimd.tensor_tensor(rot_a[:, w], rot_a[:, w], rot_b[:, w], ALU.add).then_inc(rope_summed, 1)
                for w in range(2):
                    pool.wait_ge(stack_high, 2 * t + w + 1)
                    at = 16 if w == 0 else 32
                    nc.gpsimd.tensor_tensor(tok_stack[:, w, :, at:at + HD], rot_a[:, w], tok_stack[:, w, :, 0:HD],
                                            ALU.subtract).then_inc(stack_low, 1)
            with pool.Fori(0, TT) as t:
                stack(t)
            pool.wait_ge(v_proj, TT)
            nc.gpsimd.memset(k_pad[1][:], 0.0).then_inc(pads_zeroed, 1)
            pool.wait_ge(v_kept, TT)
            pool.wait_ge(v_ones, 2)

            def ring_values(g, slot, first=False):
                if not first:
                    pool.wait_ge(pv_step, TT * (g - 1))
                nc.gpsimd.tensor_copy(v_ring[slot][:, :, :, 0:HD],
                                      v_tok[:, :, ds(g * GH * HD, GH * HD)].rearrange("p i (a d) -> p i a d", a=GH)).then_inc(v_ringed, 1)
            ring_values(0, 0, True)
            ring_values(1, 1, True)
            with pool.Fori(1, NG // 2) as k:
                for u in range(2):
                    ring_values(2 * k + u, u)
            pool.wait_ge(w1_full, 1)
            nc.gpsimd.tensor_tensor(w_full[:], w_full[:], w_scales[0][:], ALU.mult).then_inc(w1_scaled, 1)
            keep(2)
            with pool.Fori(0, M1 // 2) as k:
                for u in range(2):
                    m = 2 * k + u + 1
                    pool.wait_ge(w1_full, m + 1)
                    nc.gpsimd.tensor_tensor(w_full[:], w_full[:], w_scales[1 - u][:], ALU.mult).then_inc(w1_scaled, 1)

        @block.vector
        def _(dve):
            own = Tally(dve, dve_own)
            dve.wait_ge(ld_small, 6 * 16)
            nc.vector.tensor_copy(sel[:], fold_sb[:].unsqueeze(2).broadcast_to([P, 2 * NS, P])).then_inc(sel_built, 1)
            nc.vector.tensor_scalar(dskip_sb[:], dskip_sb[:], 1.0, None, ALU.add).then_inc(consts_made, 1)
            nc.vector.memset(series_sb[:], SERIES).then_inc(consts_made, 1)
            nc.vector.memset(dt_in[2 * NS:4 * NS, :], 1.0).then_inc(consts_made, 1)
            own.done(nc.vector.memset(bc[:], 0.0))
            dve.wait_ge(xp_done, 1)
            R = 2 * NS
            own.done(nc.vector.tensor_copy(bc[0:R, :], banks(6, 2)[0:R, :]))
            own.done(nc.vector.tensor_tensor(rest[0:R, :], banks(6, 2)[0:R, :], bc[0:R, :], ALU.subtract))
            own.done(nc.vector.tensor_copy(mid[0:R, :], rest[0:R, :]))
            own.done(nc.vector.tensor_copy(bc[R:2 * R, :], mid[0:R, :]))
            nc.vector.tensor_tensor(bc[2 * R:3 * R, :], rest[0:R, :], mid[0:R, :], ALU.subtract).then_inc(bc_split, 1)

            def make_dt(c):
                d = dt_[:, c, :]
                dve.wait_ge(softlog, 3 * c + 1)
                own.done(nc.vector.scalar_tensor_tensor(d, e_[:], -0.5, d, ALU.mult, ALU.add))
                own.done(nc.vector.scalar_tensor_tensor(d, d, 1.0, e_[:], ALU.add, ALU.mult))
                dve.wait_ge(softlog, 3 * c + 3)
                own.done(nc.vector.copy_predicated(log_e[:], small_e[:].bitcast(mybir.dt.uint16), d))
                dve.wait_ge(z_abs, c + 1)
                nc.vector.scalar_tensor_tensor(d, banks(4, 2), 0.0, log_e[:], ALU.max, ALU.add).then_inc(dt_done, 1)
                dve.wait_ge(dt_done, c + 1)
                own.done(nc.vector.tensor_tensor(dtx[:, c, :], d, xT[:, c, :], ALU.mult))

            def dbx(n, u, c):
                dve.wait_ge(b_bcast, n + NS * c + 1)
                nc.vector.tensor_tensor(banks(2 * u, 2), dtx[:, c, :], banks(2 * u, 2), ALU.mult).then_inc(dbx_done, 1)

            def scan(n, u, c, first=False):
                i = n + NS * c
                dve.wait_ge(dA_done, i + 1)
                dve.wait_ge(dbx_done, i + 1)
                if not (c == 0 and first):
                    dve.wait_ge(hc_done, i - 1)
                nc.vector.tensor_tensor_scan(hst[:, u, :], dA[:, u, :], banks(2 * u, 2), 0.0, ALU.mult, ALU.add).then_inc(scan_done, 1)

            def take_y(c):
                dve.wait_ge(y_added, NS * (c + 1))
                nc.vector.scalar_tensor_tensor(xT[:, c, :], xT[:, c, :], dskip_sb[:, c:c + 1], banks(6, 2),
                                               ALU.mult, ALU.add).then_inc(y_taken, 1)

            make_dt(0)
            dve.wait_ge(consts_made, 3)
            for c in range(DC):
                if c + 1 < DC:
                    make_dt(c + 1)
                for n in range(4):
                    dbx(n, n % 2, c)
                    scan(n, n % 2, c, n < 2)
                    if c and n == LAG - 1:
                        take_y(c - 1)
                with dve.Fori(2, NS // 2) as k:
                    for u in range(2):
                        dbx(2 * k + u, u, c)
                        scan(2 * k + u, u, c)
            take_y(DC - 1)

            def norm_stage(ln, scale, turn=True):
                def stats(t, u):
                    dve.wait_ge(ln_in, TT * ln + t + 1)
                    if ln:
                        dve.wait_ge(x_kept, TT * (ln - 1) + t + 1)
                    src = banks(u, 1)
                    if ln == 3:
                        src = xtok[:, t, :]
                        own.done(nc.vector.tensor_scalar(o_half[:], banks(u, 1), scale, None, ALU.mult))
                        own.done(nc.vector.tensor_tensor(src, src, o_half[:], ALU.add))
                    elif scale is not None:
                        src = xtok[:, t, :]
                        own.done(nc.vector.scalar_tensor_tensor(src, banks(u, 1), scale, src, ALU.mult, ALU.add))
                    own.done(nc.vector.bn_stats(st6[:], src))
                    own.done(nc.vector.bn_aggr(mv[:], st6[:]))
                    nc.vector.tensor_scalar(vare[:], mv[:, 1:2], EPS, None, ALU.add).then_inc(var_done, 1)

                def normalise(t, u, first=False):
                    dve.wait_ge(sdev_done, TT * ln + t + 1)
                    if ln == 3 and not first:
                        dve.wait_ge(out_stored[u], 16 * (t // 2))
                    elif ln or not first:
                        dve.wait_ge(x_kept, TT * ln + t - 1)
                        if turn or first:
                            dve.wait_ge(x_turned, TT * ln + t - 1)
                    own.done(nc.vector.reciprocal(rstd[:], sdev[:]))
                    src = banks(u, 1) if scale is None else xtok[:, t, :]
                    nc.vector.tensor_scalar(xn[:, u, :], src, mv[:, 0:1], rstd[:], ALU.subtract, ALU.mult).then_inc(x_normed, 1)

                def low(t, u):
                    dve.wait_ge(xh_done, TT * ln + t + 1)
                    nc.vector.tensor_tensor(XL[ln][:, :, ds(t * P, P)], ps[:, 2 + u, :].rearrange("p (c t) -> p c t", c=DC),
                                            XH[ln][:, :, ds(t * P, P)], ALU.subtract).then_inc(xl_done, 1)
                stats(0, 0)
                normalise(0, 0, True)
                dve.wait_ge(x_normed, TT * ln + 1)
                stats(1, 1)
                if turn:
                    low(0, 0)
                normalise(1, 1, True)
                for t in range(2, TT):
                    dve.wait_ge(x_normed, TT * ln + t)
                    stats(t, t % 2)
                    if turn:
                        low(t - 1, 1 - t % 2)
                    normalise(t, t % 2)
                if turn:
                    low(TT - 1, 1)
            XH = {0: xh, 1: xh}
            XL = {0: xl, 1: xl}
            norm_stage(0, None)

            for w in range(4):
                dve.wait_ge(w_high, w + 1)
                nc.vector.scalar_tensor_tensor(wsp[:, w, 1], wraw[:, w % 2], WS, wsp[:, w, 0], ALU.mult, ALU.subtract).then_inc(w_low, 1)

            def ffn0(m, u, first):
                dve.wait_ge(silu_done, m + 1)
                dve.wait_ge(up_done, m + 1)
                if not first:
                    dve.wait_ge(hl_done, m - 1)
                nc.vector.tensor_tensor(h32[:, u, :], sg[:, u, :], banks(4 * u + 2, 2), ALU.mult).then_inc(h_done, 1)
                dve.wait_ge(hh_done, m + 1)
                nc.vector.tensor_tensor(hl[:, m, :], h32[:, u, :], hh[:, m, :], ALU.subtract).then_inc(hl_done, 1)
            ffn0(0, 0, True)
            ffn0(1, 1, True)
            with dve.Fori(1, M0 // 2) as k:
                for u in range(2):
                    ffn0(2 * k + u, u, False)
            norm_stage(1, 1.0)
            dve.wait_ge(ld_tab, 3 * 16)

            def rope(w, t, u, first):
                dve.wait_ge((q_proj, k_proj)[w], t + 1)
                if not first:
                    dve.wait_ge(stack_low, 2 * t - 1 + w)
                src = banks(3 * u + w, 1).rearrange("p (h d) -> p h d", h=NH)
                h2 = HD // 2
                tab = lambda x, a, b: x[:, t, a:b].unsqueeze(1).broadcast_to([P, NH, b - a])
                nc.vector.tensor_tensor(rot_a[:, w], src, tab(cos_sb, 0, HD), ALU.mult)
                nc.vector.tensor_tensor(rot_b[:, w, :, 0:h2], src[:, :, h2:HD], tab(sin_sb, 0, h2), ALU.mult)
                nc.vector.tensor_tensor(rot_b[:, w, :, h2:HD], src[:, :, 0:h2], tab(sin_sb, h2, HD), ALU.mult).then_inc(roped, 1)

            def keep_keys(t):
                dve.wait_ge(k_turned, t + 1)
                nc.vector.tensor_copy(k_st[:, :, ds(t * P, P)], banks(6, 2).bitcast(f16).rearrange("p (r t) -> p r t", r=NP)).then_inc(k_kept, 1)

            for t in range(2):
                rope(0, t, t, t == 0)
                rope(1, t, t, t == 0)
                if t:
                    keep_keys(t - 1)
            with dve.Fori(1, TT // 2) as k:
                for u in range(2):
                    rope(0, 2 * k + u, u, False)
                    rope(1, 2 * k + u, u, False)
                    keep_keys(2 * k + u - 1)
            keep_keys(TT - 1)

            def maxima(i, use, n):
                for dst, slices in max_units(i):
                    w = slices[0][2]
                    dve.wait_ge(ring_full, use + n + 1)
                    nc.vector.reduce_max(dst, ps[:, n % 2, 0:len(slices) * w].rearrange("p (a w) -> p a w", a=len(slices)), AX).then_inc(ring_read, 1)
                    n += 1
                return n

            def negate(g, use, n):
                dve.wait_ge(ring_read, use + n)
                nc.vector.tensor_tensor(m_a[:, 4:TT, :], m_a[:, 4:TT, :], m_b[:], ALU.max).then_inc(m_joined, 1)
                dve.wait_ge(m_joined, g + 1)
                nc.vector.tensor_scalar(m_neg[:], m_a[:], -1.0, None, ALU.mult).then_inc(m_negated, 1)
                dve.wait_ge(m_negated, g + 1)

            def keep_rows(g, use, n):
                dve.wait_ge(ring_full, use + n + 1)
                if not (isinstance(g, int) and g == 0):
                    dve.wait_ge(m_rows, 64 * g)
                nc.vector.tensor_copy(m_row[0:GH, :], ps[0:GH, n % 2, :].bitcast(f16)).then_inc(ring_read, 1)

            def divide(g, use, n):
                for half in range(2):
                    dve.wait_ge(ring_full, use + n + 1)
                    src = ps[:, n % 2, :].rearrange("p (i a d) -> p i a d", i=4, a=GH)
                    nc.vector.reciprocal(r_den[:].unsqueeze(3), src[:, :, :, HD:HD + 1]).then_inc(r_made, 1)
                    dve.wait_ge(r_made, 2 * g + half + 1)
                    nc.vector.tensor_tensor(o_tok[:, 4 * half:4 * half + 4, ds(g * GH * HD, GH * HD)].rearrange("p i (a d) -> p i a d", a=GH),
                                            src[:, :, :, 0:HD], r_den[:].unsqueeze(3).broadcast_to([P, 4, GH, HD]),
                                            ALU.mult).then_inc(ring_read, 1)
                    dve.wait_ge(ring_read, use + n + 1)
                    n += 1
                return n

            n = 0
            for tiles in MAXES:
                for i in tiles:
                    n = maxima(i, 0, n)
            negate(0, 0, n)
            keep_rows(0, 0, n)

            def body(g, first=False, final=False):
                use, n = ring_base(g), 0
                for q in range(TT):
                    if not final:
                        for i in MAXES[q]:
                            n = maxima(i, use, n)
                    if q == 2 and not first:
                        n = divide(g - 1, use, n)
                    if q == TT - 1 and not final:
                        negate(g + 1, use, n)
                        keep_rows(g + 1, use, n)
            body(0, first=True)
            with dve.Fori(1, NG - 1) as g:
                body(g)
            body(NG - 1, final=True)
            divide(NG - 1, ring_base(NG - 1) + 2, 0)

            def low_out(t):
                dve.wait_ge(oh_done, t + 1)
                nc.vector.tensor_tensor(ol[:, :, t * P:(t + 1) * P], ps[:, 2 + t % 2, :].rearrange("p (c t) -> p c t", c=DC),
                                        oh[:, :, t * P:(t + 1) * P], ALU.subtract).then_inc(ol_done, 1)
            for t in range(TT):
                low_out(t)
            def unpack(m, u, loads):
                dve.wait_ge(ld_w1[u], 48 * loads)
                nib = z_nib[:].rearrange("p (n h) -> p n h", h=2)
                byte = w_zeros[u][:].bitcast(u8).unsqueeze(2)
                nc.vector.tensor_scalar(nib[:, :, 0:1], byte, 15, None, ALU.bitwise_and)
                nc.vector.tensor_scalar(nib[:, :, 1:2], byte, 4, None, ALU.logical_shift_right)
                nc.vector.tensor_scalar(w_nib[:], w_words[u][:], shift_sb[:, 0:1], 15, ALU.logical_shift_right, ALU.bitwise_and).then_inc(w1_nib, 1)
                dve.wait_ge(w1_nib, m + 1)
                nc.vector.scalar_tensor_tensor(w_full[:], w_nib[:], 1.0, z_nib[:], ALU.subtract, ALU.subtract).then_inc(w1_full, 1)
                dve.wait_ge(w1_full, m + 1)

            dve.wait_ge(ld_shift, 16)
            unpack(0, 0, 1)
            XH[2], XL[2] = x3h, x3l
            norm_stage(2, 1.0 / WS)
            def weights_low(m, u):
                dve.wait_ge(w1_high, 2 * m + 2)
                nc.vector.scalar_tensor_tensor(gu[u][:, 1].rearrange("p b n -> p (b n)"), w_full[:, 0:2 * DC * P], WS,
                                               gu[u][:, 0].rearrange("p b n -> p (b n)"), ALU.mult, ALU.subtract)
                nc.vector.scalar_tensor_tensor(wd1[:, 1, m, :], w_full[:, 2 * DC * P:], WS, wd1[:, 0, m, :],
                                               ALU.mult, ALU.subtract).then_inc(w1_low, 1)
                dve.wait_ge(w1_low, m + 1)

            def ffn1(m, u, first):
                dve.wait_ge(silu1_done, m + 1)
                dve.wait_ge(up1_done, m + 1)
                if not first:
                    dve.wait_ge(h1l_done, m - 1)
                nc.vector.scalar_tensor_tensor(h132[:, u, :], banks(4 * u + 2, 2), 1.0 / WS, sg1[:, u, :], ALU.mult, ALU.mult).then_inc(h1_done, 1)
                dve.wait_ge(h1h_done, m + 1)
                nc.vector.tensor_tensor(h1l[:, m, :], h132[:, u, :], h1h[:, m, :], ALU.subtract).then_inc(h1l_done, 1)
            weights_low(0, 0)
            unpack(1, 1, 1)
            weights_low(1, 1)
            unpack(2, 0, 2)
            ffn1(0, 0, True)
            weights_low(2, 0)
            unpack(3, 1, 2)
            ffn1(1, 1, True)
            with dve.Fori(1, M1 // 2 - 1) as k:
                for u in range(2):
                    weights_low(2 * k + u + 1, 1 - u)
                    unpack(2 * k + u + 2, u, k + 2)
                    ffn1(2 * k + u, u, False)
            weights_low(M1 - 2, 1)
            unpack(M1 - 1, 0, M1 // 2 + 1)
            ffn1(M1 - 3, 0, False)
            weights_low(M1 - 1, 0)
            ffn1(M1 - 2, 1, False)
            ffn1(M1 - 1, 0, False)
            norm_stage(3, 1.0 / WS, turn=False)


def kernel(**inputs):
    import numpy as np
    import concourse.bacc as bacc
    from concourse.bass_utils import run_bass_kernel_spmd

    nc = bacc.Bacc("TRN2", target_bir_lowering=False, num_devices=1)
    get = {k: np.asarray(v) for k, v in inputs.items()}
    xw = get["L0_attn_x_proj_w"].T
    pos = np.arange(T, dtype=np.float32)
    theta = (1.0 / 10000.0 ** (np.arange(0, HD, 2, dtype=np.float32) / HD)).astype(np.float32)
    angle = np.outer(pos, theta).astype(np.float32)
    cos = np.concatenate([np.cos(angle), np.cos(angle)], -1) / np.float32(WS)
    sin = np.concatenate([-np.sin(angle), np.sin(angle)], -1) / np.float32(WS)
    tok, key = np.arange(P)[:, None], np.arange(P)[None, :]

    def tiles(kind, rows):
        per = P if kind != "zeros" else P // PACK
        at = np.zeros((M1, rows, 3 * DC, per), get["L1_ffn_gate_" + kind].dtype)
        for i, name in enumerate(("gate", "up")):
            a = get[f"L1_ffn_{name}_{kind}"].reshape(DC, rows, -1)
            for m in range(M1):
                part = a[:, :, m * per:(m + 1) * per]
                at[m, :, i * DC:(i + 1) * DC, :part.shape[2]] = part.transpose(1, 0, 2)
        a = get["L1_ffn_down_" + kind]
        for m in range(M1):
            part = a[m * rows:(m + 1) * rows]
            at[m, :part.shape[0], 2 * DC:] = part.reshape(part.shape[0], DC, per)
        return at.reshape(M1, rows, -1)

    arrays = {
        "x_fm": get["L0_attn_x"][0].T, "a_log": get["L0_attn_A_log"], "d_skip": get["L0_attn_D"].reshape(DC, P).T,
        "xw": np.concatenate([xw[:, DTR:], xw[:, :DTR]], 1), "dtw": np.concatenate([get["L0_attn_dt_proj_w"].T, get["L0_attn_dt_proj_b"][None, :]], 0),
        "wg0": get["L0_ffn_W_gate"].T, "wu0": get["L0_ffn_W_up"].T, "wd0": get["L0_ffn_W_down"].T,
        "wq": get["L1_attn_wq"].T, "wk": get["L1_attn_wk"].T, "wv": get["L1_attn_wv"].T, "wo": get["L1_attn_wo"].T,
        "w1_q": np.repeat(tiles("qweight", P // PACK), PACK, axis=1), "w1_s": tiles("scales", 1)[:, 0], "w1_z": tiles("zeros", 1)[:, 0],
        "ident": np.eye(P, dtype=np.float32),
        "fold": np.concatenate([np.eye(2 * NS, dtype=np.float32)] * 3 + [np.zeros((2 * NS, 2 * NS), np.float32)], 0),
        "mask": np.where(key > tok, np.float32(-1e30), np.float32(0)),
        "cos": cos.astype(np.float32), "sin": sin.astype(np.float32),
        "shifts": ((np.arange(P) % PACK) * 4).astype(np.int32)[:, None],
    }
    feeds, args = {}, []
    for name, a in arrays.items():
        a = np.ascontiguousarray(a)
        feeds[f"in_{name}_dram"] = a
        args.append(nc.dram_tensor(f"in_{name}_dram", a.shape, mybir.dt.from_np(a.dtype), kind="ExternalInput").ap())
    args.append(nc.dram_tensor("out_0_dram", (1, T, D), f32_dt(), kind="ExternalOutput").ap())
    build(nc, *args)
    r = run_bass_kernel_spmd(nc, [feeds], core_ids=[0])
    return r.results[0]["out_0_dram"]


def f32_dt():
    return mybir.dt.float32
```

```python
import concourse.bass as bass
from concourse import mybir
from contextlib import ExitStack

P = 128
T = 1024
TT = T // P
D = 512
DC = D // P
NS = 16
DTR = 16
F0 = 1792
M0 = F0 // P
F1 = 1376
M1 = (F1 + P - 1) // P
TAIL = F1 - (M1 - 1) * P
NH = 32
HD = D // NH
NP = NH // 2
GH = 4
NG = NH // GH
HALF = 512
EPS = 1e-5
WS = 256.0
PACK = 8
SERIES = 2.0 ** -7
LAG = 3


class Tally:

    def __init__(self, eng, sem):
        self.eng, self.sem, self.at = eng, sem, 0

    def done(self, ins):
        ins.then_inc(self.sem, 1)
        self.at = self.at + 1
        self.eng.wait_ge(self.sem, self.at)

    def loop(self, i, per):
        self.base = self.at
        self.at = self.base + i * per

    def end(self, passes, per):
        self.at = self.base + passes * per


def build(nc, x_fm, a_log, d_skip, xw, dtw, wg0, wu0, wd0, wq, wk, wv, wo,
          w1_q, w1_s, w1_z, ident, fold, mask, cos, sin, shifts, out):
    f32, f16, bf16, i32, u8 = mybir.dt.float32, mybir.dt.float16, mybir.dt.bfloat16, mybir.dt.int32, mybir.dt.uint8
    ALU = mybir.AluOpType
    ACT = mybir.ActivationFunctionType
    AX = mybir.AxisListType.X
    ds = bass.ds

    ctx = ExitStack()
    with ctx:
        arena = ctx.enter_context(nc.sbuf_tensor("arena", [P, 200 * 256], f32))

        def view(kb, cols, dt):
            size = 4 if dt in (f32, i32) else 2
            a = int(kb * 256)
            return arena[:, a:a + cols * size // 4].bitcast(dt) if dt != f32 else arena[:, a:a + cols]

        def small(name, shape, dt=f32):
            return ctx.enter_context(nc.sbuf_tensor(name, shape, dt))

        def sem(name):
            return ctx.enter_context(nc.semaphore(name))

        ps = ctx.enter_context(nc.psum_tensor("ps", [P, 8, HALF], f32))

        def banks(a, n):
            return ps[:, a:a + n, :].rearrange("p b n -> p (b n)")

        xT = view(0, DC * T, f32).rearrange("p (c t) -> p c t", c=DC)
        dt_ = view(16, DC * T, f32).rearrange("p (c t) -> p c t", c=DC)
        dtx = view(32, DC * T, f32).rearrange("p (c t) -> p c t", c=DC)
        c_all = view(48, NS * T, f32).rearrange("p (n t) -> p n t", n=NS)
        dA = view(112, 2 * T, f32).rearrange("p (b t) -> p b t", b=2)
        hst = view(120, 2 * T, f32).rearrange("p (b t) -> p b t", b=2)
        hC = [view(kb, T, f32) for kb in (128, 132, 186, 190)]
        sel = view(136, 2 * NS * P, bf16).rearrange("p (n m) -> p n m", n=2 * NS)
        bc = view(144, T, bf16)
        rest = view(146, T, f32)
        mid = view(150, T, bf16)
        dt_in = view(152, T, f32)
        e_, log_e, small_e = rest, view(194, T, f32), view(198, T, f16)
        wg0_sb = view(158, DC * F0, f16).rearrange("p (c m) -> p c m", c=DC)
        wu0_sb = view(172, DC * F0, f16).rearrange("p (c m) -> p c m", c=DC)
        wd0_sb = view(186, M0 * D, f16).rearrange("p (m d) -> p m d", m=M0)
        xtok = view(16, TT * D, f32).rearrange("p (i d) -> p i d", i=TT)
        xh = view(32, DC * T, f16).rearrange("p (c t) -> p c t", c=DC)
        xl = view(40, DC * T, f16).rearrange("p (c t) -> p c t", c=DC)
        hh = view(48, M0 * T, f16).rearrange("p (m t) -> p m t", m=M0)
        hl = view(76, M0 * T, f16).rearrange("p (m t) -> p m t", m=M0)
        sg = view(104, 2 * T, f32).rearrange("p (b t) -> p b t", b=2)
        h32 = view(112, 2 * T, f32).rearrange("p (b t) -> p b t", b=2)
        wraw = view(0, 2 * DC * D, f32).rearrange("p (b c d) -> p b c d", b=2, c=DC)
        wsp = view(120, 4 * 2 * DC * D, f16).rearrange("p (w s c d) -> p w s c d", w=4, s=2, c=DC)

        ident_sb = small("ident_sb", [P, P])
        fold_sb = small("fold_sb", [P, 2 * NS])
        alog_sb = small("alog_sb", [P, DC, NS])
        negA = small("negA", [P, DC, NS])
        dskip_sb = small("dskip_sb", [P, DC])
        series_sb = small("series_sb", [P, 1])
        xw_sb = small("xw_sb", [P, DC, 2 * NS + DTR])
        dtw_sb = small("dtw_sb", [2 * NS + DTR + 1, D])
        xn = view(152, 2 * D, f32).rearrange("p (b d) -> p b d", b=2)
        st6 = small("st6", [P, 6])
        mv = small("mv", [P, 2])
        vare = small("vare", [P, 1])
        sdev = small("sdev", [P, 1])
        rstd = small("rstd", [P, 1])
        tok_stack = view(0, 2 * NH * 64, f16).rearrange("p (w h d) -> p w h d", w=2, h=NH)
        rot_a = view(188, 2 * D, f32).rearrange("p (w h d) -> p w h d", w=2, h=NH)
        rot_b = view(192, 2 * D, f32).rearrange("p (w h d) -> p w h d", w=2, h=NH)
        q_st = view(48, NP * T, f16).rearrange("p (r t) -> p r t", r=NP)
        k_st = view(80, NP * T, f16).rearrange("p (r t) -> p r t", r=NP)
        v_tok = view(156, TT * D, f32).rearrange("p (i d) -> p i d", i=TT)
        v_ring = [view(kb, TT * GH * 32, f32).rearrange("p (i a d) -> p i a d", i=TT, a=GH) for kb in (172, 176)]
        k_pad = [view(kb, GH * T, f16).rearrange("p (a t) -> p a t", a=GH) for kb in (112, 120)]
        p_t = [view(kb, GH * T, f32).rearrange("p (a t) -> p a t", a=GH) for kb in (0, 128)]
        o_tok = view(32, TT * D, f32).rearrange("p (i d) -> p i d", i=TT)
        o_raw = view(188, T, f32)
        m_row = view(192, T, f16)
        m_a = view(194, TT * GH, f32).rearrange("p (i a) -> p i a", i=TT)
        m_b = view(194.5, 4 * GH, f32).rearrange("p (i a) -> p i a", i=4)
        m_neg = view(195, TT * GH, f16).rearrange("p (i a) -> p i a", i=TT)
        r_den = view(195.5, 4 * GH, f32).rearrange("p (i a) -> p i a", i=4)
        oh = view(112, DC * T, f16).rearrange("p (c t) -> p c t", c=DC)
        ol = view(120, DC * T, f16).rearrange("p (c t) -> p c t", c=DC)
        x3h = view(64, DC * T, f16).rearrange("p (c t) -> p c t", c=DC)
        x3l = view(72, DC * T, f16).rearrange("p (c t) -> p c t", c=DC)
        cos_sb = small("cos_sb", [P, TT, HD])
        sin_sb = small("sin_sb", [P, TT, HD])
        mask_sb = small("mask_sb", [P, P])
        mask_b = small("mask_b", [P, P], bf16)
        ident_b = small("ident_b", [P, P], bf16)
        ident_h = small("ident_h", [P, P], f16)
        ld_tab, tables_made = sem("ld_tab"), sem("tables_made")
        q_proj, k_proj, v_proj = sem("q_proj"), sem("k_proj"), sem("v_proj")
        roped, rope_summed, stack_high, stack_low, stacks_set = (
            sem("roped"), sem("rope_summed"), sem("stack_high"), sem("stack_low"), sem("stacks_set"))
        q_turned, k_turned, q_kept, k_kept, v_kept = (
            sem("q_turned"), sem("k_turned"), sem("q_kept"), sem("k_kept"), sem("v_kept"))
        pads_zeroed, v_ones = sem("pads_zeroed"), sem("v_ones")
        k_padded = [[sem(f"k_padded{slot}_{half}") for half in range(2)] for slot in range(2)]
        v_ringed, ring_full, ring_read = sem("v_ringed"), sem("ring_full"), sem("ring_read")
        m_joined, m_negated, m_rows, r_made = sem("m_joined"), sem("m_negated"), sem("m_rows"), sem("r_made")
        st_full, exp_done, pv_step, o_kept = sem("st_full"), sem("exp_done"), sem("pv_step"), sem("o_kept")
        o_turned, oh_done, ol_done = sem("o_turned"), sem("oh_done"), sem("ol_done")

        LEAD = 7

        def max_units(i):
            w = P * (i + 1)
            if w <= HALF:
                n = HALF // w if w != 3 * P else 1
                return [(m_a[:, i, a:a + n], [(a + b, 0, w, b * w) for b in range(n)]) for a in range(0, GH, n)]
            units = [(m_a[:, i, a:a + 1], [(a, 0, HALF, 0)]) for a in range(GH)]
            w -= HALF
            n = HALF // w if w != 3 * P else 1
            return units + [(m_b[:, i - 4, a:a + n], [(a + b, HALF, w, b * w) for b in range(n)]) for a in range(0, GH, n)]
        SEARCH = [(i, dst, slices) for i in range(TT) for dst, slices in max_units(i)]
        UNITS = len(SEARCH) + 1
        BODY = UNITS + 2
        OUT_AT = 7

        def side_steps(outs, begin, ahead):
            steps = []
            for k in range(begin, len(SEARCH)):
                if outs and k == begin + OUT_AT:
                    steps += [("out", 0), ("out", 1)]
                steps.append(("search", 0, k))
            steps.append(("negate",))
            steps += [("search", 1, k) for k in range(0, 1 if ahead else 0)]
            steps.append(("turn",))
            steps += [("search", 1, k) for k in range(1, LEAD if ahead else 0)]
            return steps

        def turned_at(steps):
            return steps.index(("turn",))

        def ring_base(g):
            if isinstance(g, int) and g == 0:
                return UNITS + LEAD
            return 2 * UNITS + LEAD - BODY + g * BODY - (LEAD if isinstance(g, int) and g == NG - 1 else 0)

        def exp_units(j):
            return [(a,) for a in range(GH)] if T - P * j > HALF else [(0, 1), (2, 3)]
        EXPS = sum(len(exp_units(j)) for j in range(TT))

        def value_pieces(j):
            return ([(6, P * j, HALF, 0)] if j < 4 else []) + [(7, max(P * j - HALF, 0), HALF, max(HALF - P * j, 0))]

        def group_order(side):
            col = 0.43e-3
            main = []
            for j in range(TT + 1):
                new, old = [], []
                if j < TT:
                    w = T - P * j
                    for heads in exp_units(j):
                        new.append((("keys", j, heads), len(heads) * (w * col + 0.06), 0.2 + len(heads) * w * 0.85e-3))
                if j:
                    old = [(("values", j - 1, k), 4 * (hi - lo) * col, 0) for k, (_, lo, hi, _) in enumerate(value_pieces(j - 1))]
                main += new[:2] + old + new[2:]
            side = list(side)
            order, pe_at, dve, act, exps_of, negated = [], 0.0, [0.0, 0.0], [0.0, 0.0], {}, 0.0
            while main or side:
                if side and side[0][0] == "negate":
                    side.pop(0)
                    dve[-1] += 0.4
                    negated = dve[-1] + 0.1
                    continue
                m = s = 1e9
                if main:
                    m = max(pe_at, act[-2] if main[0][0][0] == "keys" else exps_of[main[0][0][1]] + 0.1)
                if side:
                    s = max(pe_at, dve[-2], {"turn": negated, "out": 5.5}.get(side[0][0], 0.0))
                if s <= m:
                    step = side.pop(0)
                    cols = sum(x[2] for x in SEARCH[step[2]][2]) if step[0] == "search" else 0
                    pe_at = s + (cols * col if cols else 0.9 if step[0] == "out" else 0.5)
                    dve.append(max(dve[-1], pe_at + 0.1) + 0.07 + (cols or HALF) * 1.04e-3)
                else:
                    step, cost, after = main.pop(0)
                    pe_at = m + cost
                    if after:
                        act.append(max(act[-1], pe_at + 0.1) + after)
                        exps_of[step[1]] = act[-1]
                order.append(step)
            return order
        NB = 2 * DC + DC
        w_words = [view(kb, NB * P, i32) for kb in (156, 162)]
        w_scales = [view(kb, NB * P, f16) for kb in (168, 171)]
        w_zeros = [view(kb, NB * P // PACK, i32) for kb in (174, 175)]
        w_nib = view(176, NB * P, i32)
        w_full = view(182, NB * P, f32)
        z_nib = view(196, NB * P // 2, f16).bitcast(u8)
        o_half = view(198, D, f16)
        gu = [view(kb, 2 * 2 * DC * P, f16).rearrange("p (s b n) -> p s b n", s=2, b=2 * DC) for kb in (60, 146)]
        wd1 = view(124, 2 * M1 * D, f16).rearrange("p (s m d) -> p s m d", s=2, m=M1)
        h1h = view(80, M1 * T, f16).rearrange("p (m t) -> p m t", m=M1)
        h1l = view(102, M1 * T, f16).rearrange("p (m t) -> p m t", m=M1)
        sg1 = view(0, 2 * T, f32).rearrange("p (b t) -> p b t", b=2)
        h132 = view(8, 2 * T, f32).rearrange("p (b t) -> p b t", b=2)
        shift_sb = small("shift_sb", [P, 1], i32)
        ld_shift = sem("ld_shift")
        ld_w1 = [sem("ld_w1_0"), sem("ld_w1_1")]
        w1_nib, w1_full, w1_scaled, w1_high, w1_low = (
            sem("w1_nib"), sem("w1_full"), sem("w1_scaled"), sem("w1_high"), sem("w1_low"))
        gate1_done, up1_done, silu1_done, h1_done, h1h_done, h1l_done = (
            sem("gate1_done"), sem("up1_done"), sem("silu1_done"), sem("h1_done"), sem("h1h_done"), sem("h1l_done"))
        out_stored = [sem("out_stored0"), sem("out_stored1")]

        ld_small, ld_w0 = sem("ld_small"), sem("ld_w0")
        ld_x = [sem(f"ld_x{c}") for c in range(DC)]
        ld_wraw = [sem(f"ld_wraw{w}") for w in range(4)]
        sel_built, consts_made = sem("sel_built"), sem("consts_made")
        xp_done, bc_split, dtin_done, negA_done = sem("xp_done"), sem("bc_split"), sem("dtin_done"), sem("negA_done")
        dtl_done, z_abs, softlog, dt_done = sem("dtl_done"), sem("z_abs"), sem("softlog"), sem("dt_done")
        b_bcast, c_bcast, c_kept = sem("b_bcast"), sem("c_bcast"), sem("c_kept")
        dA_done, dbx_done, scan_done, hc_done = sem("dA_done"), sem("dbx_done"), sem("scan_done"), sem("hc_done")
        y_added, y_taken = sem("y_added"), sem("y_taken")
        x_kept = sem("x_kept")
        ln_in, var_done, sdev_done, x_normed = sem("ln_in"), sem("var_done"), sem("sdev_done"), sem("x_normed")
        x_turned, xh_done, xl_done = sem("x_turned"), sem("xh_done"), sem("xl_done")
        gate_done, up_done, silu_done, h_done, hh_done, hl_done = (
            sem("gate_done"), sem("up_done"), sem("silu_done"), sem("h_done"), sem("hh_done"), sem("hl_done"))
        w_high, w_low = sem("w_high"), sem("w_low")
        dve_own, act_own, stored = sem("dve_own"), sem("act_own"), sem("stored")

        block = ctx.enter_context(nc.Block())

        @block.sync
        def _(sp):
            for dst, src in ((ident_sb[:], ident), (fold_sb[:], fold),
                             (xw_sb[:], xw.rearrange("(c p) r -> p c r", p=P)),
                             (dtw_sb[2 * NS:, :], dtw),
                             (dskip_sb[:], d_skip),
                             (alog_sb[:], a_log.rearrange("(c p) n -> p c n", p=P))):
                sp.dma_start(dst, src).then_inc(ld_small, 16)
            for c in range(DC):
                sp.dma_start(xT[:, c, :], x_fm[c * P:(c + 1) * P, :]).then_inc(ld_x[c], 16)
            sp.dma_start(wg0_sb[:], wg0.rearrange("(c p) m -> p c m", p=P)).then_inc(ld_w0, 16)
            sp.dma_start(wu0_sb[:], wu0.rearrange("(c p) m -> p c m", p=P)).then_inc(ld_w0, 16)
            sp.wait_ge(y_added, DC * NS)
            sp.dma_start(wd0_sb[:], wd0.rearrange("(m p) d -> p m d", p=P)).then_inc(ld_w0, 16)
            sp.wait_ge(ln_in, TT)
            for w, src in enumerate((wq, wk, wv, wo)):
                if w >= 2:
                    sp.wait_ge(w_low, w - 1)
                sp.dma_start(wraw[:, w % 2], src.rearrange("(c p) d -> p c d", p=P)).then_inc(ld_wraw[w], 16)
            for dst, src in ((cos_sb[:], cos.rearrange("(i p) d -> p i d", p=P)),
                             (sin_sb[:], sin.rearrange("(i p) d -> p i d", p=P)), (mask_sb[:], mask)):
                sp.dma_start(dst, src).then_inc(ld_tab, 16)

            def pad_keys(g, slot, half):
                at = slice(half * HALF, (half + 1) * HALF)
                for b in range(2):
                    sp.dma_start(k_pad[slot][64 * b:64 * b + 64, b::2, at],
                                 k_st[64 * b:64 * b + 64, ds(2 * g, 2), at]).then_inc(k_padded[slot][half], 16)

            def put_rows(g, use):
                sp.wait_ge(ring_read, use)
                for b in range(2):
                    for r in range(2):
                        sp.dma_start(q_st[64 * b + 48:64 * b + 49, ds(2 * g + r, 1), :],
                                     m_row[2 * r + b:2 * r + b + 1, :].unsqueeze(1)).then_inc(m_rows, 16)
            sp.wait_ge(k_kept, TT)
            sp.wait_ge(q_kept, TT)
            for slot in range(2):
                sp.wait_ge(pads_zeroed, slot + 1)
                for half in range(2):
                    pad_keys(slot, slot, half)
            put_rows(0, turned_at(side_steps(False, 0, True)))

            def sync_body(g, slot, first=False, ahead=True):
                if ahead:
                    sp.wait_ge(st_full, EXPS * g + TT // 2 * GH)
                    pad_keys(g + 2, slot, 0)
                put_rows(g + 1, ring_base(g) + turned_at(side_steps(not first, LEAD, ahead)))
                if ahead:
                    sp.wait_ge(st_full, EXPS * (g + 1))
                    pad_keys(g + 2, slot, 1)
            sync_body(0, 0, first=True)
            with sp.Fori(0, 2) as k:
                for b in range(2):
                    sync_body(2 * k + 1 + b, 1 - b)
            sync_body(5, 1)
            sync_body(6, 0, ahead=False)
            sp.dma_start(shift_sb[:], shifts).then_inc(ld_shift, 16)

            def load_tile(m, slot):
                sp.dma_start(w_words[slot][:], w1_q[ds(m, 1)].rearrange("m r n -> (m r) n")).then_inc(ld_w1[slot], 16)
                sp.dma_start(w_scales[slot][:], w1_s[ds(m, 1), :].broadcast_to([P, NB * P])).then_inc(ld_w1[slot], 16)
                sp.dma_start(w_zeros[slot][:], w1_z[ds(m, 1), :].broadcast_to([P, NB * P // PACK])).then_inc(ld_w1[slot], 16)
            sp.wait_ge(pv_step, NG * TT)
            load_tile(0, 0)
            load_tile(1, 1)
            with sp.Fori(1, M1 // 2) as k:
                for u in range(2):
                    sp.wait_ge(w1_nib, 2 * k + u - 1)
                    sp.wait_ge(w1_scaled, 2 * k + u - 1)
                    load_tile(2 * k + u, u)
            sp.wait_ge(w1_nib, M1 - 2)
            sp.wait_ge(w1_scaled, M1 - 2)
            load_tile(M1 - 1, 0)
            for t in range(TT):
                sp.wait_ge(x_normed, 3 * TT + t + 1)
                sp.dma_start(out[0, t * P:(t + 1) * P, :], xn[:, t % 2, :]).then_inc(out_stored[t % 2], 16)
            for u in range(2):
                sp.wait_ge(out_stored[u], 16 * TT // 2)

        @block.tensor
        def _(pe):
            pe.wait_ge(ld_small, 6 * 16)
            for c in range(DC):
                pe.wait_ge(ld_x[c], 16)
                for h in range(2):
                    last = nc.tensor.matmul(banks(6 + h, 1)[0:2 * NS + DTR, :], xw_sb[:, c, :],
                                            xT[:, c, h * HALF:(h + 1) * HALF], start=(c == 0), stop=(c == DC - 1))
            last.then_inc(xp_done, 1)

            def dt_linear(c):
                for h in range(2):
                    last = nc.tensor.matmul(banks(4 + h, 1), dtw_sb[2 * NS:, c * P:(c + 1) * P],
                                            dt_in[2 * NS:2 * NS + DTR + 1, h * HALF:(h + 1) * HALF], start=True, stop=True)
                last.then_inc(dtl_done, 1)

            def bcast(row, bank, signal):
                for h in range(2):
                    last = nc.tensor.matmul(banks(bank + h, 1), sel[:, row, :], bc[:, h * HALF:(h + 1) * HALF],
                                            start=True, stop=True)
                last.then_inc(signal, 1)

            def add_y(slot, start, stop):
                for h in range(2):
                    last = nc.tensor.matmul(banks(6 + h, 1), ident_sb[:], hC[slot][:, h * HALF:(h + 1) * HALF],
                                            start=start, stop=stop)
                last.then_inc(y_added, 1)

            pe.wait_ge(dtin_done, 1)
            dt_linear(0)
            pe.wait_ge(bc_split, 1)
            pe.wait_ge(sel_built, 1)
            for c in range(DC):
                if c + 1 < DC:
                    pe.wait_ge(z_abs, c + 1)
                    pe.wait_ge(dt_done, c + 1)
                    if c == 1:
                        pe.wait_ge(c_kept, NS)
                    dt_linear(c + 1)
                def step(n, u, lagged, start=False, stop=False, first=False):
                    i = n + NS * c
                    if not first:
                        pe.wait_ge(scan_done, i - 1)
                    bcast(n, 2 * (u % 2), b_bcast)
                    if c == 0:
                        if first and u == 0:
                            pe.wait_ge(z_abs, 2)
                            pe.wait_ge(dt_done, 2)
                        else:
                            pe.wait_ge(c_kept, n)
                        bcast(n + NS, 4, c_bcast)
                    if lagged:
                        pe.wait_ge(hc_done, i - LAG + 1)
                        if start and c:
                            pe.wait_ge(y_taken, c)
                        add_y((u - LAG) % 4, start, stop)
                for n in range(4):
                    step(n, n, c > 0 or n == LAG, start=(n == LAG), stop=(n == LAG - 1), first=(c == 0 and n < 2))
                with pe.Fori(1, NS // 4) as k:
                    for u in range(4):
                        step(4 * k + u, u, True)
            for n in range(NS - LAG, NS):
                pe.wait_ge(hc_done, (DC - 1) * NS + n + 1)
                add_y(n % 4, False, n == NS - 1)

            def norm_stage(ln, make, turn=True, straight=False):
                def produce(t, u, first):
                    if not first:
                        pe.wait_ge(x_normed, TT * ln + t - 1)
                    make(t, u).then_inc(ln_in, 1)

                def turn_tile(t, u, first):
                    pe.wait_ge(x_normed, TT * ln + t + 1)
                    if not first:
                        pe.wait_ge(xl_done, TT * ln + t - 1)
                    for c in range(DC):
                        last = nc.tensor.transpose(ps[:, 2 + u, c * P:(c + 1) * P], xn[:, u, c * P:(c + 1) * P], ident_sb[:])
                    last.then_inc(x_turned, 1)

                produce(0, 0, True)
                produce(1, 1, True)
                if turn:
                    turn_tile(0, 0, True)
                    produce(2, 0, False)
                    turn_tile(1, 1, True)
                    produce(3, 1, False)
                    turn_tile(2, 0, False)
                    if straight:
                        for t in range(4, TT):
                            produce(t, t % 2, False)
                            turn_tile(t - 1, 1 - t % 2, False)
                    else:
                        with pe.Fori(2, TT // 2) as k:
                            for u in range(2):
                                produce(2 * k + u, u, False)
                                turn_tile(2 * k + u - 1, 1 - u, False)
                    turn_tile(TT - 1, 1, False)
                else:
                    with pe.Fori(1, TT // 2) as k:
                        for u in range(2):
                            produce(2 * k + u, u, False)

            def turn_residual(t, u):
                for c in range(DC):
                    last = nc.tensor.transpose(ps[:, u, c * P:(c + 1) * P], xT[:, c, t * P:(t + 1) * P], ident_sb[:])
                return last

            pe.wait_ge(y_taken, DC)
            norm_stage(0, turn_residual, straight=True)

            pe.wait_ge(ld_w0, 3 * 16)
            pe.wait_ge(xl_done, TT)

            def ffn0(m, u, first):
                for w, bank, free, signal in ((wg0_sb, 4 * u, silu_done, gate_done), (wu0_sb, 4 * u + 2, h_done, up_done)):
                    if not first:
                        pe.wait_ge(free, m - 1)
                    for c in range(DC):
                        for part in (xh, xl):
                            for h in range(2):
                                last = nc.tensor.matmul(banks(bank + h, 1), w[:, c, ds(m * P, P)],
                                                        part[:, c, h * HALF:(h + 1) * HALF],
                                                        start=(c == 0 and part is xh), stop=(c == DC - 1 and part is xl))
                    last.then_inc(signal, 1)
            ffn0(0, 0, True)
            ffn0(1, 1, True)
            with pe.Fori(1, M0 // 2) as k:
                for u in range(2):
                    ffn0(2 * k + u, u, False)

            def down0(t, u):
                for m in range(M0):
                    for part in (hh, hl):
                        last = nc.tensor.matmul(banks(u, 1), part[:, m, ds(t * P, P)], wd0_sb[:, m, :],
                                                start=(m == 0 and part is hh), stop=(m == M0 - 1 and part is hl))
                return last
            pe.wait_ge(h_done, M0)
            pe.wait_ge(hl_done, M0)
            norm_stage(1, down0)
            pe.wait_ge(xl_done, 2 * TT)
            pe.wait_ge(w_low, 4)
            pe.wait_ge(tables_made, 3)

            def project(w, src_h, src_l, t, bank, signal):
                for c in range(DC):
                    for part, s in ((src_h, 0), (src_l, 0), (src_h, 1)):
                        last = nc.tensor.matmul(banks(bank, 1), part[:, c, ds(t * P, P)], wsp[:, w, s, c, :],
                                                start=(c == 0 and part is src_h and s == 0), stop=(c == DC - 1 and s == 1))
                return last.then_inc(signal, 1) if signal is not None else last

            turned = banks(6, 2).bitcast(f16)

            def turn_stack(w, t):
                pe.wait_ge(stack_low, 2 * t + w + 1)
                for r in range(NP):
                    last = nc.tensor.transpose(turned[:, r * P:(r + 1) * P],
                                               tok_stack[:, w, 2 * r:2 * r + 2, :].rearrange("p h d -> p (h d)"), ident_h[:])
                last.then_inc((q_turned, k_turned)[w], 1)

            def qkv(t, u, first, lagged):
                if not first:
                    pe.wait_ge(roped, 2 * t - 3)
                project(0, xh, xl, t, 3 * u, q_proj)
                if lagged:
                    if not first:
                        pe.wait_ge(k_kept, t - 1)
                    turn_stack(0, t - 1)
                if not first:
                    pe.wait_ge(roped, 2 * t - 2)
                project(1, xh, xl, t, 3 * u + 1, k_proj)
                if lagged:
                    pe.wait_ge(q_kept, t)
                    turn_stack(1, t - 1)
                if not first:
                    pe.wait_ge(v_kept, t - 1)
                project(2, xh, xl, t, 3 * u + 2, v_proj)
            qkv(0, 0, True, False)
            qkv(1, 1, True, True)
            with pe.Fori(1, TT // 2) as k:
                for u in range(2):
                    qkv(2 * k + u, u, False, True)
            pe.wait_ge(k_kept, TT - 1)
            turn_stack(0, TT - 1)
            pe.wait_ge(q_kept, TT)
            turn_stack(1, TT - 1)

            def ring_slot(use, n):
                need = use + n - (n > 0)
                if not isinstance(need, int) or need > 0:
                    pe.wait_ge(ring_read, need)
                return n % 2

            def search(g, slot, k, use, n):
                i, _, slices = SEARCH[k]
                bank = ring_slot(use, n)
                for a, key, w, col in slices:
                    dst = ps[:, bank, col:col + w]
                    diag = key + w == P * (i + 1)
                    last = nc.tensor.matmul(dst, q_st[:, ds(2 * g + a // 2, 1), i * P:(i + 1) * P].rearrange("p a t -> p (a t)"),
                                            k_pad[slot][:, a, key:key + w], start=True, stop=not diag)
                    if diag:
                        last = nc.tensor.matmul(dst[:, w - P:w], ident_b[:], mask_b[:], start=False, stop=True)
                last.then_inc(ring_full, 1)

            def turn_maxima(g, use, n):
                pe.wait_ge(m_negated, g + 1)
                bank = ring_slot(use, n)
                dst = ps[:, bank, :].bitcast(f16)
                for i in range(TT):
                    last = nc.tensor.transpose(dst[0:GH, i * P:(i + 1) * P], m_neg[:, i, :], ident_h[:])
                last.then_inc(ring_full, 1)

            def keys(g, slot, j, heads, e):
                w = T - P * j
                bank = 2 + 2 * (e % 2)
                if not (isinstance(g, int) and g == 0 and e < 2):
                    pe.wait_ge(exp_done, EXPS * g + e - 1)
                for b, a in enumerate(heads):
                    row = ds(2 * g + a // 2, 1)
                    for h in range(2 if w > HALF else 1):
                        lo, hi = h * HALF, min(w, (h + 1) * HALF)
                        dst = ps[:, bank + b + h, 0:hi - lo]
                        last = nc.tensor.matmul(dst, k_pad[slot][:, a, j * P:(j + 1) * P],
                                                q_st[:, row, j * P + lo:j * P + hi].rearrange("p a t -> p (a t)"),
                                                start=True, stop=(h == 1))
                        if h == 0:
                            last = nc.tensor.matmul(dst[:, 0:P], mask_b[:], ident_b[:], start=False, stop=True)
                last.then_inc(st_full, 1)

            def values(slot, j, k):
                pieces = value_pieces(j)
                bank, lo, hi, col = pieces[k]
                for a in range(GH):
                    last = nc.tensor.matmul(ps[32 * a:32 * a + 32, bank, lo:hi], v_ring[slot][:, j, a, :],
                                            p_t[j % 2][:, a, col:col + hi - lo], start=(j == 0), stop=(j == (TT // 2 - 1 if bank == 6 else TT - 1)))
                if k == len(pieces) - 1:
                    last.then_inc(pv_step, 1)

            def turn_out(use, n, half):
                bank = ring_slot(use, n)
                for b in range(4):
                    i = 4 * half + b
                    last = nc.tensor.transpose(ps[:, bank, b * P:(b + 1) * P], o_raw[:, i * P:(i + 1) * P], ident_sb[:])
                last.then_inc(ring_full, 1)

            def beside(g, slot, use, n, kind, at):
                if kind == "search":
                    search(g + 1 + at[0], (slot, 1 - slot)[at[0] == 0], at[1], use, n)
                elif kind == "out":
                    turn_out(use, n, at[0])
                else:
                    turn_maxima(g + 1, use, n)

            def body(g, slot, pads=(0, 0), first=False, final=False):
                use, n, e = ring_base(g), 0, 0
                made = [0] * TT
                side = [("out", 0), ("out", 1)] if final else side_steps(not first, LEAD, pads[1] is not None)
                pe.wait_ge(m_rows, 64 * (g + 1))
                for kind, *at in group_order(side):
                    if kind == "keys":
                        keys(g, slot, at[0], at[1], e)
                        e += 1
                        made[at[0]] = e
                    elif kind == "values":
                        if at == [0, 0]:
                            pe.wait_ge(v_ringed, g + 1)
                            if not first:
                                pe.wait_ge(o_kept, g)
                        if at[1] == 0:
                            pe.wait_ge(exp_done, EXPS * g + made[at[0]])
                        values(slot, *at)
                    else:
                        if at == [0, FIRST_HIGH]:
                            pe.wait_ge(k_padded[1 - slot][1], 32 * pads[0])
                        if at == [1, 0]:
                            pe.wait_ge(k_padded[slot][0], 32 * pads[1])
                        if (kind, at) == ("out", [0]):
                            pe.wait_ge(o_kept, g)
                        beside(g, slot, use, n, kind, at)
                        n += 1
            pe.wait_ge(roped, 2 * TT)
            pe.wait_ge(v_kept, TT)
            pe.wait_ge(k_kept, TT)
            FIRST_HIGH = next(k for k, (i, _, slices) in enumerate(SEARCH) if slices[0][1] + slices[0][2] > HALF)
            for half in range(2):
                pe.wait_ge(k_padded[0][half], 32)
            n = 0
            for kind, *at in side_steps(False, 0, True):
                if at == [1, 0]:
                    pe.wait_ge(k_padded[1][0], 32)
                if kind != "negate":
                    beside(-1, 1, 0, n, kind, at)
                    n += 1
            body(0, 0, (1, 2), first=True)
            with pe.Fori(0, 2) as k:
                for b in range(2):
                    body(2 * k + 1 + b, 1 - b, (k + 2, k + 2 + b))
            body(5, 1, (4, 4))
            body(6, 0, (4, None))
            body(7, 1, final=True)
            pe.wait_ge(o_kept, NG)
            for half in range(2):
                turn_out(ring_base(NG - 1) + 2, half, half)

            for t in range(TT):
                if t < 2:
                    pe.wait_ge(ring_read, ring_base(NG - 1) + 4)
                else:
                    pe.wait_ge(ol_done, t - 1)
                for c in range(DC):
                    last = nc.tensor.transpose(ps[:, 2 + t % 2, c * P:(c + 1) * P], o_tok[:, t, c * P:(c + 1) * P], ident_sb[:])
                last.then_inc(o_turned, 1)
            pe.wait_ge(ol_done, TT)
            norm_stage(2, lambda t, u: project(3, oh, ol, t, u, None))
            pe.wait_ge(xl_done, 3 * TT)

            def ffn1(m, u, first):
                pe.wait_ge(w1_low, m + 1)
                for w, bank, free, signal in ((0, 4 * u, silu1_done, gate1_done), (1, 4 * u + 2, h1_done, up1_done)):
                    if not first:
                        pe.wait_ge(free, m - 1)
                    for c in range(DC):
                        for s, part in ((0, x3h), (0, x3l), (1, x3h)):
                            for h in range(2):
                                last = nc.tensor.matmul(banks(bank + h, 1), gu[u][:, s, w * DC + c, :],
                                                        part[:, c, h * HALF:(h + 1) * HALF],
                                                        start=(c == 0 and s == 0 and part is x3h), stop=(c == DC - 1 and s == 1))
                    last.then_inc(signal, 1)
            ffn1(0, 0, True)
            ffn1(1, 1, True)
            with pe.Fori(1, M1 // 2) as k:
                for u in range(2):
                    ffn1(2 * k + u, u, False)
            ffn1(M1 - 1, 0, False)

            def down1(t, u):
                for m in range(M1):
                    for part, s in ((h1h, 0), (h1l, 0), (h1h, 1)):
                        last = nc.tensor.matmul(banks(u, 1), part[:, m, ds(t * P, P)], wd1[:, s, m, :],
                                                start=(m == 0 and part is h1h and s == 0), stop=(m == M1 - 1 and s == 1))
                return last
            pe.wait_ge(h1_done, M1)
            pe.wait_ge(h1l_done, M1)
            norm_stage(3, down1, turn=False)

        @block.scalar
        def _(act):
            own = Tally(act, act_own)
            nc.scalar.preload_act_table_set("natural_log_exp_and_others")
            act.wait_ge(ld_small, 6 * 16)
            own.done(nc.scalar.activation(negA[:], alog_sb[:], ACT.Exp))
            nc.scalar.mul(negA[:], negA[:], -1.0).then_inc(negA_done, 1)
            act.wait_ge(negA_done, 1)
            act.wait_ge(xp_done, 1)
            act.wait_ge(consts_made, 3)
            nc.scalar.copy(dt_in[2 * NS:2 * NS + DTR, :], banks(6, 2)[2 * NS:2 * NS + DTR, :]).then_inc(dtin_done, 1)

            def soft_log(c):
                act.wait_ge(dtl_done, c + 1)
                if c:
                    act.wait_ge(dt_done, c)
                nc.scalar.activation(e_[:], banks(4, 2), ACT.Abs).then_inc(z_abs, 1)
                act.wait_ge(z_abs, c + 1)
                own.done(nc.scalar.activation(e_[:], e_[:], ACT.Exp, scale=-1.0))
                nc.scalar.activation(dt_[:, c, :], e_[:], ACT.Square, scale=3.0 ** -0.5).then_inc(softlog, 1)
                nc.scalar.activation(small_e[:], e_[:], ACT.Relu, bias=series_sb[:], scale=-1.0).then_inc(softlog, 1)
                nc.scalar.activation(log_e[:], e_[:], ACT.Ln, bias=1.0).then_inc(softlog, 1)

            act.wait_ge(bc_split, 1)
            soft_log(0)
            for c in range(DC):
                if c + 1 < DC:
                    soft_log(c + 1)
                act.wait_ge(dt_done, c + 1)

                def step(n, u, first):
                    i = n + NS * c
                    if not (c == 0 and first):
                        act.wait_ge(scan_done, i - 1)
                    nc.scalar.activation(dA[:, u, :], dt_[:, c, :], ACT.Exp, scale=negA[:, c, ds(n, 1)]).then_inc(dA_done, 1)
                    if c == 0:
                        act.wait_ge(c_bcast, n + 1)
                        nc.scalar.copy(c_all[:, n, :], banks(4, 2)).then_inc(c_kept, 1)
                step(0, 0, True)
                step(1, 1, True)
                with act.Fori(1, NS // 2) as k:
                    for u in range(2):
                        step(2 * k + u, u, False)

            def norm_stage(ln, turn=True):
                def high(t, u):
                    act.wait_ge(x_turned, TT * ln + t + 1)
                    nc.scalar.copy(XH[ln][:, :, ds(t * P, P)], ps[:, 2 + u, :].rearrange("p (c t) -> p c t", c=DC)).then_inc(xh_done, 1)

                def root(t):
                    act.wait_ge(var_done, TT * ln + t + 1)
                    nc.scalar.activation(sdev[:], vare[:], ACT.Sqrt).then_inc(sdev_done, 1)
                root(0)
                if turn:
                    high(0, 0)
                root(1)
                with act.Fori(1, TT // 2) as k:
                    for u in range(2):
                        if turn:
                            high(2 * k + u - 1, 1 - u)
                        root(2 * k + u)
                if turn:
                    high(TT - 1, 1)
            XH = {0: xh, 1: xh}
            norm_stage(0)

            for w in range(4):
                act.wait_ge(ld_wraw[w], 16)
                nc.scalar.mul(wsp[:, w, 0], wraw[:, w % 2], WS).then_inc(w_high, 1)

            def ffn0(m, u, first):
                act.wait_ge(gate_done, m + 1)
                if not first:
                    act.wait_ge(h_done, m - 1)
                nc.scalar.activation(sg[:, u, :], banks(4 * u, 2), ACT.Silu).then_inc(silu_done, 1)
                act.wait_ge(h_done, m + 1)
                nc.scalar.copy(hh[:, m, :], h32[:, u, :]).then_inc(hh_done, 1)
            ffn0(0, 0, True)
            ffn0(1, 1, True)
            with act.Fori(1, M0 // 2) as k:
                for u in range(2):
                    ffn0(2 * k + u, u, False)
            norm_stage(1)
            act.wait_ge(ld_tab, 3 * 16)
            nc.scalar.copy(mask_b[:], mask_sb[:]).then_inc(tables_made, 1)
            nc.scalar.copy(ident_b[:], ident_sb[:]).then_inc(tables_made, 1)
            nc.scalar.copy(ident_h[:], ident_sb[:]).then_inc(tables_made, 1)
            nc.scalar.preload_act_table_set("natural_log_exp_and_others")

            def keep_queries(t):
                act.wait_ge(q_turned, t + 1)
                nc.scalar.copy(q_st[:, :, ds(t * P, P)], banks(6, 2).bitcast(f16).rearrange("p (r t) -> p r t", r=NP)).then_inc(q_kept, 1)

            def stack(t, u, first):
                for w in range(2):
                    act.wait_ge(rope_summed, 2 * t + w + 1)
                    if not first:
                        act.wait_ge((q_turned, k_turned)[w], t)
                    dst = tok_stack[:, w, :, 0:64 if w == 0 else 32].rearrange("p h (b d) -> p h b d", b=4 if w == 0 else 2)
                    nc.scalar.copy(dst[:, :, 0:3:2, :] if w == 0 else dst,
                                   rot_a[:, w].unsqueeze(2).broadcast_to([P, NH, 2, HD])).then_inc(stack_high, 1)
                act.wait_ge(v_proj, t + 1)
                nc.scalar.mul(v_tok[:, t, :], banks(3 * u + 2, 1), 1.0 / WS).then_inc(v_kept, 1)
            act.wait_ge(stacks_set, 2)
            stack(0, 0, True)
            keep_queries(0)
            stack(1, 1, False)
            with act.Fori(1, TT // 2) as k:
                for u in range(2):
                    keep_queries(2 * k + u - 1)
                    stack(2 * k + u, u, False)
            keep_queries(TT - 1)

            def keep_out(g, use):
                act.wait_ge(pv_step, TT * (g + 1))
                act.wait_ge(ring_read, use)
                nc.scalar.copy(o_raw[:], banks(6, 2)).then_inc(o_kept, 1)

            def body(g, first=False):
                e = 0
                for j in range(TT):
                    w = T - P * j
                    if not (first and j < 2):
                        act.wait_ge(pv_step, TT * g + j - 1)
                    for heads in exp_units(j):
                        act.wait_ge(st_full, EXPS * g + e + 1)
                        bank, a = 2 + 2 * (e % 2), heads[0]
                        if len(heads) == 1:
                            dst, src = p_t[j % 2][:, a, 0:w], banks(bank, 2)[:, 0:w]
                        else:
                            dst, src = p_t[j % 2][:, a:a + 2, 0:w], ps[:, bank:bank + 2, 0:w]
                        nc.scalar.activation(dst, src, ACT.Exp, scale=float(HD) ** -0.5).then_inc(exp_done, 1)
                        e += 1
                    if j == 0 and not first:
                        keep_out(g - 1, ring_base(g))
            body(0, True)
            with act.Fori(1, NG - 1) as g:
                body(g)
            body(NG - 1)
            keep_out(NG - 1, ring_base(NG - 1) + 2)

            def high_out(t):
                act.wait_ge(o_turned, t + 1)
                nc.scalar.copy(oh[:, :, t * P:(t + 1) * P], ps[:, 2 + t % 2, :].rearrange("p (c t) -> p c t", c=DC)).then_inc(oh_done, 1)
            for t in range(TT):
                high_out(t)
            XH[2] = x3h
            norm_stage(2)
            def weights_high(m, u, first=False):
                act.wait_ge(w1_scaled, m + 1)
                if not first:
                    act.wait_ge(up1_done, m - 1)
                nc.scalar.mul(gu[u][:, 0], w_full[:, 0:2 * DC * P].rearrange("p (b n) -> p b n", n=P), WS).then_inc(w1_high, 1)
                nc.scalar.mul(wd1[:, 0, m, :], w_full[:, 2 * DC * P:], WS).then_inc(w1_high, 1)

            def ffn1(m, u, first):
                act.wait_ge(gate1_done, m + 1)
                if not first:
                    act.wait_ge(h1_done, m - 1)
                nc.scalar.activation(sg1[:, u, :], banks(4 * u, 2), ACT.Silu, scale=1.0 / WS).then_inc(silu1_done, 1)
                act.wait_ge(h1_done, m + 1)
                nc.scalar.copy(h1h[:, m, :], h132[:, u, :]).then_inc(h1h_done, 1)
            weights_high(0, 0, True)
            weights_high(1, 1, True)
            ffn1(0, 0, True)
            weights_high(2, 0)
            ffn1(1, 1, True)
            with act.Fori(1, M1 // 2) as k:
                for u in range(2):
                    weights_high(2 * k + u + 1, 1 - u)
                    ffn1(2 * k + u, u, False)
            ffn1(M1 - 1, 0, False)
            norm_stage(3, turn=False)

        @block.gpsimd
        def _(pool):
            for c in range(DC):
                def step(n, u, first):
                    i = n + NS * c
                    pool.wait_ge(scan_done, i + 1)
                    if c == 0:
                        pool.wait_ge(c_kept, n + 1)
                    if not first:
                        pool.wait_ge(y_added, i - 3)
                    nc.gpsimd.tensor_tensor(hC[u][:], hst[:, u % 2, :], c_all[:, n, :], ALU.mult).then_inc(hc_done, 1)
                for n in range(4):
                    step(n, n, c == 0)
                with pool.Fori(1, NS // 4) as k:
                    for u in range(4):
                        step(4 * k + u, u, False)

            def keep(ln):
                with pool.Fori(0, TT // 2) as k:
                    for u in range(2):
                        pool.wait_ge(x_normed, TT * ln + 2 * k + u + 1)
                        nc.gpsimd.tensor_copy(xtok[:, 2 * k + u, :], xn[:, u, :]).then_inc(x_kept, 1)
            keep(0)
            keep(1)
            pool.wait_ge(w_low, 4)
            nc.gpsimd.memset(tok_stack[:], 0.0).then_inc(stacks_set, 1)
            pool.wait_ge(stacks_set, 1)
            nc.gpsimd.memset(tok_stack[:, 1, :, 48:49], 1.0).then_inc(stacks_set, 1)
            for slot in range(2):
                nc.gpsimd.memset(v_ring[slot][:], 1.0).then_inc(v_ones, 1)
            nc.gpsimd.memset(k_pad[0][:], 0.0).then_inc(pads_zeroed, 1)

            def stack(t):
                for w in range(2):
                    pool.wait_ge(roped, 2 * t + w + 1)
                    nc.gpsimd.tensor_tensor(rot_a[:, w], rot_a[:, w], rot_b[:, w], ALU.add).then_inc(rope_summed, 1)
                for w in range(2):
                    pool.wait_ge(stack_high, 2 * t + w + 1)
                    at = 16 if w == 0 else 32
                    nc.gpsimd.tensor_tensor(tok_stack[:, w, :, at:at + HD], rot_a[:, w], tok_stack[:, w, :, 0:HD],
                                            ALU.subtract).then_inc(stack_low, 1)
            with pool.Fori(0, TT) as t:
                stack(t)
            pool.wait_ge(v_proj, TT)
            nc.gpsimd.memset(k_pad[1][:], 0.0).then_inc(pads_zeroed, 1)
            pool.wait_ge(v_kept, TT)
            pool.wait_ge(v_ones, 2)

            def ring_values(g, slot, first=False):
                if not first:
                    pool.wait_ge(pv_step, TT * (g - 1))
                nc.gpsimd.tensor_copy(v_ring[slot][:, :, :, 0:HD],
                                      v_tok[:, :, ds(g * GH * HD, GH * HD)].rearrange("p i (a d) -> p i a d", a=GH)).then_inc(v_ringed, 1)
            ring_values(0, 0, True)
            ring_values(1, 1, True)
            with pool.Fori(1, NG // 2) as k:
                for u in range(2):
                    ring_values(2 * k + u, u)
            pool.wait_ge(w1_full, 1)
            nc.gpsimd.tensor_tensor(w_full[:], w_full[:], w_scales[0][:], ALU.mult).then_inc(w1_scaled, 1)
            keep(2)
            with pool.Fori(0, M1 // 2) as k:
                for u in range(2):
                    m = 2 * k + u + 1
                    pool.wait_ge(w1_full, m + 1)
                    nc.gpsimd.tensor_tensor(w_full[:], w_full[:], w_scales[1 - u][:], ALU.mult).then_inc(w1_scaled, 1)

        @block.vector
        def _(dve):
            own = Tally(dve, dve_own)
            dve.wait_ge(ld_small, 6 * 16)
            nc.vector.tensor_copy(sel[:], fold_sb[:].unsqueeze(2).broadcast_to([P, 2 * NS, P])).then_inc(sel_built, 1)
            nc.vector.tensor_scalar(dskip_sb[:], dskip_sb[:], 1.0, None, ALU.add).then_inc(consts_made, 1)
            nc.vector.memset(series_sb[:], SERIES).then_inc(consts_made, 1)
            nc.vector.memset(dt_in[2 * NS:4 * NS, :], 1.0).then_inc(consts_made, 1)
            own.done(nc.vector.memset(bc[:], 0.0))
            dve.wait_ge(xp_done, 1)
            R = 2 * NS
            own.done(nc.vector.tensor_copy(bc[0:R, :], banks(6, 2)[0:R, :]))
            own.done(nc.vector.tensor_tensor(rest[0:R, :], banks(6, 2)[0:R, :], bc[0:R, :], ALU.subtract))
            own.done(nc.vector.tensor_copy(mid[0:R, :], rest[0:R, :]))
            own.done(nc.vector.tensor_copy(bc[R:2 * R, :], mid[0:R, :]))
            nc.vector.tensor_tensor(bc[2 * R:3 * R, :], rest[0:R, :], mid[0:R, :], ALU.subtract).then_inc(bc_split, 1)

            def make_dt(c):
                d = dt_[:, c, :]
                dve.wait_ge(softlog, 3 * c + 1)
                own.done(nc.vector.scalar_tensor_tensor(d, e_[:], -0.5, d, ALU.mult, ALU.add))
                own.done(nc.vector.scalar_tensor_tensor(d, d, 1.0, e_[:], ALU.add, ALU.mult))
                dve.wait_ge(softlog, 3 * c + 3)
                own.done(nc.vector.copy_predicated(log_e[:], small_e[:].bitcast(mybir.dt.uint16), d))
                dve.wait_ge(z_abs, c + 1)
                nc.vector.scalar_tensor_tensor(d, banks(4, 2), 0.0, log_e[:], ALU.max, ALU.add).then_inc(dt_done, 1)
                dve.wait_ge(dt_done, c + 1)
                own.done(nc.vector.tensor_tensor(dtx[:, c, :], d, xT[:, c, :], ALU.mult))

            def dbx(n, u, c):
                dve.wait_ge(b_bcast, n + NS * c + 1)
                nc.vector.tensor_tensor(banks(2 * u, 2), dtx[:, c, :], banks(2 * u, 2), ALU.mult).then_inc(dbx_done, 1)

            def scan(n, u, c, first=False):
                i = n + NS * c
                dve.wait_ge(dA_done, i + 1)
                dve.wait_ge(dbx_done, i + 1)
                if not (c == 0 and first):
                    dve.wait_ge(hc_done, i - 1)
                nc.vector.tensor_tensor_scan(hst[:, u, :], dA[:, u, :], banks(2 * u, 2), 0.0, ALU.mult, ALU.add).then_inc(scan_done, 1)

            def take_y(c):
                dve.wait_ge(y_added, NS * (c + 1))
                nc.vector.scalar_tensor_tensor(xT[:, c, :], xT[:, c, :], dskip_sb[:, c:c + 1], banks(6, 2),
                                               ALU.mult, ALU.add).then_inc(y_taken, 1)

            make_dt(0)
            dve.wait_ge(consts_made, 3)
            for c in range(DC):
                if c + 1 < DC:
                    make_dt(c + 1)
                for n in range(4):
                    dbx(n, n % 2, c)
                    scan(n, n % 2, c, n < 2)
                    if c and n == LAG - 1:
                        take_y(c - 1)
                with dve.Fori(2, NS // 2) as k:
                    for u in range(2):
                        dbx(2 * k + u, u, c)
                        scan(2 * k + u, u, c)
            take_y(DC - 1)

            def norm_stage(ln, scale, turn=True):
                def stats(t, u):
                    dve.wait_ge(ln_in, TT * ln + t + 1)
                    if ln:
                        dve.wait_ge(x_kept, TT * (ln - 1) + t + 1)
                    src = banks(u, 1)
                    if ln == 3:
                        src = xtok[:, t, :]
                        own.done(nc.vector.tensor_scalar(o_half[:], banks(u, 1), scale, None, ALU.mult))
                        own.done(nc.vector.tensor_tensor(src, src, o_half[:], ALU.add))
                    elif scale is not None:
                        src = xtok[:, t, :]
                        own.done(nc.vector.scalar_tensor_tensor(src, banks(u, 1), scale, src, ALU.mult, ALU.add))
                    own.done(nc.vector.bn_stats(st6[:], src))
                    own.done(nc.vector.bn_aggr(mv[:], st6[:]))
                    nc.vector.tensor_scalar(vare[:], mv[:, 1:2], EPS, None, ALU.add).then_inc(var_done, 1)

                def normalise(t, u, first=False):
                    dve.wait_ge(sdev_done, TT * ln + t + 1)
                    if ln == 3 and not first:
                        dve.wait_ge(out_stored[u], 16 * (t // 2))
                    elif ln or not first:
                        dve.wait_ge(x_kept, TT * ln + t - 1)
                        if turn or first:
                            dve.wait_ge(x_turned, TT * ln + t - 1)
                    own.done(nc.vector.reciprocal(rstd[:], sdev[:]))
                    src = banks(u, 1) if scale is None else xtok[:, t, :]
                    nc.vector.tensor_scalar(xn[:, u, :], src, mv[:, 0:1], rstd[:], ALU.subtract, ALU.mult).then_inc(x_normed, 1)

                def low(t, u):
                    dve.wait_ge(xh_done, TT * ln + t + 1)
                    nc.vector.tensor_tensor(XL[ln][:, :, ds(t * P, P)], ps[:, 2 + u, :].rearrange("p (c t) -> p c t", c=DC),
                                            XH[ln][:, :, ds(t * P, P)], ALU.subtract).then_inc(xl_done, 1)
                stats(0, 0)
                normalise(0, 0, True)
                dve.wait_ge(x_normed, TT * ln + 1)
                stats(1, 1)
                if turn:
                    low(0, 0)
                normalise(1, 1, True)
                for t in range(2, TT):
                    dve.wait_ge(x_normed, TT * ln + t)
                    stats(t, t % 2)
                    if turn:
                        low(t - 1, 1 - t % 2)
                    normalise(t, t % 2)
                if turn:
                    low(TT - 1, 1)
            XH = {0: xh, 1: xh}
            XL = {0: xl, 1: xl}
            norm_stage(0, None)

            for w in range(4):
                dve.wait_ge(w_high, w + 1)
                nc.vector.scalar_tensor_tensor(wsp[:, w, 1], wraw[:, w % 2], WS, wsp[:, w, 0], ALU.mult, ALU.subtract).then_inc(w_low, 1)

            def ffn0(m, u, first):
                dve.wait_ge(silu_done, m + 1)
                dve.wait_ge(up_done, m + 1)
                if not first:
                    dve.wait_ge(hl_done, m - 1)
                nc.vector.tensor_tensor(h32[:, u, :], sg[:, u, :], banks(4 * u + 2, 2), ALU.mult).then_inc(h_done, 1)
                dve.wait_ge(hh_done, m + 1)
                nc.vector.tensor_tensor(hl[:, m, :], h32[:, u, :], hh[:, m, :], ALU.subtract).then_inc(hl_done, 1)
            ffn0(0, 0, True)
            ffn0(1, 1, True)
            with dve.Fori(1, M0 // 2) as k:
                for u in range(2):
                    ffn0(2 * k + u, u, False)
            norm_stage(1, 1.0)
            dve.wait_ge(ld_tab, 3 * 16)

            def rope(w, t, u, first):
                dve.wait_ge((q_proj, k_proj)[w], t + 1)
                if not first:
                    dve.wait_ge(stack_low, 2 * t - 1 + w)
                src = banks(3 * u + w, 1).rearrange("p (h d) -> p h d", h=NH)
                h2 = HD // 2
                tab = lambda x, a, b: x[:, t, a:b].unsqueeze(1).broadcast_to([P, NH, b - a])
                nc.vector.tensor_tensor(rot_a[:, w], src, tab(cos_sb, 0, HD), ALU.mult)
                nc.vector.tensor_tensor(rot_b[:, w, :, 0:h2], src[:, :, h2:HD], tab(sin_sb, 0, h2), ALU.mult)
                nc.vector.tensor_tensor(rot_b[:, w, :, h2:HD], src[:, :, 0:h2], tab(sin_sb, h2, HD), ALU.mult).then_inc(roped, 1)

            def keep_keys(t):
                dve.wait_ge(k_turned, t + 1)
                nc.vector.tensor_copy(k_st[:, :, ds(t * P, P)], banks(6, 2).bitcast(f16).rearrange("p (r t) -> p r t", r=NP)).then_inc(k_kept, 1)

            for t in range(2):
                rope(0, t, t, t == 0)
                rope(1, t, t, t == 0)
                if t:
                    keep_keys(t - 1)
            with dve.Fori(1, TT // 2) as k:
                for u in range(2):
                    rope(0, 2 * k + u, u, False)
                    rope(1, 2 * k + u, u, False)
                    keep_keys(2 * k + u - 1)
            keep_keys(TT - 1)

            def maxima(k, use, n):
                _, dst, slices = SEARCH[k]
                w = slices[0][2]
                dve.wait_ge(ring_full, use + n + 1)
                nc.vector.reduce_max(dst, ps[:, n % 2, 0:len(slices) * w].rearrange("p (a w) -> p a w", a=len(slices)), AX).then_inc(ring_read, 1)

            def negate(g, use, n):
                dve.wait_ge(ring_read, use + n)
                nc.vector.tensor_tensor(m_a[:, 4:TT, :], m_a[:, 4:TT, :], m_b[:], ALU.max).then_inc(m_joined, 1)
                dve.wait_ge(m_joined, g + 1)
                nc.vector.tensor_scalar(m_neg[:], m_a[:], -1.0, None, ALU.mult).then_inc(m_negated, 1)
                dve.wait_ge(m_negated, g + 1)

            def keep_rows(g, use, n):
                dve.wait_ge(ring_full, use + n + 1)
                if not (isinstance(g, int) and g == 0):
                    dve.wait_ge(m_rows, 64 * g)
                nc.vector.tensor_copy(m_row[0:GH, :], ps[0:GH, n % 2, :].bitcast(f16)).then_inc(ring_read, 1)

            def divide(g, use, n, half):
                dve.wait_ge(ring_full, use + n + 1)
                src = ps[:, n % 2, :].rearrange("p (i a d) -> p i a d", i=4, a=GH)
                nc.vector.reciprocal(r_den[:].unsqueeze(3), src[:, :, :, HD:HD + 1]).then_inc(r_made, 1)
                dve.wait_ge(r_made, 2 * g + half + 1)
                nc.vector.tensor_tensor(o_tok[:, 4 * half:4 * half + 4, ds(g * GH * HD, GH * HD)].rearrange("p i (a d) -> p i a d", a=GH),
                                        src[:, :, :, 0:HD], r_den[:].unsqueeze(3).broadcast_to([P, 4, GH, HD]),
                                        ALU.mult).then_inc(ring_read, 1)
                dve.wait_ge(ring_read, use + n + 1)

            def body(g, use, side):
                n = 0
                for kind, *at in side:
                    if kind == "search":
                        maxima(at[1], use, n)
                    elif kind == "negate":
                        negate(g + 1, use, n)
                        continue
                    elif kind == "turn":
                        keep_rows(g + 1, use, n)
                    else:
                        divide(g - 1, use, n, at[0])
                    n += 1
            body(-1, 0, side_steps(False, 0, True))
            body(0, ring_base(0), side_steps(False, LEAD, True))
            with dve.Fori(1, NG - 2) as g:
                body(g, ring_base(g), side_steps(True, LEAD, True))
            body(NG - 2, ring_base(NG - 2), side_steps(True, LEAD, False))
            body(NG - 1, ring_base(NG - 1), [("out", 0), ("out", 1)])
            for half in range(2):
                divide(NG - 1, ring_base(NG - 1) + 2, half, half)

            def low_out(t):
                dve.wait_ge(oh_done, t + 1)
                nc.vector.tensor_tensor(ol[:, :, t * P:(t + 1) * P], ps[:, 2 + t % 2, :].rearrange("p (c t) -> p c t", c=DC),
                                        oh[:, :, t * P:(t + 1) * P], ALU.subtract).then_inc(ol_done, 1)
            for t in range(TT):
                low_out(t)
            def unpack(m, u, loads):
                dve.wait_ge(ld_w1[u], 48 * loads)
                nib = z_nib[:].rearrange("p (n h) -> p n h", h=2)
                byte = w_zeros[u][:].bitcast(u8).unsqueeze(2)
                nc.vector.tensor_scalar(nib[:, :, 0:1], byte, 15, None, ALU.bitwise_and)
                nc.vector.tensor_scalar(nib[:, :, 1:2], byte, 4, None, ALU.logical_shift_right)
                nc.vector.tensor_scalar(w_nib[:], w_words[u][:], shift_sb[:, 0:1], 15, ALU.logical_shift_right, ALU.bitwise_and).then_inc(w1_nib, 1)
                dve.wait_ge(w1_nib, m + 1)
                nc.vector.scalar_tensor_tensor(w_full[:], w_nib[:], 1.0, z_nib[:], ALU.subtract, ALU.subtract).then_inc(w1_full, 1)
                dve.wait_ge(w1_full, m + 1)

            dve.wait_ge(ld_shift, 16)
            unpack(0, 0, 1)
            XH[2], XL[2] = x3h, x3l
            norm_stage(2, 1.0 / WS)
            def weights_low(m, u):
                dve.wait_ge(w1_high, 2 * m + 2)
                nc.vector.scalar_tensor_tensor(gu[u][:, 1].rearrange("p b n -> p (b n)"), w_full[:, 0:2 * DC * P], WS,
                                               gu[u][:, 0].rearrange("p b n -> p (b n)"), ALU.mult, ALU.subtract)
                nc.vector.scalar_tensor_tensor(wd1[:, 1, m, :], w_full[:, 2 * DC * P:], WS, wd1[:, 0, m, :],
                                               ALU.mult, ALU.subtract).then_inc(w1_low, 1)
                dve.wait_ge(w1_low, m + 1)

            def ffn1(m, u, first):
                dve.wait_ge(silu1_done, m + 1)
                dve.wait_ge(up1_done, m + 1)
                if not first:
                    dve.wait_ge(h1l_done, m - 1)
                nc.vector.scalar_tensor_tensor(h132[:, u, :], banks(4 * u + 2, 2), 1.0 / WS, sg1[:, u, :], ALU.mult, ALU.mult).then_inc(h1_done, 1)
                dve.wait_ge(h1h_done, m + 1)
                nc.vector.tensor_tensor(h1l[:, m, :], h132[:, u, :], h1h[:, m, :], ALU.subtract).then_inc(h1l_done, 1)
            weights_low(0, 0)
            unpack(1, 1, 1)
            weights_low(1, 1)
            unpack(2, 0, 2)
            ffn1(0, 0, True)
            weights_low(2, 0)
            unpack(3, 1, 2)
            ffn1(1, 1, True)
            with dve.Fori(1, M1 // 2 - 1) as k:
                for u in range(2):
                    weights_low(2 * k + u + 1, 1 - u)
                    unpack(2 * k + u + 2, u, k + 2)
                    ffn1(2 * k + u, u, False)
            weights_low(M1 - 2, 1)
            unpack(M1 - 1, 0, M1 // 2 + 1)
            ffn1(M1 - 3, 0, False)
            weights_low(M1 - 1, 0)
            ffn1(M1 - 2, 1, False)
            ffn1(M1 - 1, 0, False)
            norm_stage(3, 1.0 / WS, turn=False)


def kernel(**inputs):
    import numpy as np
    import concourse.bacc as bacc
    from concourse.bass_utils import run_bass_kernel_spmd

    nc = bacc.Bacc("TRN2", target_bir_lowering=False, num_devices=1)
    get = {k: np.asarray(v) for k, v in inputs.items()}
    xw = get["L0_attn_x_proj_w"].T
    pos = np.arange(T, dtype=np.float32)
    theta = (1.0 / 10000.0 ** (np.arange(0, HD, 2, dtype=np.float32) / HD)).astype(np.float32)
    angle = np.outer(pos, theta).astype(np.float32)
    cos = np.concatenate([np.cos(angle), np.cos(angle)], -1) / np.float32(WS)
    sin = np.concatenate([-np.sin(angle), np.sin(angle)], -1) / np.float32(WS)
    tok, key = np.arange(P)[:, None], np.arange(P)[None, :]

    def tiles(kind, rows):
        per = P if kind != "zeros" else P // PACK
        at = np.zeros((M1, rows, 3 * DC, per), get["L1_ffn_gate_" + kind].dtype)
        for i, name in enumerate(("gate", "up")):
            a = get[f"L1_ffn_{name}_{kind}"].reshape(DC, rows, -1)
            for m in range(M1):
                part = a[:, :, m * per:(m + 1) * per]
                at[m, :, i * DC:(i + 1) * DC, :part.shape[2]] = part.transpose(1, 0, 2)
        a = get["L1_ffn_down_" + kind]
        for m in range(M1):
            part = a[m * rows:(m + 1) * rows]
            at[m, :part.shape[0], 2 * DC:] = part.reshape(part.shape[0], DC, per)
        return at.reshape(M1, rows, -1)

    arrays = {
        "x_fm": get["L0_attn_x"][0].T, "a_log": get["L0_attn_A_log"], "d_skip": get["L0_attn_D"].reshape(DC, P).T,
        "xw": np.concatenate([xw[:, DTR:], xw[:, :DTR]], 1), "dtw": np.concatenate([get["L0_attn_dt_proj_w"].T, get["L0_attn_dt_proj_b"][None, :]], 0),
        "wg0": get["L0_ffn_W_gate"].T, "wu0": get["L0_ffn_W_up"].T, "wd0": get["L0_ffn_W_down"].T,
        "wq": get["L1_attn_wq"].T, "wk": get["L1_attn_wk"].T, "wv": get["L1_attn_wv"].T, "wo": get["L1_attn_wo"].T,
        "w1_q": np.repeat(tiles("qweight", P // PACK), PACK, axis=1), "w1_s": tiles("scales", 1)[:, 0], "w1_z": tiles("zeros", 1)[:, 0],
        "ident": np.eye(P, dtype=np.float32),
        "fold": np.concatenate([np.eye(2 * NS, dtype=np.float32)] * 3 + [np.zeros((2 * NS, 2 * NS), np.float32)], 0),
        "mask": np.where(key > tok, np.float32(-1e30), np.float32(0)),
        "cos": cos.astype(np.float32), "sin": sin.astype(np.float32),
        "shifts": ((np.arange(P) % PACK) * 4).astype(np.int32)[:, None],
    }
    feeds, args = {}, []
    for name, a in arrays.items():
        a = np.ascontiguousarray(a)
        feeds[f"in_{name}_dram"] = a
        args.append(nc.dram_tensor(f"in_{name}_dram", a.shape, mybir.dt.from_np(a.dtype), kind="ExternalInput").ap())
    args.append(nc.dram_tensor("out_0_dram", (1, T, D), f32_dt(), kind="ExternalOutput").ap())
    build(nc, *args)
    r = run_bass_kernel_spmd(nc, [feeds], core_ids=[0])
    return r.results[0]["out_0_dram"]


def f32_dt():
    return mybir.dt.float32
```

```python
import concourse.bass as bass
from concourse import mybir
from contextlib import ExitStack

P = 128
T = 1024
TT = T // P
D = 512
DC = D // P
NS = 16
DTR = 16
F0 = 1792
M0 = F0 // P
F1 = 1376
M1 = (F1 + P - 1) // P
TAIL = F1 - (M1 - 1) * P
NH = 32
HD = D // NH
NP = NH // 2
GH = 4
NG = NH // GH
HALF = 512
EPS = 1e-5
WS = 256.0
PACK = 8
SERIES = 2.0 ** -7
DT_BANK = (4, 6, 4, 4)
LN_BANKS = ((4, 5, 6, 7), (0, 1), (0, 1), (0, 1))
LAG = 4


class Tally:

    def __init__(self, eng, sem):
        self.eng, self.sem, self.at = eng, sem, 0

    def done(self, ins):
        ins.then_inc(self.sem, 1)
        self.at = self.at + 1
        self.eng.wait_ge(self.sem, self.at)

    def loop(self, i, per):
        self.base = self.at
        self.at = self.base + i * per

    def end(self, passes, per):
        self.at = self.base + passes * per


def build(nc, x_fm, a_log, d_skip, xw, dtw, wg0, wu0, wd0, wq, wk, wv, wo,
          w1_q, w1_s, w1_z, ident, fold, mask, cos, sin, shifts, out):
    f32, f16, bf16, i32, u8 = mybir.dt.float32, mybir.dt.float16, mybir.dt.bfloat16, mybir.dt.int32, mybir.dt.uint8
    ALU = mybir.AluOpType
    ACT = mybir.ActivationFunctionType
    AX = mybir.AxisListType.X
    ds = bass.ds

    ctx = ExitStack()
    with ctx:
        arena = ctx.enter_context(nc.sbuf_tensor("arena", [P, 200 * 256], f32))

        def view(kb, cols, dt):
            size = 4 if dt in (f32, i32) else 2
            a = int(kb * 256)
            return arena[:, a:a + cols * size // 4].bitcast(dt) if dt != f32 else arena[:, a:a + cols]

        def small(name, shape, dt=f32):
            return ctx.enter_context(nc.sbuf_tensor(name, shape, dt))

        def sem(name):
            return ctx.enter_context(nc.semaphore(name))

        ps = ctx.enter_context(nc.psum_tensor("ps", [P, 8, HALF], f32))

        def banks(a, n):
            return ps[:, a:a + n, :].rearrange("p b n -> p (b n)")

        xT = view(0, DC * T, f32).rearrange("p (c t) -> p c t", c=DC)
        dt_ = view(16, DC * T, f32).rearrange("p (c t) -> p c t", c=DC)
        dtx = view(32, DC * T, f32).rearrange("p (c t) -> p c t", c=DC)
        c_all = view(48, NS * T, f32).rearrange("p (n t) -> p n t", n=NS)
        dA = view(112, 2 * T, f32).rearrange("p (b t) -> p b t", b=2)
        hst = view(120, 2 * T, f32).rearrange("p (b t) -> p b t", b=2)
        hC = [view(kb, T, f32) for kb in (128, 132, 186, 190)]
        sel = view(136, 2 * NS * P, bf16).rearrange("p (n m) -> p n m", n=2 * NS)
        bc = view(144, T, bf16)
        rest = view(108, T, f32)
        mid = view(104, T, bf16)
        dt_in = view(146, T, f32)
        dBx = [view(kb, T, f32) for kb in (154, 172, 176, 180)]
        e_, log_e, small_e = view(150, T, f32), view(194, T, f32), view(198, T, f16)
        wg0_sb = view(158, DC * F0, f16).rearrange("p (c m) -> p c m", c=DC)
        wu0_sb = view(172, DC * F0, f16).rearrange("p (c m) -> p c m", c=DC)
        wd0_sb = view(186, M0 * D, f16).rearrange("p (m d) -> p m d", m=M0)
        xtok = view(16, TT * D, f32).rearrange("p (i d) -> p i d", i=TT)
        xh = view(32, DC * T, f16).rearrange("p (c t) -> p c t", c=DC)
        xl = view(40, DC * T, f16).rearrange("p (c t) -> p c t", c=DC)
        hh = view(48, M0 * T, f16).rearrange("p (m t) -> p m t", m=M0)
        hl = view(76, M0 * T, f16).rearrange("p (m t) -> p m t", m=M0)
        sg = view(104, 2 * T, f32).rearrange("p (b t) -> p b t", b=2)
        h32 = view(112, 2 * T, f32).rearrange("p (b t) -> p b t", b=2)
        wraw = view(0, 2 * DC * D, f32).rearrange("p (b c d) -> p b c d", b=2, c=DC)
        wsp = view(120, 4 * 2 * DC * D, f16).rearrange("p (w s c d) -> p w s c d", w=4, s=2, c=DC)

        ident_sb = small("ident_sb", [P, P])
        fold_sb = small("fold_sb", [P, 2 * NS])
        alog_sb = small("alog_sb", [P, DC, NS])
        negA = small("negA", [P, DC, NS])
        dskip_sb = small("dskip_sb", [P, DC])
        series_sb = small("series_sb", [P, 1])
        square_sb = small("square_sb", [P, 1])
        xw_sb = small("xw_sb", [P, DC, 2 * NS + DTR])
        dtw_sb = small("dtw_sb", [2 * NS + DTR + 1, D])
        xn = view(152, 2 * D, f32).rearrange("p (b d) -> p b d", b=2)
        st6 = small("st6", [P, 6])
        mv = small("mv", [P, 2, 2])
        vare = small("vare", [P, 2])
        sdev = small("sdev", [P, 2])
        rstd = small("rstd", [P, 1])
        tok_stack = view(0, 2 * NH * 64, f16).rearrange("p (w h d) -> p w h d", w=2, h=NH)
        rot_a = view(188, 2 * D, f32).rearrange("p (w h d) -> p w h d", w=2, h=NH)
        rot_b = view(192, 2 * D, f32).rearrange("p (w h d) -> p w h d", w=2, h=NH)
        q_st = view(48, NP * T, f16).rearrange("p (r t) -> p r t", r=NP)
        k_st = view(80, NP * T, f16).rearrange("p (r t) -> p r t", r=NP)
        v_tok = view(156, TT * D, f32).rearrange("p (i d) -> p i d", i=TT)
        def qkv_bank(t, w):
            return (4, 5, 2, 3)[(3 * t + w) % 4]

        v_ring = [view(kb, TT * GH * 32, f32).rearrange("p (i a d) -> p i a d", i=TT, a=GH) for kb in (172, 176)]
        k_pad = [view(kb, GH * T, f16).rearrange("p (a t) -> p a t", a=GH) for kb in (112, 120)]
        p_t = [view(kb, GH * T, f32).rearrange("p (a t) -> p a t", a=GH) for kb in (0, 128)]
        o_tok = view(32, TT * D, f32).rearrange("p (i d) -> p i d", i=TT)
        o_raw = view(188, T, f32)
        m_row = view(192, T, f16)
        m_a = view(199, TT * GH, f32).rearrange("p (i a) -> p i a", i=TT)
        m_b = view(199.25, 4 * GH, f32).rearrange("p (i a) -> p i a", i=4)
        m_neg = view(199.5, TT * GH, f16).rearrange("p (i a) -> p i a", i=TT)
        r_den = view(199.75, 4 * GH, f32).rearrange("p (i a) -> p i a", i=4)
        oh = view(96, DC * T, f16).rearrange("p (c t) -> p c t", c=DC)
        ol = view(104, DC * T, f16).rearrange("p (c t) -> p c t", c=DC)
        x3h = view(64, DC * T, f16).rearrange("p (c t) -> p c t", c=DC)
        x3l = view(72, DC * T, f16).rearrange("p (c t) -> p c t", c=DC)
        cos_sb = small("cos_sb", [P, TT, HD])
        sin_sb = small("sin_sb", [P, TT, HD])
        mask_sb = small("mask_sb", [P, P])
        mask_b = small("mask_b", [P, P], bf16)
        ident_b = small("ident_b", [P, P], bf16)
        ident_h = small("ident_h", [P, P], f16)
        ld_tab, tables_made = sem("ld_tab"), sem("tables_made")
        q_proj, k_proj, v_proj = sem("q_proj"), sem("k_proj"), sem("v_proj")
        roped, rope_summed, stack_high, stack_low, stacks_set = (
            sem("roped"), sem("rope_summed"), sem("stack_high"), sem("stack_low"), sem("stacks_set"))
        q_turned, k_turned, q_kept, k_kept, v_kept = (
            sem("q_turned"), sem("k_turned"), sem("q_kept"), sem("k_kept"), sem("v_kept"))
        pads_zeroed, v_ones = sem("pads_zeroed"), sem("v_ones")
        k_first = [sem(f"k_first{i}") for i in range(TT)]
        k_padded = [[sem(f"k_padded{slot}_{half}") for half in range(2)] for slot in range(2)]
        v_ringed, ring_full, ring_read = sem("v_ringed"), sem("ring_full"), sem("ring_read")
        m_joined, m_negated, m_rows, r_made = sem("m_joined"), sem("m_negated"), sem("m_rows"), sem("r_made")
        st_full, exp_done, pv_step, o_kept = sem("st_full"), sem("exp_done"), sem("pv_step"), sem("o_kept")
        o_turned, oh_done, ol_done = sem("o_turned"), sem("oh_done"), sem("ol_done")

        LEAD = 9
        BEFORE_TURN = 1

        def max_units(i):
            w = P * (i + 1)
            if w <= HALF:
                n = HALF // w if w != 3 * P else 1
                return [(m_a[:, i, a:a + n], [(a + b, 0, w, b * w) for b in range(n)]) for a in range(0, GH, n)]
            units = [(m_a[:, i, a:a + 1], [(a, 0, HALF, 0)]) for a in range(GH)]
            w -= HALF
            n = HALF // w if w != 3 * P else 1
            return units + [(m_b[:, i - 4, a:a + n], [(a + b, HALF, w, b * w) for b in range(n)]) for a in range(0, GH, n)]
        SEARCH = [(i, dst, slices) for i in range(TT) for dst, slices in max_units(i)]
        UNITS = len(SEARCH) + 1
        BODY = UNITS + 2
        SIDE_FIRST = 0.05
        OUT_AT = 8

        def side_steps(outs, begin, ahead):
            steps = []
            for k in range(begin, len(SEARCH)):
                if outs and k == begin + OUT_AT:
                    steps += [("out", 0), ("out", 1)]
                steps.append(("search", 0, k))
            steps.append(("negate",))
            steps += [("search", 1, k) for k in range(0, BEFORE_TURN if ahead else 0)]
            steps.append(("turn",))
            steps += [("search", 1, k) for k in range(BEFORE_TURN, LEAD if ahead else 0)]
            return steps

        EARLY_TILES = TT - 2
        EARLY = sum(len(max_units(i)) for i in range(EARLY_TILES))
        FIRST_HIGH = next(k for k, (i, _, slices) in enumerate(SEARCH) if slices[0][1] + slices[0][2] > HALF)

        def early_units(t, place):
            units = [k for k, (i, _, _) in enumerate(SEARCH) if i == t - 2]
            return units[2 * place:2 * place + 2]

        def turned_at(steps):
            return steps.index(("turn",))

        def ring_base(g):
            if isinstance(g, int) and g == 0:
                return UNITS + LEAD
            return 2 * UNITS + LEAD - BODY + g * BODY - (LEAD if isinstance(g, int) and g == NG - 1 else 0)

        def exp_units(j):
            return [(a,) for a in range(GH)] if T - P * j > HALF else [(0, 1), (2, 3)]
        EXPS = sum(len(exp_units(j)) for j in range(TT))

        def value_pieces(j):
            return ([(6, P * j, HALF, 0)] if j < 4 else []) + [(7, max(P * j - HALF, 0), HALF, max(HALF - P * j, 0))]

        def group_order(side):
            col = 0.43e-3
            main = []
            for j in range(TT + 1):
                new, old = [], []
                if j < TT:
                    w = T - P * j
                    for heads in exp_units(j):
                        new.append((("keys", j, heads), len(heads) * (w * col + 0.06), 0.05 + len(heads) * w * 0.83e-3))
                if j:
                    old = [(("values", j - 1, k), 4 * (hi - lo) * col, 0) for k, (_, lo, hi, _) in enumerate(value_pieces(j - 1))]
                main += new[:2] + old + new[2:]
            side = list(side)
            order, pe_at, dve, act, exps_of, negated, kept, padded = [], 0.0, [0.0, 0.0], [0.0, 0.0], {}, 0.0, 1e8, 1e8
            while main or side:
                if side and side[0][0] == "negate":
                    side.pop(0)
                    dve[-1] += 0.4
                    negated = dve[-1] + 0.1
                    continue
                m = s = 1e9
                if main:
                    m = max(pe_at, 0.2 + (act[-2] if main[0][0][0] == "keys" else exps_of[main[0][0][1]]))
                if side:
                    s = max(pe_at, dve[-2] + 0.3, {"turn": negated, "out": kept, "search": padded if side[0][1:2] == (1,) else 0.0}[side[0][0]])
                if s <= m + SIDE_FIRST:
                    step = side.pop(0)
                    cols = sum(x[2] for x in SEARCH[step[2]][2]) if step[0] == "search" else 0
                    pe_at = s + (cols * col if cols else 0.45)
                    dve.append(max(dve[-1], pe_at) + (0.4 if step[0] == "out" else 0.0) + 0.07 + (cols or HALF) * 1.04e-3)
                else:
                    step, cost, after = main.pop(0)
                    pe_at = m + cost
                    if after:
                        act.append(max(act[-1], pe_at) + after)
                        exps_of[step[1]] = act[-1]
                        if step[1] == TT // 2 - 1:
                            padded = pe_at + 3.0
                        if step[:2] == ("keys", 0) and step[2][-1] == GH - 1:
                            act[-1] += 0.9
                            kept = act[-1] + 0.2
                order.append(step)
            return order
        NB = 2 * DC + DC
        w_words = [view(kb, NB * P, i32) for kb in (156, 162)]
        w_scales = [view(kb, NB * P, f16) for kb in (168, 171)]
        w_zeros = [view(kb, NB * P // PACK, i32) for kb in (174, 175)]
        w_nib = view(182, NB * P, i32)
        w_full = view(80, NB * P, f32)
        z_nib = view(196, NB * P // 2, f16).bitcast(u8)
        o_half = view(198, D, f16)
        gu = [view(kb, 2 * 2 * DC * P, f16).rearrange("p (s b n) -> p s b n", s=2, b=2 * DC) for kb in (56, 60)]
        wd1 = view(124, 2 * M1 * D, f16).rearrange("p (s m d) -> p s m d", s=2, m=M1)
        h1h = view(102, M1 * T, f16).rearrange("p (m t) -> p m t", m=M1)
        h1l = view(32, M1 * T, f16).rearrange("p (m t) -> p m t", m=M1)
        sg1 = view(0, 2 * T, f32).rearrange("p (b t) -> p b t", b=2)
        h132 = view(8, 2 * T, f32).rearrange("p (b t) -> p b t", b=2)
        shift_sb = small("shift_sb", [P, 1], i32)
        ld_shift = sem("ld_shift")
        ld_w1 = [sem("ld_w1_0"), sem("ld_w1_1")]
        w1_nib, w1_full, w1_scaled, w1_high, w1_low = (
            sem("w1_nib"), sem("w1_full"), sem("w1_scaled"), sem("w1_high"), sem("w1_low"))
        gate1_done, up1_done, silu1_done, h1_done, h1h_done, h1l_done = (
            sem("gate1_done"), sem("up1_done"), sem("silu1_done"), sem("h1_done"), sem("h1h_done"), sem("h1l_done"))
        out_stored = [sem("out_stored0"), sem("out_stored1")]

        ld_xw, ld_small, ld_w0 = sem("ld_xw"), sem("ld_small"), sem("ld_w0")
        ld_x = [sem(f"ld_x{c}") for c in range(DC)]
        ld_wraw = [sem(f"ld_wraw{w}") for w in range(4)]
        sel_built, consts_made = sem("sel_built"), sem("consts_made")
        xp_done, bc_split, dtin_done, negA_done = sem("xp_done"), sem("bc_split"), sem("dtin_done"), sem("negA_done")
        dtl_done, z_abs, softlog, dt_done = sem("dtl_done"), sem("z_abs"), sem("softlog"), sem("dt_done")
        b_bcast, c_bcast, c_kept = sem("b_bcast"), sem("c_bcast"), sem("c_kept")
        dA_done, dbx_done, scan_done, hc_done = sem("dA_done"), sem("dbx_done"), sem("scan_done"), sem("hc_done")
        y_added, y_taken = sem("y_added"), sem("y_taken")
        x_kept = sem("x_kept")
        ln_in, ln_taken, var_done, sdev_done, x_normed = sem("ln_in"), sem("ln_taken"), sem("var_done"), sem("sdev_done"), sem("x_normed")
        x_turned, xh_done, xl_done = sem("x_turned"), sem("xh_done"), sem("xl_done")
        gate_done, up_done, silu_done, h_done, hh_done, hl_done = (
            sem("gate_done"), sem("up_done"), sem("silu_done"), sem("h_done"), sem("hh_done"), sem("hl_done"))
        w_high, w_low = sem("w_high"), sem("w_low")
        dve_own, act_own = sem("dve_own"), sem("act_own")

        block = ctx.enter_context(nc.Block())

        @block.sync
        def _(sp):
            sp.dma_start(xw_sb[:], xw.rearrange("(c p) r -> p c r", p=P)).then_inc(ld_xw, 16)
            for c in range(DC):
                sp.dma_start(xT[:, c, :], x_fm[c * P:(c + 1) * P, :]).then_inc(ld_x[c], 16)
            for dst, src in ((fold_sb[:], fold), (dtw_sb[2 * NS:, :], dtw), (dskip_sb[:], d_skip),
                             (alog_sb[:], a_log.rearrange("(c p) n -> p c n", p=P)), (ident_sb[:], ident)):
                sp.dma_start(dst, src).then_inc(ld_small, 16)
            sp.dma_start(wg0_sb[:], wg0.rearrange("(c p) m -> p c m", p=P)).then_inc(ld_w0, 16)
            sp.wait_ge(scan_done, DC * NS)
            sp.dma_start(wu0_sb[:], wu0.rearrange("(c p) m -> p c m", p=P)).then_inc(ld_w0, 16)
            sp.wait_ge(y_added, DC * NS)
            sp.dma_start(wd0_sb[:], wd0.rearrange("(m p) d -> p m d", p=P)).then_inc(ld_w0, 16)
            sp.wait_ge(ln_in, TT)
            for w, src in enumerate((wq, wk, wv, wo)):
                if w >= 2:
                    sp.wait_ge(w_low, w - 1)
                sp.dma_start(wraw[:, w % 2], src.rearrange("(c p) d -> p c d", p=P)).then_inc(ld_wraw[w], 16)
            for dst, src in ((cos_sb[:], cos.rearrange("(i p) d -> p i d", p=P)),
                             (sin_sb[:], sin.rearrange("(i p) d -> p i d", p=P)), (mask_sb[:], mask)):
                sp.dma_start(dst, src).then_inc(ld_tab, 16)

            def pad_keys(g, slot, half):
                at = slice(half * HALF, (half + 1) * HALF)
                for b in range(2):
                    sp.dma_start(k_pad[slot][64 * b:64 * b + 64, b::2, at],
                                 k_st[64 * b:64 * b + 64, ds(2 * g, 2), at]).then_inc(k_padded[slot][half], 16)

            def put_rows(g, use):
                sp.wait_ge(ring_read, use)
                for b in range(2):
                    for r in range(2):
                        sp.dma_start(q_st[64 * b + 48:64 * b + 49, ds(2 * g + r, 1), :],
                                     m_row[2 * r + b:2 * r + b + 1, :].unsqueeze(1)).then_inc(m_rows, 16)
            sp.wait_ge(pads_zeroed, 1)
            for i in range(TT):
                sp.wait_ge(k_kept, i + 1)
                at = slice(i * P, (i + 1) * P)
                for b in range(2):
                    sp.dma_start(k_pad[0][64 * b:64 * b + 64, b::2, at],
                                 k_st[64 * b:64 * b + 64, 0:2, at]).then_inc(k_first[i], 16)
            sp.wait_ge(pads_zeroed, 2)
            for half in range(2):
                pad_keys(1, 1, half)
            sp.wait_ge(q_kept, TT)
            put_rows(0, turned_at(side_steps(False, 0, True)))

            def sync_body(g, slot, first=False, ahead=True):
                if ahead:
                    sp.wait_ge(st_full, EXPS * g + TT // 2 * GH)
                    pad_keys(g + 2, slot, 0)
                put_rows(g + 1, ring_base(g) + turned_at(side_steps(not first, LEAD, ahead)))
                if ahead:
                    sp.wait_ge(st_full, EXPS * (g + 1))
                    pad_keys(g + 2, slot, 1)
            sync_body(0, 0, first=True)
            with sp.Fori(0, 2) as k:
                for b in range(2):
                    sync_body(2 * k + 1 + b, 1 - b)
            sync_body(5, 1)
            sync_body(6, 0, ahead=False)
            sp.dma_start(shift_sb[:], shifts).then_inc(ld_shift, 16)

            def load_tile(m, slot):
                sp.dma_start(w_words[slot][:], w1_q[ds(m, 1)].rearrange("m r n -> (m r) n")).then_inc(ld_w1[slot], 16)
                sp.dma_start(w_scales[slot][:], w1_s[ds(m, 1), :].broadcast_to([P, NB * P])).then_inc(ld_w1[slot], 16)
                sp.dma_start(w_zeros[slot][:], w1_z[ds(m, 1), :].broadcast_to([P, NB * P // PACK])).then_inc(ld_w1[slot], 16)
            sp.wait_ge(v_ringed, NG)
            sp.wait_ge(pv_step, (NG - 1) * TT)
            load_tile(0, 0)
            load_tile(1, 1)
            with sp.Fori(1, M1 // 2) as k:
                for u in range(2):
                    sp.wait_ge(w1_nib, 2 * k + u - 1)
                    sp.wait_ge(w1_scaled, 2 * k + u - 1)
                    load_tile(2 * k + u, u)
            sp.wait_ge(w1_nib, M1 - 2)
            sp.wait_ge(w1_scaled, M1 - 2)
            load_tile(M1 - 1, 0)
            for t in range(TT):
                sp.wait_ge(x_normed, 3 * TT + t + 1)
                sp.dma_start(out[0, t * P:(t + 1) * P, :], xn[:, t % 2, :]).then_inc(out_stored[t % 2], 16)
            for u in range(2):
                sp.wait_ge(out_stored[u], 16 * TT // 2)

        @block.tensor
        def _(pe):
            pe.wait_ge(ld_xw, 16)
            for c in range(DC):
                pe.wait_ge(ld_x[c], 16)
                for h in range(2):
                    last = nc.tensor.matmul(banks(6 + h, 1)[0:2 * NS + DTR, :], xw_sb[:, c, :],
                                            xT[:, c, h * HALF:(h + 1) * HALF], start=(c == 0), stop=(c == DC - 1))
            last.then_inc(xp_done, 1)

            def dt_linear(c):
                for h in range(2):
                    last = nc.tensor.matmul(banks(DT_BANK[c] + h, 1), dtw_sb[2 * NS:, c * P:(c + 1) * P],
                                            dt_in[2 * NS:2 * NS + DTR + 1, h * HALF:(h + 1) * HALF], start=True, stop=True)
                last.then_inc(dtl_done, 1)

            def bcast(row, bank, signal):
                for h in range(2):
                    last = nc.tensor.matmul(banks(bank + h, 1), sel[:, row, :], bc[:, h * HALF:(h + 1) * HALF],
                                            start=True, stop=True)
                last.then_inc(signal, 1)

            def add_y(slot, start, stop):
                for h in range(2):
                    last = nc.tensor.matmul(banks(6 + h, 1), ident_sb[:], hC[slot][:, h * HALF:(h + 1) * HALF],
                                            start=start, stop=stop)
                last.then_inc(y_added, 1)

            pe.wait_ge(dtin_done, 1)
            pe.wait_ge(ld_small, 5 * 16)
            dt_linear(0)
            pe.wait_ge(bc_split, 1)
            dt_linear(1)
            pe.wait_ge(sel_built, 1)
            for c in range(DC):
                if c and c + 1 < DC:
                    if c == 1:
                        pe.wait_ge(c_kept, NS)
                    else:
                        pe.wait_ge(dt_done, c + 1)
                    dt_linear(c + 1)
                def step(n, u, lagged, start=False, stop=False, first=False):
                    i = n + NS * c
                    if not first:
                        pe.wait_ge(dbx_done, i - 1)
                    bcast(n, 2 * (u % 2), b_bcast)
                    if c == 0:
                        if first and u == 0:
                            pe.wait_ge(z_abs, 1)
                            pe.wait_ge(dt_done, 1)
                        else:
                            pe.wait_ge(c_kept, n)
                        bcast(n + NS, 4, c_bcast)
                    if lagged:
                        pe.wait_ge(hc_done, i - LAG + 1)
                        if start and c:
                            pe.wait_ge(y_taken, c)
                        if start and c == 0:
                            pe.wait_ge(dt_done, 2)
                        add_y((u - LAG) % 4, start, stop)
                for n in range(8):
                    step(n, n % 4, c > 0 or n >= LAG, start=(n == LAG), stop=(n == LAG - 1), first=(c == 0 and n < 2))
                with pe.Fori(2, NS // 4) as k:
                    for u in range(4):
                        step(4 * k + u, u, True)
            for n in range(NS - LAG, NS):
                pe.wait_ge(hc_done, (DC - 1) * NS + n + 1)
                add_y(n % 4, False, n == NS - 1)

            def norm_stage(ln, make, turn=True, straight=False, between=None):
                def produce(t, u, first):
                    if not first:
                        pe.wait_ge(ln_taken if ln else x_normed, TT * max(ln - 1, 0) + t + 1 - len(LN_BANKS[ln]))
                    make(t, LN_BANKS[ln][t % 4] if ln == 0 else u).then_inc(ln_in, 1)

                def turn_tile(t, u, first):
                    pe.wait_ge(x_normed, TT * ln + t + 1)
                    if not first:
                        pe.wait_ge(xl_done, TT * ln + t - 1)
                    for c in range(DC):
                        last = nc.tensor.transpose(ps[:, 2 + u, c * P:(c + 1) * P], xn[:, u, c * P:(c + 1) * P], ident_sb[:])
                    last.then_inc(x_turned, 1)

                produce(0, 0, True)
                produce(1, 1, True)
                for t in range(2, TT if straight else 4):
                    produce(t, t % 2, ln == 0 and t < 4)
                    if turn:
                        turn_tile(t - 2, t % 2, t < 4)
                if not straight:
                    with pe.Fori(2, TT // 2) as k:
                        for u in range(2):
                            produce(2 * k + u, u, False)
                            if turn:
                                turn_tile(2 * k + u - 2, u, False)
                if between is not None:
                    between()
                if turn:
                    turn_tile(TT - 2, 0, False)
                    turn_tile(TT - 1, 1, False)

            def turn_residual(t, u):
                for c in range(DC):
                    last = nc.tensor.transpose(ps[:, u, c * P:(c + 1) * P], xT[:, c, t * P:(t + 1) * P], ident_sb[:])
                return last

            pe.wait_ge(y_taken, DC)
            def project(w, src_h, src_l, t, bank, signal):
                for c in range(DC):
                    for part, s in ((src_h, 0), (src_l, 0), (src_h, 1)):
                        last = nc.tensor.matmul(banks(bank, 1), part[:, c, ds(t * P, P)], wsp[:, w, s, c, :],
                                                start=(c == 0 and part is src_h and s == 0), stop=(c == DC - 1 and s == 1))
                return last.then_inc(signal, 1) if signal is not None else last

            def first_projections():
                pe.wait_ge(xl_done, TT + 1)
                pe.wait_ge(w_low, 4)
                project(0, xh, xl, 0, qkv_bank(0, 0), q_proj)
                project(1, xh, xl, 0, qkv_bank(0, 1), k_proj)


            def gate_up0(m, u, halves=(0, 1), first=False):
                for w, bank, free, signal in ((wg0_sb, 4 - 4 * u, silu_done, gate_done), (wu0_sb, 6 - 4 * u, h_done, up_done)):
                    if not first:
                        pe.wait_ge(free, m - 1)
                    elif halves == (0,):
                        pe.wait_ge(x_normed, bank + 1)
                    for c in range(DC):
                        for part in (xh, xl):
                            for h in halves:
                                last = nc.tensor.matmul(banks(bank + h, 1), w[:, c, ds(m * P, P)],
                                                        part[:, c, h * HALF:(h + 1) * HALF],
                                                        start=(c == 0 and part is xh), stop=(c == DC - 1 and part is xl))
                    if halves != (0,):
                        last.then_inc(signal, 1)

            def first_gate_up0():
                pe.wait_ge(ld_w0, 3 * 16)
                pe.wait_ge(xl_done, TT // 2)
                gate_up0(0, 0, (0,), first=True)
            norm_stage(0, turn_residual, straight=True, between=first_gate_up0)
            pe.wait_ge(xl_done, TT)
            gate_up0(0, 0, (1,), first=True)
            gate_up0(1, 1, first=True)
            with pe.Fori(1, M0 // 2) as k:
                for u in range(2):
                    gate_up0(2 * k + u, u)

            def down0(t, u):
                for m in range(M0):
                    if isinstance(t, int) and t == 0 and m == M0 - 1:
                        pe.wait_ge(hl_done, M0)
                    for part in (hh, hl):
                        last = nc.tensor.matmul(banks(u, 1), part[:, m, ds(t * P, P)], wd0_sb[:, m, :],
                                                start=(m == 0 and part is hh), stop=(m == M0 - 1 and part is hl))
                return last
            pe.wait_ge(silu_done, M0)
            pe.wait_ge(hl_done, M0 - 1)
            norm_stage(1, down0, between=first_projections)
            pe.wait_ge(xl_done, 2 * TT)
            pe.wait_ge(tables_made, 3)

            turned = banks(6, 2).bitcast(f16)

            def turn_stack(w, t):
                pe.wait_ge(stack_low, 2 * t + w + 1)
                for r in range(NP):
                    last = nc.tensor.transpose(turned[:, r * P:(r + 1) * P],
                                               tok_stack[:, w, 2 * r:2 * r + 2, :].rearrange("p h d -> p (h d)"), ident_h[:])
                last.then_inc((q_turned, k_turned)[w], 1)

            def ring_slot(use, n):
                need = use + n - (n > 0)
                if not isinstance(need, int) or need > 0:
                    pe.wait_ge(ring_read, need)
                return n % 2

            def search(g, slot, k, use, n):
                i, _, slices = SEARCH[k]
                bank = ring_slot(use, n)
                for a, key, w, col in slices:
                    dst = ps[:, bank, col:col + w]
                    diag = key + w == P * (i + 1)
                    last = nc.tensor.matmul(dst, q_st[:, ds(2 * g + a // 2, 1), i * P:(i + 1) * P].rearrange("p a t -> p (a t)"),
                                            k_pad[slot][:, a, key:key + w], start=True, stop=not diag)
                    if diag:
                        last = nc.tensor.matmul(dst[:, w - P:w], ident_b[:], mask_b[:], start=False, stop=True)
                last.then_inc(ring_full, 1)

            project(2, xh, xl, 0, qkv_bank(0, 2), v_proj)
            for t in range(1, TT):
                for w, signal in ((0, q_proj), (1, k_proj), (2, v_proj)):
                    if w:
                        pe.wait_ge(roped, 2 * t - 2 + w)
                    elif t >= 2:
                        pe.wait_ge(v_kept, t - 1)
                    project(w, xh, xl, t, qkv_bank(t, w), signal)
                    if w == 0 and t >= 2:
                        pe.wait_ge(k_kept, t - 1)
                    if w == 1:
                        pe.wait_ge(q_kept, t)
                    if w < 2:
                        turn_stack(w, t - 1)
                    for k in early_units(t, w):
                        pe.wait_ge(k_first[t - 2], 32)
                        search(0, 0, k, 0, k)
            pe.wait_ge(k_kept, TT - 1)
            turn_stack(0, TT - 1)
            pe.wait_ge(q_kept, TT)
            turn_stack(1, TT - 1)

            def turn_maxima(g, use, n):
                pe.wait_ge(m_negated, g + 1)
                bank = ring_slot(use, n)
                dst = ps[:, bank, :].bitcast(f16)
                for i in range(TT):
                    last = nc.tensor.transpose(dst[0:GH, i * P:(i + 1) * P], m_neg[:, i, :], ident_h[:])
                last.then_inc(ring_full, 1)

            def keys(g, slot, j, heads, e):
                w = T - P * j
                bank = 2 + 2 * (e % 2)
                if not (isinstance(g, int) and g == 0 and e < 2):
                    pe.wait_ge(exp_done, EXPS * g + e - 1)
                for b, a in enumerate(heads):
                    row = ds(2 * g + a // 2, 1)
                    for h in range(2 if w > HALF else 1):
                        lo, hi = h * HALF, min(w, (h + 1) * HALF)
                        dst = ps[:, bank + b + h, 0:hi - lo]
                        last = nc.tensor.matmul(dst, k_pad[slot][:, a, j * P:(j + 1) * P],
                                                q_st[:, row, j * P + lo:j * P + hi].rearrange("p a t -> p (a t)"),
                                                start=True, stop=(h == 1))
                        if h == 0:
                            last = nc.tensor.matmul(dst[:, 0:P], mask_b[:], ident_b[:], start=False, stop=True)
                last.then_inc(st_full, 1)

            def values(slot, j, k):
                pieces = value_pieces(j)
                bank, lo, hi, col = pieces[k]
                for a in range(GH):
                    last = nc.tensor.matmul(ps[32 * a:32 * a + 32, bank, lo:hi], v_ring[slot][:, j, a, :],
                                            p_t[j % 2][:, a, col:col + hi - lo], start=(j == 0), stop=(j == (TT // 2 - 1 if bank == 6 else TT - 1)))
                if k == len(pieces) - 1:
                    last.then_inc(pv_step, 1)

            def turn_out(use, n, half):
                bank = ring_slot(use, n)
                for b in range(4):
                    i = 4 * half + b
                    last = nc.tensor.transpose(ps[:, bank, b * P:(b + 1) * P], o_raw[:, i * P:(i + 1) * P], ident_sb[:])
                last.then_inc(ring_full, 1)

            def beside(g, slot, use, n, kind, at):
                if kind == "search":
                    search(g + 1 + at[0], (slot, 1 - slot)[at[0] == 0], at[1], use, n)
                elif kind == "out":
                    turn_out(use, n, at[0])
                else:
                    turn_maxima(g + 1, use, n)

            def body(g, slot, pads=(0, 0), first=False, final=False):
                use, n, e = ring_base(g), 0, 0
                made = [0] * TT
                side = [("out", 0), ("out", 1)] if final else side_steps(not first, LEAD, pads[1] is not None)
                pe.wait_ge(m_rows, 64 * (g + 1))
                for kind, *at in group_order(side):
                    if kind == "keys":
                        keys(g, slot, at[0], at[1], e)
                        e += 1
                        made[at[0]] = e
                    elif kind == "values":
                        if at == [0, 0]:
                            pe.wait_ge(v_ringed, g + 1)
                            if not first:
                                pe.wait_ge(o_kept, g)
                        if at[1] == 0:
                            pe.wait_ge(exp_done, EXPS * g + made[at[0]])
                        values(slot, *at)
                    else:
                        if at == [0, FIRST_HIGH]:
                            pe.wait_ge(k_padded[1 - slot][1], 32 * pads[0])
                        if at == [1, 0]:
                            pe.wait_ge(k_padded[slot][0], 32 * pads[1])
                        if (kind, at) == ("out", [0]):
                            pe.wait_ge(o_kept, g)
                        beside(g, slot, use, n, kind, at)
                        n += 1
            n = EARLY
            for kind, *at in side_steps(False, EARLY, True):
                if kind == "search" and at[0] == 0:
                    pe.wait_ge(k_first[SEARCH[at[1]][0]], 32)
                if at == [1, 0]:
                    pe.wait_ge(k_padded[1][0], 32)
                if kind != "negate":
                    beside(-1, 1, 0, n, kind, at)
                    n += 1
            pe.wait_ge(roped, 2 * TT)
            pe.wait_ge(v_kept, TT)
            pe.wait_ge(k_kept, TT)
            body(0, 0, (1, 1), first=True)
            with pe.Fori(0, 2) as k:
                for b in range(2):
                    body(2 * k + 1 + b, 1 - b, (k + 1 + b, k + 2))
            body(5, 1, (3, 4))
            body(6, 0, (4, None))
            body(7, 1, final=True)
            pe.wait_ge(o_kept, NG)
            for half in range(2):
                turn_out(ring_base(NG - 1) + 2, half, half)

            pe.wait_ge(ring_read, ring_base(NG - 1) + 4)
            for t in range(TT):
                if t >= 4:
                    pe.wait_ge(ol_done, t - 3)
                for c in range(DC):
                    last = nc.tensor.transpose(ps[:, 4 + t % 4, c * P:(c + 1) * P], o_tok[:, t, c * P:(c + 1) * P], ident_sb[:])
                last.then_inc(o_turned, 1)

            def project_out(t, u):
                pe.wait_ge(ol_done, t + 1)
                return project(3, oh, ol, t, u, None)
            def gate_up1(m, u, halves=(0, 1), first=False):
                for w, bank, free, signal in ((0, 4 - 4 * u, silu1_done, gate1_done), (1, 6 - 4 * u, h1_done, up1_done)):
                    if not first:
                        pe.wait_ge(free, m - 1)
                    for c in range(DC):
                        for s, part in ((0, x3h), (0, x3l), (1, x3h)):
                            for h in halves:
                                last = nc.tensor.matmul(banks(bank + h, 1), gu[u][:, s, w * DC + c, :],
                                                        part[:, c, h * HALF:(h + 1) * HALF],
                                                        start=(c == 0 and s == 0 and part is x3h), stop=(c == DC - 1 and s == 1))
                    if halves != (0,):
                        last.then_inc(signal, 1)

            def first_gate_up1():
                pe.wait_ge(w1_low, 1)
                pe.wait_ge(xl_done, 2 * TT + TT // 2)
                gate_up1(0, 0, (0,), first=True)
            norm_stage(2, project_out, straight=True, between=first_gate_up1)
            pe.wait_ge(xl_done, 3 * TT)
            gate_up1(0, 0, (1,), first=True)
            for m in range(1, 3):
                pe.wait_ge(w1_low, m + 1)
                gate_up1(m, m % 2, first=(m == 1))
            with pe.Fori(1, M1 // 2) as k:
                for v in range(2):
                    pe.wait_ge(w1_low, 2 * k + 2 + v)
                    gate_up1(2 * k + 1 + v, 1 - v)

            def down1(t, u):
                for m in range(M1):
                    if isinstance(t, int) and t == 0 and m == M1 - 1:
                        pe.wait_ge(h1l_done, M1)
                    for part, s in ((h1h, 0), (h1l, 0), (h1h, 1)):
                        last = nc.tensor.matmul(banks(u, 1), part[:, m, ds(t * P, P)], wd1[:, s, m, :],
                                                start=(m == 0 and part is h1h and s == 0), stop=(m == M1 - 1 and s == 1))
                return last
            pe.wait_ge(silu1_done, M1)
            pe.wait_ge(h1l_done, M1 - 1)
            norm_stage(3, down1, turn=False)

        @block.scalar
        def _(act):
            own = Tally(act, act_own)
            nc.scalar.preload_act_table_set("natural_log_exp_and_others")
            act.wait_ge(ld_small, 5 * 16)
            own.done(nc.scalar.activation(negA[:], alog_sb[:], ACT.Exp))
            nc.scalar.mul(negA[:], negA[:], -1.0).then_inc(negA_done, 1)
            act.wait_ge(negA_done, 1)
            act.wait_ge(xp_done, 1)
            act.wait_ge(consts_made, 4)
            nc.scalar.copy(dt_in[2 * NS:2 * NS + DTR, :], banks(6, 2)[2 * NS:2 * NS + DTR, :]).then_inc(dtin_done, 1)

            def soft_log(c, part):
                if part == 0:
                    act.wait_ge(dtl_done, c + 1)
                    if c:
                        act.wait_ge(dt_done, c)
                    nc.scalar.activation(e_[:], banks(DT_BANK[c], 2), ACT.Abs).then_inc(z_abs, 1)
                    act.wait_ge(z_abs, c + 1)
                    own.done(nc.scalar.activation(e_[:], e_[:], ACT.Exp, scale=-1.0))
                elif part == 1:
                    nc.scalar.activation(dt_[:, c, :], e_[:], ACT.Square, bias=square_sb[:], scale=3.0 ** -0.5).then_inc(softlog, 1)
                    nc.scalar.activation(small_e[:], e_[:], ACT.Relu, bias=series_sb[:], scale=-1.0).then_inc(softlog, 1)
                else:
                    nc.scalar.activation(log_e[:], e_[:], ACT.Ln, bias=1.0).then_inc(softlog, 1)

            for part in range(3):
                soft_log(0, part)
            for c in range(DC):
                act.wait_ge(dt_done, c + 1)

                def step(n, u, first):
                    i = n + NS * c
                    if not (c == 0 and first):
                        act.wait_ge(scan_done, i - 1)
                    nc.scalar.activation(dA[:, u, :], dt_[:, c, :], ACT.Exp, scale=negA[:, c, ds(n, 1)]).then_inc(dA_done, 1)
                    if c == 0:
                        act.wait_ge(c_bcast, n + 1)
                        nc.scalar.copy(c_all[:, n, :], banks(4, 2)).then_inc(c_kept, 1)
                for n in range(4):
                    step(n, n % 2, n < 2)
                    if n < 3 and c + 1 < DC:
                        soft_log(c + 1, n)
                with act.Fori(2, NS // 2) as k:
                    for u in range(2):
                        step(2 * k + u, u, False)

            def norm_stage(ln, turn=True):
                def high(t, u):
                    act.wait_ge(x_turned, TT * ln + t + 1)
                    nc.scalar.copy(XH[ln][:, :, ds(t * P, P)], ps[:, 2 + u, :].rearrange("p (c t) -> p c t", c=DC)).then_inc(xh_done, 1)

                def root(t, u):
                    act.wait_ge(var_done, TT * ln + t + 1)
                    nc.scalar.activation(sdev[:, u:u + 1], vare[:, u:u + 1], ACT.Sqrt).then_inc(sdev_done, 1)
                root(0, 0)
                root(1, 1)
                with act.Fori(0, TT // 2 - 1) as k:
                    for u in range(2):
                        if turn:
                            high(2 * k + u, u)
                        root(2 * k + u + 2, u)
                if turn:
                    high(TT - 2, 0)
                    high(TT - 1, 1)
            XH = {0: xh, 1: xh}
            norm_stage(0)

            def weight_high(w):
                act.wait_ge(ld_wraw[w], 16)
                nc.scalar.mul(wsp[:, w, 0], wraw[:, w % 2], WS).then_inc(w_high, 1)

            def ffn0(m, u, first):
                act.wait_ge(gate_done, m + 1)
                if not first:
                    act.wait_ge(h_done, m - 1)
                nc.scalar.activation(sg[:, u, :], banks(4 - 4 * u, 2), ACT.Silu).then_inc(silu_done, 1)
                act.wait_ge(h_done, m + 1)
                nc.scalar.copy(hh[:, m, :], h32[:, u, :]).then_inc(hh_done, 1)
            for m in range(4):
                ffn0(m, m % 2, m < 2)
                weight_high(m)
            with act.Fori(2, M0 // 2) as k:
                for u in range(2):
                    ffn0(2 * k + u, u, False)
            norm_stage(1)
            act.wait_ge(ld_tab, 3 * 16)
            nc.scalar.copy(mask_b[:], mask_sb[:]).then_inc(tables_made, 1)
            nc.scalar.copy(ident_b[:], ident_sb[:]).then_inc(tables_made, 1)
            nc.scalar.copy(ident_h[:], ident_sb[:]).then_inc(tables_made, 1)
            nc.scalar.preload_act_table_set("natural_log_exp_and_others")

            def keep_queries(t):
                act.wait_ge(q_turned, t + 1)
                nc.scalar.copy(q_st[:, :, ds(t * P, P)], banks(6, 2).bitcast(f16).rearrange("p (r t) -> p r t", r=NP)).then_inc(q_kept, 1)

            def stack(t, first):
                for w in range(2):
                    act.wait_ge(rope_summed, 2 * t + w + 1)
                    if not first:
                        act.wait_ge((q_turned, k_turned)[w], t)
                    dst = tok_stack[:, w, :, 0:64 if w == 0 else 32].rearrange("p h (b d) -> p h b d", b=4 if w == 0 else 2)
                    nc.scalar.copy(dst[:, :, 0:3:2, :] if w == 0 else dst,
                                   rot_a[:, w].unsqueeze(2).broadcast_to([P, NH, 2, HD])).then_inc(stack_high, 1)
                act.wait_ge(v_proj, t + 1)
                nc.scalar.mul(v_tok[:, t, :], banks(qkv_bank(t, 2), 1), 1.0 / WS).then_inc(v_kept, 1)
            act.wait_ge(stacks_set, 2)
            for t in range(TT):
                if t:
                    keep_queries(t - 1)
                stack(t, t == 0)
            keep_queries(TT - 1)

            def keep_out(g, use):
                act.wait_ge(pv_step, TT * (g + 1))
                act.wait_ge(ring_read, use)
                nc.scalar.copy(o_raw[:], banks(6, 2)).then_inc(o_kept, 1)

            def body(g, first=False):
                e = 0
                for j in range(TT):
                    w = T - P * j
                    if not (first and j < 2):
                        act.wait_ge(pv_step, TT * g + j - 1)
                    for heads in exp_units(j):
                        act.wait_ge(st_full, EXPS * g + e + 1)
                        bank, a = 2 + 2 * (e % 2), heads[0]
                        if len(heads) == 1:
                            dst, src = p_t[j % 2][:, a, 0:w], banks(bank, 2)[:, 0:w]
                        else:
                            dst, src = p_t[j % 2][:, a:a + 2, 0:w], ps[:, bank:bank + 2, 0:w]
                        nc.scalar.activation(dst, src, ACT.Exp, scale=float(HD) ** -0.5).then_inc(exp_done, 1)
                        e += 1
                    if j == 0 and not first:
                        keep_out(g - 1, ring_base(g))
            body(0, True)
            with act.Fori(1, NG - 1) as g:
                body(g)
            body(NG - 1)
            keep_out(NG - 1, ring_base(NG - 1) + 2)

            def high_out(t):
                act.wait_ge(o_turned, t + 1)
                nc.scalar.copy(oh[:, :, t * P:(t + 1) * P], ps[:, 4 + t % 4, :].rearrange("p (c t) -> p c t", c=DC)).then_inc(oh_done, 1)
            for t in range(TT):
                high_out(t)
            def weights_high(m, u, first=False):
                act.wait_ge(w1_scaled, m + 1)
                if not first:
                    act.wait_ge(up1_done, m - 1)
                nc.scalar.mul(gu[u][:, 0], w_full[:, 0:2 * DC * P].rearrange("p (b n) -> p b n", n=P), WS).then_inc(w1_high, 1)
                nc.scalar.mul(wd1[:, 0, m, :], w_full[:, 2 * DC * P:], WS).then_inc(w1_high, 1)

            weights_high(0, 0, True)
            XH[2] = x3h
            norm_stage(2)
            def ffn1(m, u, first):
                act.wait_ge(gate1_done, m + 1)
                if not first:
                    act.wait_ge(h1_done, m - 1)
                nc.scalar.activation(sg1[:, u, :], banks(4 - 4 * u, 2), ACT.Silu, scale=1.0 / WS).then_inc(silu1_done, 1)
                act.wait_ge(h1_done, m + 1)
                nc.scalar.copy(h1h[:, m, :], h132[:, u, :]).then_inc(h1h_done, 1)
            weights_high(1, 1, True)
            ffn1(0, 0, True)
            weights_high(2, 0)
            ffn1(1, 1, True)
            with act.Fori(1, M1 // 2) as k:
                for u in range(2):
                    weights_high(2 * k + u + 1, 1 - u)
                    ffn1(2 * k + u, u, False)
            ffn1(M1 - 1, 0, False)
            norm_stage(3, turn=False)

        @block.gpsimd
        def _(pool):
            for c in range(DC):
                def step(n, u, first):
                    i = n + NS * c
                    pool.wait_ge(scan_done, i + 1)
                    if c == 0:
                        pool.wait_ge(c_kept, n + 1)
                    if not first:
                        pool.wait_ge(y_added, i - 3)
                    nc.gpsimd.tensor_tensor(hC[u][:], hst[:, u % 2, :], c_all[:, n, :], ALU.mult).then_inc(hc_done, 1)
                for n in range(4):
                    step(n, n, c == 0)
                with pool.Fori(1, NS // 4) as k:
                    for u in range(4):
                        step(4 * k + u, u, False)

            def keep(ln):
                with pool.Fori(0, TT // 2) as k:
                    for u in range(2):
                        pool.wait_ge(x_normed, TT * ln + 2 * k + u + 1)
                        nc.gpsimd.tensor_copy(xtok[:, 2 * k + u, :], xn[:, u, :]).then_inc(x_kept, 1)
            keep(0)
            pool.wait_ge(w_low, 4)
            nc.gpsimd.memset(tok_stack[:], 0.0).then_inc(stacks_set, 1)
            pool.wait_ge(stacks_set, 1)
            nc.gpsimd.memset(tok_stack[:, 1, :, 48:49], 1.0).then_inc(stacks_set, 1)
            pool.wait_ge(hl_done, M0)
            pool.wait_ge(up_done, M0)
            for slot in range(2):
                nc.gpsimd.memset(v_ring[slot][:], 1.0).then_inc(v_ones, 1)
            nc.gpsimd.memset(view(112, GH * T // 2, f32), 0.0).then_inc(pads_zeroed, 1)
            keep(1)

            def stack(t):
                for w in range(2):
                    pool.wait_ge(roped, 2 * t + w + 1)
                    nc.gpsimd.tensor_tensor(rot_a[:, w], rot_a[:, w], rot_b[:, w], ALU.add).then_inc(rope_summed, 1)
                for w in range(2):
                    pool.wait_ge(stack_high, 2 * t + w + 1)
                    at = 16 if w == 0 else 32
                    nc.gpsimd.tensor_tensor(tok_stack[:, w, :, at:at + HD], rot_a[:, w], tok_stack[:, w, :, 0:HD],
                                            ALU.subtract).then_inc(stack_low, 1)
            with pool.Fori(0, TT) as t:
                stack(t)
            pool.wait_ge(v_proj, TT)
            nc.gpsimd.memset(view(120, GH * T // 2, f32), 0.0).then_inc(pads_zeroed, 1)
            pool.wait_ge(v_kept, TT)
            pool.wait_ge(v_ones, 2)

            def ring_values(g, slot, first=False):
                if not first:
                    pool.wait_ge(pv_step, TT * (g - 1))
                nc.gpsimd.tensor_copy(v_ring[slot][:, :, :, 0:HD],
                                      v_tok[:, :, ds(g * GH * HD, GH * HD)].rearrange("p i (a d) -> p i a d", a=GH)).then_inc(v_ringed, 1)

            ring_values(0, 0, True)
            ring_values(1, 1, True)
            with pool.Fori(1, NG // 2) as k:
                for u in range(2):
                    ring_values(2 * k + u, u)
            for m in range(2):
                pool.wait_ge(w1_full, m + 1)
                nc.gpsimd.tensor_tensor(w_full[:], w_full[:], w_scales[m][:], ALU.mult).then_inc(w1_scaled, 1)
            keep(2)
            with pool.Fori(1, M1 // 2) as k:
                for u in range(2):
                    pool.wait_ge(w1_full, 2 * k + u + 1)
                    nc.gpsimd.tensor_tensor(w_full[:], w_full[:], w_scales[u][:], ALU.mult).then_inc(w1_scaled, 1)
            pool.wait_ge(w1_full, M1)
            nc.gpsimd.tensor_tensor(w_full[:], w_full[:], w_scales[0][:], ALU.mult).then_inc(w1_scaled, 1)

        @block.vector
        def _(dve):
            own = Tally(dve, dve_own)
            dve.wait_ge(ld_small, 5 * 16)
            nc.vector.tensor_copy(sel[:], fold_sb[:].unsqueeze(2).broadcast_to([P, 2 * NS, P])).then_inc(sel_built, 1)
            nc.vector.tensor_scalar(dskip_sb[:], dskip_sb[:], 1.0, None, ALU.add).then_inc(consts_made, 1)
            nc.vector.memset(square_sb[:], -(3.0 ** 0.5) / 4).then_inc(consts_made, 1)
            nc.vector.memset(series_sb[:], SERIES).then_inc(consts_made, 1)
            nc.vector.memset(dt_in[2 * NS:4 * NS, :], 1.0).then_inc(consts_made, 1)
            own.done(nc.vector.memset(bc[:], 0.0))
            dve.wait_ge(xp_done, 1)
            R = 2 * NS
            own.done(nc.vector.tensor_copy(bc[0:R, :], banks(6, 2)[0:R, :]))
            own.done(nc.vector.tensor_tensor(rest[0:R, :], banks(6, 2)[0:R, :], bc[0:R, :], ALU.subtract))
            own.done(nc.vector.tensor_copy(mid[0:R, :], rest[0:R, :]))
            own.done(nc.vector.tensor_copy(bc[R:2 * R, :], mid[0:R, :]))
            nc.vector.tensor_tensor(bc[2 * R:3 * R, :], rest[0:R, :], mid[0:R, :], ALU.subtract).then_inc(bc_split, 1)

            def make_dt(c, part):
                d = dt_[:, c, :]
                if part == 0:
                    dve.wait_ge(softlog, 3 * c + 1)
                    own.done(nc.vector.scalar_tensor_tensor(d, d, 13.0 / 16, e_[:], ALU.add, ALU.mult))
                elif part == 1:
                    dve.wait_ge(softlog, 3 * c + 3)
                    own.done(nc.vector.copy_predicated(log_e[:], small_e[:].bitcast(mybir.dt.uint16), d))
                elif part == 2:
                    dve.wait_ge(z_abs, c + 1)
                    nc.vector.scalar_tensor_tensor(d, banks(DT_BANK[c], 2), 0.0, log_e[:], ALU.max, ALU.add).then_inc(dt_done, 1)
                else:
                    dve.wait_ge(dt_done, c + 1)
                    own.done(nc.vector.tensor_tensor(dtx[:, c, :], d, xT[:, c, :], ALU.mult))

            def dbx(n, u, c, first=False):
                i = n + NS * c
                dve.wait_ge(b_bcast, i + 1)
                if not first:
                    dve.wait_ge(scan_done, i - 3)
                nc.vector.tensor_tensor(dBx[u][:], dtx[:, c, :], banks(2 * (u % 2), 2), ALU.mult).then_inc(dbx_done, 1)

            def scan(n, u, c, first=False):
                i = n + NS * c
                dve.wait_ge(dA_done, i + 1)
                dve.wait_ge(dbx_done, i + 1)
                if not first:
                    dve.wait_ge(hc_done, i - 1)
                nc.vector.tensor_tensor_scan(hst[:, u % 2, :], dA[:, u % 2, :], dBx[u][:], 0.0, ALU.mult, ALU.add).then_inc(scan_done, 1)

            def take_y(c):
                dve.wait_ge(y_added, NS * (c + 1))
                nc.vector.scalar_tensor_tensor(xT[:, c, :], xT[:, c, :], dskip_sb[:, c:c + 1], banks(6, 2),
                                               ALU.mult, ALU.add).then_inc(y_taken, 1)

            for part in range(4):
                make_dt(0, part)
            dve.wait_ge(consts_made, 4)
            for c in range(DC):
                for n in range(8):
                    dbx(n, n % 4, c, c == 0 and n < 4)
                    if n:
                        scan(n - 1, (n - 1) % 4, c, c == 0 and n < 3)
                    elif c:
                        scan(NS - 1, 3, c - 1)
                    if c and n == 3:
                        take_y(c - 1)
                    if c == 0 and 2 <= n < 6:
                        make_dt(1, n - 2)
                    elif n >= 4 and c and c + 1 < DC:
                        make_dt(c + 1, n - 4)
                with dve.Fori(2, NS // 4) as k:
                    for u in range(4):
                        dbx(4 * k + u, u, c)
                        scan(4 * k + u - 1, (u - 1) % 4, c)
            scan(NS - 1, 3, DC - 1)
            take_y(DC - 1)

            def norm_stage(ln, scale, turn=True):
                def bank(t):
                    return banks(LN_BANKS[ln][t % len(LN_BANKS[ln])], 1)

                def take(t):
                    dve.wait_ge(ln_in, TT * ln + t + 1)
                    if scale is None:
                        return
                    dve.wait_ge(x_kept, TT * (ln - 1) + t + 1)
                    src = xtok[:, t, :]
                    if ln == 3:
                        nc.vector.tensor_scalar(o_half[:], bank(t), scale, None, ALU.mult).then_inc(ln_taken, 1)
                        dve.wait_ge(ln_taken, TT * (ln - 1) + t + 1)
                        own.done(nc.vector.tensor_tensor(src, src, o_half[:], ALU.add))
                    else:
                        nc.vector.scalar_tensor_tensor(src, bank(t), scale, src, ALU.mult, ALU.add).then_inc(ln_taken, 1)
                        dve.wait_ge(ln_taken, TT * (ln - 1) + t + 1)

                def stats(t):
                    return nc.vector.bn_stats(st6[:], bank(t) if scale is None else xtok[:, t, :])

                def variance(t, u):
                    own.done(nc.vector.bn_aggr(mv[:, u, :], st6[:]))
                    nc.vector.tensor_scalar(vare[:, u:u + 1], mv[:, u, 1:2], EPS, None, ALU.add).then_inc(var_done, 1)

                def root_taken(t, u):
                    dve.wait_ge(sdev_done, TT * ln + t + 1)
                    own.done(nc.vector.reciprocal(rstd[:], sdev[:, u:u + 1]))

                def normalise(t, u):
                    if ln == 3 and t >= 2:
                        dve.wait_ge(out_stored[u], 16 * (t // 2))
                    elif ln or t >= 2:
                        dve.wait_ge(x_kept, TT * ln + t - 1)
                        if turn or t < 2:
                            dve.wait_ge(x_turned, TT * ln + t - 1)
                    src = bank(t) if scale is None else xtok[:, t, :]
                    nc.vector.tensor_scalar(xn[:, u, :], src, mv[:, u, 0:1], rstd[:], ALU.subtract, ALU.mult).then_inc(x_normed, 1)

                def low(t, u):
                    dve.wait_ge(xh_done, TT * ln + t + 1)
                    nc.vector.tensor_tensor(XL[ln][:, :, ds(t * P, P)], ps[:, 2 + u, :].rearrange("p (c t) -> p c t", c=DC),
                                            XH[ln][:, :, ds(t * P, P)], ALU.subtract).then_inc(xl_done, 1)
                take(0)
                own.done(stats(0))
                variance(0, 0)
                for t in range(TT):
                    u, more = t % 2, t + 1 < TT
                    if more:
                        take(t + 1)
                        own.done(stats(t + 1))
                    if t:
                        dve.wait_ge(x_normed, TT * ln + t)
                    root_taken(t, u)
                    if more:
                        variance(t + 1, 1 - u)
                    normalise(t, u)
                    if turn and t:
                        low(t - 1, 1 - u)
                    if t + 1 == TT and turn:
                        low(TT - 1, 1)
            XH, XL = {0: xh, 1: xh}, {0: xl, 1: xl}
            norm_stage(0, None)

            def weight_low(w):
                dve.wait_ge(w_high, w + 1)
                nc.vector.scalar_tensor_tensor(wsp[:, w, 1], wraw[:, w % 2], WS, wsp[:, w, 0], ALU.mult, ALU.subtract).then_inc(w_low, 1)

            def ffn0(m, u, first):
                dve.wait_ge(silu_done, m + 1)
                dve.wait_ge(up_done, m + 1)
                if not first:
                    dve.wait_ge(hl_done, m - 1)
                nc.vector.tensor_tensor(h32[:, u, :], sg[:, u, :], banks(6 - 4 * u, 2), ALU.mult).then_inc(h_done, 1)
                dve.wait_ge(hh_done, m + 1)
                nc.vector.tensor_tensor(hl[:, m, :], h32[:, u, :], hh[:, m, :], ALU.subtract).then_inc(hl_done, 1)
            for m in range(4):
                ffn0(m, m % 2, m < 2)
                weight_low(m)
            with dve.Fori(2, M0 // 2) as k:
                for u in range(2):
                    ffn0(2 * k + u, u, False)
            norm_stage(1, 1.0)
            dve.wait_ge(ld_tab, 3 * 16)

            def rope(w, t):
                dve.wait_ge((q_proj, k_proj)[w], t + 1)
                if t:
                    dve.wait_ge(stack_low, 2 * t - 1 + w)
                src = banks(qkv_bank(t, w), 1).rearrange("p (h d) -> p h d", h=NH)
                h2 = HD // 2
                tab = lambda x, a, b: x[:, t, a:b].unsqueeze(1).broadcast_to([P, NH, b - a])
                nc.vector.tensor_tensor(rot_a[:, w], src, tab(cos_sb, 0, HD), ALU.mult)
                nc.vector.tensor_tensor(rot_b[:, w, :, 0:h2], src[:, :, h2:HD], tab(sin_sb, 0, h2), ALU.mult)
                nc.vector.tensor_tensor(rot_b[:, w, :, h2:HD], src[:, :, 0:h2], tab(sin_sb, h2, HD), ALU.mult).then_inc(roped, 1)

            def keep_keys(t):
                dve.wait_ge(k_turned, t + 1)
                nc.vector.tensor_copy(k_st[:, :, ds(t * P, P)], banks(6, 2).bitcast(f16).rearrange("p (r t) -> p r t", r=NP)).then_inc(k_kept, 1)

            def maxima(k, use, n):
                _, dst, slices = SEARCH[k]
                w = slices[0][2]
                dve.wait_ge(ring_full, use + n + 1)
                nc.vector.reduce_max(dst, ps[:, n % 2, 0:len(slices) * w].rearrange("p (a w) -> p a w", a=len(slices)), AX).then_inc(ring_read, 1)

            for t in range(TT):
                rope(0, t)
                for k in early_units(t, 0):
                    maxima(k, 0, k)
                rope(1, t)
                if t:
                    keep_keys(t - 1)
                for k in early_units(t, 1) + early_units(t, 2):
                    maxima(k, 0, k)
            keep_keys(TT - 1)

            def negate(g, use, n):
                dve.wait_ge(ring_read, use + n)
                nc.vector.tensor_tensor(m_a[:, 4:TT, :], m_a[:, 4:TT, :], m_b[:], ALU.max).then_inc(m_joined, 1)
                dve.wait_ge(m_joined, g + 1)
                nc.vector.tensor_scalar(m_neg[:], m_a[:], -1.0, None, ALU.mult).then_inc(m_negated, 1)
                dve.wait_ge(m_negated, g + 1)

            def keep_rows(g, use, n):
                dve.wait_ge(ring_full, use + n + 1)
                if not (isinstance(g, int) and g == 0):
                    dve.wait_ge(m_rows, 64 * g)
                nc.vector.tensor_copy(m_row[0:GH, :], ps[0:GH, n % 2, :].bitcast(f16)).then_inc(ring_read, 1)

            def divide(g, use, n, half):
                dve.wait_ge(ring_full, use + n + 1)
                src = ps[:, n % 2, :].rearrange("p (i a d) -> p i a d", i=4, a=GH)
                nc.vector.reciprocal(r_den[:].unsqueeze(3), src[:, :, :, HD:HD + 1]).then_inc(r_made, 1)
                dve.wait_ge(r_made, 2 * g + half + 1)
                nc.vector.tensor_tensor(o_tok[:, 4 * half:4 * half + 4, ds(g * GH * HD, GH * HD)].rearrange("p i (a d) -> p i a d", a=GH),
                                        src[:, :, :, 0:HD], r_den[:].unsqueeze(3).broadcast_to([P, 4, GH, HD]),
                                        ALU.mult).then_inc(ring_read, 1)
                dve.wait_ge(ring_read, use + n + 1)

            def body(g, use, side, n=0):
                for kind, *at in side:
                    if kind == "search":
                        maxima(at[1], use, n)
                    elif kind == "negate":
                        negate(g + 1, use, n)
                        continue
                    elif kind == "turn":
                        keep_rows(g + 1, use, n)
                    else:
                        divide(g - 1, use, n, at[0])
                    n += 1
            body(-1, 0, side_steps(False, EARLY, True), EARLY)
            body(0, ring_base(0), side_steps(False, LEAD, True))
            with dve.Fori(1, NG - 2) as g:
                body(g, ring_base(g), side_steps(True, LEAD, True))
            def nibbles(m, u, loads):
                dve.wait_ge(ld_w1[u], 48 * loads)
                nib = z_nib[:].rearrange("p (n h) -> p n h", h=2)
                byte = w_zeros[u][:].bitcast(u8).unsqueeze(2)
                nc.vector.tensor_scalar(nib[:, :, 0:1], byte, 15, None, ALU.bitwise_and)
                nc.vector.tensor_scalar(nib[:, :, 1:2], byte, 4, None, ALU.logical_shift_right)
                nc.vector.tensor_scalar(w_nib[:], w_words[u][:], shift_sb[:, 0:1], 15, ALU.logical_shift_right, ALU.bitwise_and).then_inc(w1_nib, 1)
                dve.wait_ge(w1_nib, m + 1)

            def unscaled(m):
                nc.vector.scalar_tensor_tensor(w_full[:], w_nib[:], 1.0, z_nib[:], ALU.subtract, ALU.subtract).then_inc(w1_full, 1)
                dve.wait_ge(w1_full, m + 1)

            body(NG - 2, ring_base(NG - 2), side_steps(True, LEAD, False))
            body(NG - 1, ring_base(NG - 1), [("out", 0), ("out", 1)])
            dve.wait_ge(ld_shift, 16)
            nibbles(0, 0, 1)
            unscaled(0)
            nibbles(1, 1, 1)
            for half in range(2):
                divide(NG - 1, ring_base(NG - 1) + 2, half, half)

            def low_out(t):
                dve.wait_ge(oh_done, t + 1)
                nc.vector.tensor_tensor(ol[:, :, t * P:(t + 1) * P], ps[:, 4 + t % 4, :].rearrange("p (c t) -> p c t", c=DC),
                                        oh[:, :, t * P:(t + 1) * P], ALU.subtract).then_inc(ol_done, 1)
            for t in range(TT):
                low_out(t)
            def weights_low(m, u):
                dve.wait_ge(w1_high, 2 * m + 2)
                nc.vector.scalar_tensor_tensor(gu[u][:, 1].rearrange("p b n -> p (b n)"), w_full[:, 0:2 * DC * P], WS,
                                               gu[u][:, 0].rearrange("p b n -> p (b n)"), ALU.mult, ALU.subtract)
                nc.vector.scalar_tensor_tensor(wd1[:, 1, m, :], w_full[:, 2 * DC * P:], WS, wd1[:, 0, m, :],
                                               ALU.mult, ALU.subtract).then_inc(w1_low, 1)
                dve.wait_ge(w1_low, m + 1)

            weights_low(0, 0)
            unscaled(1)
            XH[2], XL[2] = x3h, x3l
            norm_stage(2, 1.0 / WS)
            def ffn1(m, u, first):
                dve.wait_ge(silu1_done, m + 1)
                dve.wait_ge(up1_done, m + 1)
                if not first:
                    dve.wait_ge(h1l_done, m - 1)
                nc.vector.scalar_tensor_tensor(h132[:, u, :], banks(6 - 4 * u, 2), 1.0 / WS, sg1[:, u, :], ALU.mult, ALU.mult).then_inc(h1_done, 1)
                dve.wait_ge(h1h_done, m + 1)
                nc.vector.tensor_tensor(h1l[:, m, :], h132[:, u, :], h1h[:, m, :], ALU.subtract).then_inc(h1l_done, 1)
            weights_low(1, 1)
            nibbles(2, 0, 2)
            unscaled(2)
            ffn1(0, 0, True)
            weights_low(2, 0)
            nibbles(3, 1, 2)
            unscaled(3)
            ffn1(1, 1, True)
            with dve.Fori(1, M1 // 2 - 1) as k:
                for u in range(2):
                    weights_low(2 * k + u + 1, 1 - u)
                    nibbles(2 * k + u + 2, u, k + 2)
                    unscaled(2 * k + u + 2)
                    ffn1(2 * k + u, u, False)
            weights_low(M1 - 2, 1)
            nibbles(M1 - 1, 0, M1 // 2 + 1)
            unscaled(M1 - 1)
            ffn1(M1 - 3, 0, False)
            weights_low(M1 - 1, 0)
            ffn1(M1 - 2, 1, False)
            ffn1(M1 - 1, 0, False)
            norm_stage(3, 1.0 / WS, turn=False)


def kernel(**inputs):
    import numpy as np
    import concourse.bacc as bacc
    from concourse.bass_utils import run_bass_kernel_spmd

    nc = bacc.Bacc("TRN2", target_bir_lowering=False, num_devices=1)
    get = {k: np.asarray(v) for k, v in inputs.items()}
    xw = get["L0_attn_x_proj_w"].T
    pos = np.arange(T, dtype=np.float32)
    theta = (1.0 / 10000.0 ** (np.arange(0, HD, 2, dtype=np.float32) / HD)).astype(np.float32)
    angle = np.outer(pos, theta).astype(np.float32)
    cos = np.concatenate([np.cos(angle), np.cos(angle)], -1) / np.float32(WS)
    sin = np.concatenate([-np.sin(angle), np.sin(angle)], -1) / np.float32(WS)
    tok, key = np.arange(P)[:, None], np.arange(P)[None, :]

    def tiles(kind, rows):
        per = P if kind != "zeros" else P // PACK
        at = np.zeros((M1, rows, 3 * DC, per), get["L1_ffn_gate_" + kind].dtype)
        for i, name in enumerate(("gate", "up")):
            a = get[f"L1_ffn_{name}_{kind}"].reshape(DC, rows, -1)
            for m in range(M1):
                part = a[:, :, m * per:(m + 1) * per]
                at[m, :, i * DC:(i + 1) * DC, :part.shape[2]] = part.transpose(1, 0, 2)
        a = get["L1_ffn_down_" + kind]
        for m in range(M1):
            part = a[m * rows:(m + 1) * rows]
            at[m, :part.shape[0], 2 * DC:] = part.reshape(part.shape[0], DC, per)
        return at.reshape(M1, rows, -1)

    arrays = {
        "x_fm": get["L0_attn_x"][0].T, "a_log": get["L0_attn_A_log"], "d_skip": get["L0_attn_D"].reshape(DC, P).T,
        "xw": np.concatenate([xw[:, DTR:], xw[:, :DTR]], 1), "dtw": np.concatenate([get["L0_attn_dt_proj_w"].T, get["L0_attn_dt_proj_b"][None, :]], 0),
        "wg0": get["L0_ffn_W_gate"].T, "wu0": get["L0_ffn_W_up"].T, "wd0": get["L0_ffn_W_down"].T,
        "wq": get["L1_attn_wq"].T, "wk": get["L1_attn_wk"].T, "wv": get["L1_attn_wv"].T, "wo": get["L1_attn_wo"].T,
        "w1_q": np.repeat(tiles("qweight", P // PACK), PACK, axis=1), "w1_s": tiles("scales", 1)[:, 0], "w1_z": tiles("zeros", 1)[:, 0],
        "ident": np.eye(P, dtype=np.float32),
        "fold": np.concatenate([np.eye(2 * NS, dtype=np.float32)] * 3 + [np.zeros((2 * NS, 2 * NS), np.float32)], 0),
        "mask": np.where(key > tok, np.float32(-1e30), np.float32(0)),
        "cos": cos.astype(np.float32), "sin": sin.astype(np.float32),
        "shifts": ((np.arange(P) % PACK) * 4).astype(np.int32)[:, None],
    }
    feeds, args = {}, []
    for name, a in arrays.items():
        a = np.ascontiguousarray(a)
        feeds[f"in_{name}_dram"] = a
        args.append(nc.dram_tensor(f"in_{name}_dram", a.shape, mybir.dt.from_np(a.dtype), kind="ExternalInput").ap())
    args.append(nc.dram_tensor("out_0_dram", (1, T, D), mybir.dt.float32, kind="ExternalOutput").ap())
    build(nc, *args)
    r = run_bass_kernel_spmd(nc, [feeds], core_ids=[0])
    return r.results[0]["out_0_dram"]
```
